# Optimizing a Trainium2 kernel written in Bass

```python
import numpy as np
import jax
import jax.numpy as jnp

def _softmax(x, axis=-1):
    return jax.nn.softmax(x, axis=axis)

def _gelu(x):
    return jax.nn.gelu(x, approximate=True)

def _silu(x):
    return jax.nn.silu(x)

def _sigmoid(x):
    return jax.nn.sigmoid(x)

def _layernorm(x, axis=-1, eps=1e-05):
    m = jnp.mean(x, axis=axis, keepdims=True)
    v = jnp.var(x, axis=axis, keepdims=True)
    return (x - m) / jnp.sqrt(v + eps)

def _scatter_add(tgt, idx, src, axis=0):
    return tgt.at[idx].add(src)

def _segment_sum(src, seg, n):
    return jax.ops.segment_sum(src, seg, n)
kernel_name = 'mk_perceiver_d2_seqx_r2_e5ca62'

def setup_inputs(seed: int=0):
    np.random.seed(seed)
    _w = jnp.asarray

    def _rec_inputs():
        import jax
        import jax.numpy as jnp
        _rk = jax.random.key(seed)
        x = -0.0002928 + 1 * jax.random.normal(jax.random.fold_in(_rk, 1), (8, 64, 512), jnp.float32)
        _lenS = 64 - jax.random.randint(jax.random.fold_in(_rk, 7), (8,), 0, max(1, 64 // 4) + 1, jnp.int32)
        _lenS2 = 1601 - jax.random.randint(jax.random.fold_in(_rk, 8), (8,), 0, max(1, 1601 // 4) + 1, jnp.int32)
        _ctx_1024P = jax.random.normal(jax.random.fold_in(_rk, 11), (8, 16, 512), jnp.float32)
        _ctx_1024c = jax.random.dirichlet(jax.random.fold_in(_rk, 511), 0.3 * jnp.ones((16,), jnp.float32), (8, 1601))
        _ctx_1024t = jnp.einsum('bsk,bkd->bsd', _ctx_1024c, _ctx_1024P)
        _ctx_1024t = _ctx_1024t * jax.lax.rsqrt(jnp.mean(jnp.square(_ctx_1024t)) + 1e-12) * 0.953939
        ctx_1024 = -1.39393e-06 + 0.999914 * (_ctx_1024t + 0.3 * jax.random.normal(jax.random.fold_in(_rk, 611), (8, 1601, 512), jnp.float32))
        _validS = jnp.arange(64)[None, :] < _lenS[:, None]
        _validS2 = jnp.arange(1601)[None, :] < _lenS2[:, None]
        _causal = jnp.tril(jnp.ones((64, 64), dtype=bool))
        mask_BxS2_ik0 = jnp.where(jnp.broadcast_to(_validS2[:, :], (8, 1601)), 0, 1).astype(jnp.int32)
        return (x, ctx_1024, mask_BxS2_ik0)
    x, ctx_1024, mask_BxS2_ik0 = _rec_inputs()

    def _L0_xattn_setup():
        import jax, jax.numpy as jnp
        import numpy as np
        import math
        B, S, D, H = (2, 1024, 512, 16)
        DH = D // H

        def _split_heads(x):
            b, s, _ = x.shape
            return x.reshape(b, s, H, DH).transpose(0, 2, 1, 3)
        key = jax.random.key(seed)
        ks = jax.random.split(key, 8)
        queries = jax.random.normal(ks[0], (B, S, D), dtype=jnp.float32)
        keys_ = jax.random.normal(ks[1], (B, S, D), dtype=jnp.float32)
        values = jax.random.normal(ks[2], (B, S, D), dtype=jnp.float32)
        masks = jax.random.randint(ks[3], (B, S), 0, 2, dtype=jnp.int32)
        scale = 1.0 / math.sqrt(D)
        Wq = jax.random.normal(ks[4], (D, D), dtype=jnp.float32) * scale
        Wk = jax.random.normal(ks[5], (D, D), dtype=jnp.float32) * scale
        Wv = jax.random.normal(ks[6], (D, D), dtype=jnp.float32) * scale
        Wo = jax.random.normal(ks[7], (D, D), dtype=jnp.float32) * scale
        return {'queries': queries, 'keys': keys_, 'values': values, 'masks': masks, 'Wq': Wq, 'Wk': Wk, 'Wv': Wv, 'Wo': Wo}
    _L0_xattn_all = _L0_xattn_setup()
    _L0_xattn_in = {k: v for k, v in _L0_xattn_all.items() if k in ('Wq', 'Wk', 'Wv', 'Wo')}
    del _L0_xattn_all

    def _L0_attn_setup():
        import jax, jax.numpy as jnp
        import numpy as np
        B, L, D, S = (4, 1024, 512, 16)
        key = jax.random.key(seed)
        ks = jax.random.split(key, 8)
        inv_d = 1.0 / np.sqrt(D)
        inv_s = 1.0 / np.sqrt(S)
        A_log = jnp.broadcast_to(jnp.clip(jnp.log(jnp.arange(1, S + 1, dtype=jnp.float32)), -7.0, None), (D, S))
        return {'x': jax.random.normal(ks[0], (B, L, D), jnp.float32), 'A_log': A_log, 'W_B': jax.random.uniform(ks[1], (S, D), jnp.float32, -inv_d, inv_d), 'W_C': jax.random.uniform(ks[2], (D, S), jnp.float32, -inv_s, inv_s), 'D_skip': jnp.ones((D,), jnp.float32), 'log_dt': jax.random.normal(ks[3], (D,), jnp.float32) * 0.01 - 4.0, 'W_in': jax.random.uniform(ks[4], (2 * D, D), jnp.float32, -inv_d, inv_d), 'b_in': jax.random.uniform(ks[5], (2 * D,), jnp.float32, -inv_d, inv_d), 'W_out': jax.random.uniform(ks[6], (D, D), jnp.float32, -inv_d, inv_d), 'b_out': jax.random.uniform(ks[7], (D,), jnp.float32, -inv_d, inv_d), 'ln_g': jnp.ones((D,), jnp.float32), 'ln_b': jnp.zeros((D,), jnp.float32)}
    _L0_attn_all = _L0_attn_setup()
    _L0_attn_in = {k: v for k, v in _L0_attn_all.items() if k in ('A_log', 'W_B', 'W_C', 'D_skip', 'log_dt', 'W_in', 'b_in', 'W_out', 'b_out', 'ln_g', 'ln_b')}
    del _L0_attn_all

    def _L0_ffn_setup():
        import jax, jax.numpy as jnp
        import numpy as np
        H = 8
        KD = 128
        TOPK = 8
        NUM_KEYS = 128
        N_EXPERTS = NUM_KEYS * NUM_KEYS
        N_DIM = 512
        BN_EPS = 1e-05

        def gelu_new(x):
            c = jnp.sqrt(jnp.asarray(2.0 / jnp.pi, x.dtype))
            return 0.5 * x * (1.0 + jnp.tanh(c * (x + 0.044715 * x * x * x)))
        key = jax.random.key(seed)
        ks = jax.random.split(key, 5)
        b, s = (2, 512)
        x = jax.random.normal(ks[0], (b, s, N_DIM), dtype=jnp.float32)
        w_q = jax.random.normal(ks[1], (N_DIM, 2 * H * KD), dtype=jnp.float32) * 0.02
        bn_gamma = jnp.ones((2 * H * KD,), dtype=jnp.float32)
        bn_beta = jnp.zeros((2 * H * KD,), dtype=jnp.float32)
        keys = jax.random.normal(ks[2], (H, NUM_KEYS, 2, KD), dtype=jnp.float32) * 0.02
        down_embed = jax.random.normal(ks[3], (N_EXPERTS, N_DIM), dtype=jnp.float32) * 0.02
        up_embed = jax.random.normal(ks[4], (N_EXPERTS, N_DIM), dtype=jnp.float32) * 0.02
        return {'x': x, 'w_q': w_q, 'bn_gamma': bn_gamma, 'bn_beta': bn_beta, 'keys': keys, 'down_embed': down_embed, 'up_embed': up_embed}
    _L0_ffn_all = _L0_ffn_setup()
    _L0_ffn_in = {k: v for k, v in _L0_ffn_all.items() if k in ('w_q', 'bn_gamma', 'bn_beta', 'keys', 'down_embed', 'up_embed')}
    del _L0_ffn_all

    def _L1_xattn_setup():
        import jax, jax.numpy as jnp
        import numpy as np
        import math
        B, S, D, H = (1, 1024, 512, 16)
        DK = D // H
        DH = 64
        LOG_T_MIN = math.log(0.1)
        LOG_T_MAX = math.log(10.0)

        def _linear(x, W, b):
            return x @ W.T + b
        key = jax.random.key(seed)
        ks = jax.random.split(key, 20)
        p = 0.02
        return {'query': jax.random.normal(ks[0], (B, S, D), jnp.float32), 'key': jax.random.normal(ks[1], (B, S, D), jnp.float32), 'value': jax.random.normal(ks[2], (B, S, D), jnp.float32), 'Wq': jax.random.normal(ks[3], (D, D), jnp.float32) * p, 'bq': jax.random.normal(ks[4], (D,), jnp.float32) * p, 'Wk': jax.random.normal(ks[5], (D, D), jnp.float32) * p, 'bk': jax.random.normal(ks[6], (D,), jnp.float32) * p, 'Wv': jax.random.normal(ks[7], (D, D), jnp.float32) * p, 'bv': jax.random.normal(ks[8], (D,), jnp.float32) * p, 'Wo': jax.random.normal(ks[9], (D, D), jnp.float32) * p, 'bo': jax.random.normal(ks[10], (D,), jnp.float32) * p, 'w1': jax.random.normal(ks[11], (DH, 3), jnp.float32) * 0.3, 'b1': jax.random.normal(ks[12], (DH,), jnp.float32) * 0.1, 'w2': jax.random.normal(ks[13], (DH, DH), jnp.float32) * 0.1, 'b2': jax.random.normal(ks[14], (DH,), jnp.float32) * 0.1, 'w3': jax.random.normal(ks[15], (1, DH), jnp.float32) * 0.1, 'b3': jnp.full((1,), (LOG_T_MIN + LOG_T_MAX) / 2, jnp.float32)}
    _L1_xattn_all = _L1_xattn_setup()
    _L1_xattn_in = {k: v for k, v in _L1_xattn_all.items() if k in ('Wq', 'bq', 'Wk', 'bk', 'Wv', 'bv', 'Wo', 'bo', 'w1', 'b1', 'w2', 'b2', 'w3', 'b3')}
    del _L1_xattn_all

    def _L1_attn_setup():
        import jax, jax.numpy as jnp
        import numpy as np
        N_HEADS = 16
        D_MODEL = 512
        SEQ_LEN = 1024
        BATCH = 4
        key = jax.random.key(seed)
        k1, k2, k3 = jax.random.split(key, 3)
        std = 1.0 / np.sqrt(D_MODEL)
        x = jax.random.normal(k1, (BATCH, SEQ_LEN, D_MODEL), dtype=jnp.float32)
        w_qkv = std * jax.random.normal(k2, (D_MODEL, 3 * D_MODEL), dtype=jnp.float32)
        w_o = std * jax.random.normal(k3, (D_MODEL, D_MODEL), dtype=jnp.float32)
        return {'x': x, 'w_qkv': w_qkv, 'w_o': w_o}
    _L1_attn_all = _L1_attn_setup()
    _L1_attn_in = {k: v for k, v in _L1_attn_all.items() if k in ('w_qkv', 'w_o')}
    del _L1_attn_all

    def _L1_ffn_setup():
        import jax, jax.numpy as jnp
        import numpy as np
        D_MODEL = 512
        D_FF = 2048
        N_EXPERTS = 8
        TOP_K = 2

        def _ffn(x, w1, b1, w2, b2):
            h = jax.nn.gelu(x @ w1.T + b1)
            return h @ w2.T + b2
        key = jax.random.key(seed)
        ks = jax.random.split(key, 12)
        s = 0.02
        x = jax.random.normal(ks[0], (4, 1024, D_MODEL), dtype=jnp.float32)
        shared_w1 = jax.random.normal(ks[1], (D_FF, D_MODEL), dtype=jnp.float32) * s
        shared_b1 = jnp.zeros((D_FF,), dtype=jnp.float32)
        shared_w2 = jax.random.normal(ks[2], (D_MODEL, D_FF), dtype=jnp.float32) * s
        shared_b2 = jnp.zeros((D_MODEL,), dtype=jnp.float32)
        router_w = jax.random.normal(ks[3], (N_EXPERTS, D_MODEL), dtype=jnp.float32) * s
        router_b = jnp.zeros((N_EXPERTS,), dtype=jnp.float32)
        spec_w1 = jax.random.normal(ks[4], (N_EXPERTS, D_FF, D_MODEL), dtype=jnp.float32) * s
        spec_b1 = jnp.zeros((N_EXPERTS, D_FF), dtype=jnp.float32)
        spec_w2 = jax.random.normal(ks[5], (N_EXPERTS, D_MODEL, D_FF), dtype=jnp.float32) * s
        spec_b2 = jnp.zeros((N_EXPERTS, D_MODEL), dtype=jnp.float32)
        return dict(x=x, shared_w1=shared_w1, shared_b1=shared_b1, shared_w2=shared_w2, shared_b2=shared_b2, router_w=router_w, router_b=router_b, spec_w1=spec_w1, spec_b1=spec_b1, spec_w2=spec_w2, spec_b2=spec_b2)
    _L1_ffn_all = _L1_ffn_setup()
    _L1_ffn_in = {k: v for k, v in _L1_ffn_all.items() if k in ('shared_w1', 'shared_b1', 'shared_w2', 'shared_b2', 'router_w', 'router_b', 'spec_w1', 'spec_b1', 'spec_w2', 'spec_b2')}
    del _L1_ffn_all
    return {'x': x, 'ctx_1024': ctx_1024, 'mask_BxS2_ik0': mask_BxS2_ik0, 'L0_xattn_Wq': _L0_xattn_in['Wq'], 'L0_xattn_Wk': _L0_xattn_in['Wk'], 'L0_xattn_Wv': _L0_xattn_in['Wv'], 'L0_xattn_Wo': _L0_xattn_in['Wo'], 'L0_attn_A_log': _L0_attn_in['A_log'], 'L0_attn_W_B': _L0_attn_in['W_B'], 'L0_attn_W_C': _L0_attn_in['W_C'], 'L0_attn_D_skip': _L0_attn_in['D_skip'], 'L0_attn_log_dt': _L0_attn_in['log_dt'], 'L0_attn_W_in': _L0_attn_in['W_in'], 'L0_attn_b_in': _L0_attn_in['b_in'], 'L0_attn_W_out': _L0_attn_in['W_out'], 'L0_attn_b_out': _L0_attn_in['b_out'], 'L0_attn_ln_g': _L0_attn_in['ln_g'], 'L0_attn_ln_b': _L0_attn_in['ln_b'], 'L0_ffn_w_q': _L0_ffn_in['w_q'], 'L0_ffn_bn_gamma': _L0_ffn_in['bn_gamma'], 'L0_ffn_bn_beta': _L0_ffn_in['bn_beta'], 'L0_ffn_keys': _L0_ffn_in['keys'], 'L0_ffn_down_embed': _L0_ffn_in['down_embed'], 'L0_ffn_up_embed': _L0_ffn_in['up_embed'], 'L1_xattn_Wq': _L1_xattn_in['Wq'], 'L1_xattn_bq': _L1_xattn_in['bq'], 'L1_xattn_Wk': _L1_xattn_in['Wk'], 'L1_xattn_bk': _L1_xattn_in['bk'], 'L1_xattn_Wv': _L1_xattn_in['Wv'], 'L1_xattn_bv': _L1_xattn_in['bv'], 'L1_xattn_Wo': _L1_xattn_in['Wo'], 'L1_xattn_bo': _L1_xattn_in['bo'], 'L1_xattn_w1': _L1_xattn_in['w1'], 'L1_xattn_b1': _L1_xattn_in['b1'], 'L1_xattn_w2': _L1_xattn_in['w2'], 'L1_xattn_b2': _L1_xattn_in['b2'], 'L1_xattn_w3': _L1_xattn_in['w3'], 'L1_xattn_b3': _L1_xattn_in['b3'], 'L1_attn_w_qkv': _L1_attn_in['w_qkv'], 'L1_attn_w_o': _L1_attn_in['w_o'], 'L1_ffn_shared_w1': _L1_ffn_in['shared_w1'], 'L1_ffn_shared_b1': _L1_ffn_in['shared_b1'], 'L1_ffn_shared_w2': _L1_ffn_in['shared_w2'], 'L1_ffn_shared_b2': _L1_ffn_in['shared_b2'], 'L1_ffn_router_w': _L1_ffn_in['router_w'], 'L1_ffn_router_b': _L1_ffn_in['router_b'], 'L1_ffn_spec_w1': _L1_ffn_in['spec_w1'], 'L1_ffn_spec_b1': _L1_ffn_in['spec_b1'], 'L1_ffn_spec_w2': _L1_ffn_in['spec_w2'], 'L1_ffn_spec_b2': _L1_ffn_in['spec_b2']}

def reference(x, ctx_1024, mask_BxS2_ik0, L0_xattn_Wq, L0_xattn_Wk, L0_xattn_Wv, L0_xattn_Wo, L0_attn_A_log, L0_attn_W_B, L0_attn_W_C, L0_attn_D_skip, L0_attn_log_dt, L0_attn_W_in, L0_attn_b_in, L0_attn_W_out, L0_attn_b_out, L0_attn_ln_g, L0_attn_ln_b, L0_ffn_w_q, L0_ffn_bn_gamma, L0_ffn_bn_beta, L0_ffn_keys, L0_ffn_down_embed, L0_ffn_up_embed, L1_xattn_Wq, L1_xattn_bq, L1_xattn_Wk, L1_xattn_bk, L1_xattn_Wv, L1_xattn_bv, L1_xattn_Wo, L1_xattn_bo, L1_xattn_w1, L1_xattn_b1, L1_xattn_w2, L1_xattn_b2, L1_xattn_w3, L1_xattn_b3, L1_attn_w_qkv, L1_attn_w_o, L1_ffn_shared_w1, L1_ffn_shared_b1, L1_ffn_shared_w2, L1_ffn_shared_b2, L1_ffn_router_w, L1_ffn_router_b, L1_ffn_spec_w1, L1_ffn_spec_b1, L1_ffn_spec_w2, L1_ffn_spec_b2):
    import jax
    import jax.numpy as jnp

    def _L0_xattn_ref(queries, keys, values, masks, Wq, Wk, Wv, Wo):
        import jax, jax.numpy as jnp
        import numpy as np
        import math
        B, S, D, H = (2, 1024, 512, 16)
        DH = D // H

        def _split_heads(x):
            b, s, _ = x.shape
            return x.reshape(b, s, H, DH).transpose(0, 2, 1, 3)
        Q = _split_heads(queries @ Wq)
        K = _split_heads(keys @ Wk)
        V = _split_heads(values @ Wv)
        scale = math.sqrt(DH)
        scores = jnp.einsum('bhqd,bhkd->bhqk', Q, K) / scale
        scores = jnp.where(masks[:, None, None, :] == 0, -jnp.inf, scores)
        attn = jax.nn.softmax(scores, axis=-1)
        out = jnp.einsum('bhqk,bhkd->bhqd', attn, V)
        out = out.transpose(0, 2, 1, 3).reshape(queries.shape[0], queries.shape[1], D)
        return out @ Wo

    def _L0_attn_ref(x, A_log, W_B, W_C, D_skip, log_dt, W_in, b_in, W_out, b_out, ln_g, ln_b):
        import jax, jax.numpy as jnp
        import numpy as np
        B, L, D, S = (4, 1024, 512, 16)
        Bb, Ll, Dd = x.shape
        residual = x
        mu = x.mean(-1, keepdims=True)
        var = ((x - mu) ** 2).mean(-1, keepdims=True)
        xn = (x - mu) / jnp.sqrt(var + 1e-05) * ln_g + ln_b
        xz = xn @ W_in.T + b_in
        x_proj, z = jnp.split(xz, 2, axis=-1)
        z = jax.nn.silu(z)
        dt = jnp.clip(jnp.exp(log_dt), 0.0001, 1.0)
        A_bar = jnp.exp(-jnp.exp(A_log) * dt[:, None])
        A_bar = jnp.clip(A_bar, 1e-08, 1.0 - 1e-08)
        B_proj = x_proj @ W_B.T * dt.mean()
        t_idx = jnp.arange(Ll, dtype=jnp.float32)
        log_A = jnp.log(A_bar)
        A_mean = jnp.exp(t_idx[:, None, None] * log_A[None]).mean(axis=1)
        kernel = jnp.flip(A_mean.T, -1)[:, None, :]
        lhs = jnp.transpose(B_proj, (0, 2, 1))
        x_mean = jax.lax.conv_general_dilated(lhs, kernel, window_strides=(1,), padding=((Ll - 1, 0),), dimension_numbers=('NCH', 'OIH', 'NCH'), feature_group_count=kernel.shape[0])
        x_mean = jnp.transpose(x_mean, (0, 2, 1))
        y = x_mean @ W_C.T + D_skip * x_proj
        y = y * z
        y = y @ W_out.T + b_out
        return y + residual

    def _L0_ffn_ref(x, w_q, bn_gamma, bn_beta, keys, down_embed, up_embed):
        import jax, jax.numpy as jnp
        import numpy as np
        H = 8
        KD = 128
        TOPK = 8
        NUM_KEYS = 128
        N_EXPERTS = NUM_KEYS * NUM_KEYS
        N_DIM = 512
        BN_EPS = 1e-05

        def gelu_new(x):
            c = jnp.sqrt(jnp.asarray(2.0 / jnp.pi, x.dtype))
            return 0.5 * x * (1.0 + jnp.tanh(c * (x + 0.044715 * x * x * x)))
        b, n, d = x.shape
        q = jnp.einsum('bnd,de->bne', x, w_q)
        mean = jnp.mean(q, axis=(0, 1))
        var = jnp.var(q, axis=(0, 1))
        q = (q - mean) * jax.lax.rsqrt(var + BN_EPS) * bn_gamma + bn_beta
        q = q.reshape(b, n, 2, H, KD).transpose(2, 0, 1, 3, 4)
        sim = jnp.einsum('pbnhd,hkpd->pbnhk', q, keys)
        sx, ix = jax.lax.top_k(sim[0], TOPK)
        sy, iy = jax.lax.top_k(sim[1], TOPK)
        all_scores = (sx[..., :, None] + sy[..., None, :]).reshape(b, n, H, TOPK * TOPK)
        all_indices = (ix[..., :, None] * NUM_KEYS + iy[..., None, :]).reshape(b, n, H, TOPK * TOPK)
        scores, pk = jax.lax.top_k(all_scores, TOPK)
        indices = jnp.take_along_axis(all_indices, pk, axis=-1)
        wd = down_embed[indices]
        wu = up_embed[indices]
        h = jnp.einsum('bnd,bnhkd->bnhk', x, wd)
        h = gelu_new(h)
        h = jax.nn.softmax(scores, axis=-1) * h
        out = jnp.einsum('bnhk,bnhkd->bnd', h, wu)
        return out

    def _L1_xattn_ref(query, key, value, Wq, bq, Wk, bk, Wv, bv, Wo, bo, w1, b1, w2, b2, w3, b3):
        import jax, jax.numpy as jnp
        import numpy as np
        import math
        B, S, D, H = (1, 1024, 512, 16)
        DK = D // H
        DH = 64
        LOG_T_MIN = math.log(0.1)
        LOG_T_MAX = math.log(10.0)

        def _linear(x, W, b):
            return x @ W.T + b
        b, sq, d = query.shape
        sk = key.shape[1]
        h, dk = (H, DK)
        Q = _linear(query, Wq, bq).reshape(b, sq, h, dk).transpose(0, 2, 1, 3)
        K = _linear(key, Wk, bk).reshape(b, sk, h, dk).transpose(0, 2, 1, 3)
        V = _linear(value, Wv, bv).reshape(b, sk, h, dk).transpose(0, 2, 1, 3)
        qk = jnp.einsum('bhqd,bhkd->bhqk', Q, K)
        scores = qk / math.sqrt(dk)
        mean_sim = scores.mean(axis=(-2, -1))
        max_sim = scores.max(axis=-1).mean(axis=-1)
        probs = jax.nn.softmax(scores, axis=-1)
        entropy_proxy = jnp.var(probs, axis=-1, ddof=1).mean(axis=-1)
        feats = jnp.stack([mean_sim, max_sim, entropy_proxy], axis=-1)
        hidden = jax.nn.gelu(_linear(feats, w1, b1), approximate=False)
        hidden = jax.nn.gelu(_linear(hidden, w2, b2), approximate=False)
        log_t = jnp.clip(_linear(hidden, w3, b3), LOG_T_MIN, LOG_T_MAX)
        t = jnp.exp(log_t)[..., None]
        attn_scores = qk / (2.0 * t)
        attn = jax.nn.softmax(attn_scores, axis=-1)
        attn = jnp.nan_to_num(attn, nan=0.0)
        out = jnp.einsum('bhqk,bhkd->bhqd', attn, V)
        out = out.transpose(0, 2, 1, 3).reshape(b, sq, d)
        return _linear(out, Wo, bo)

    def _L1_attn_ref(x, w_qkv, w_o):
        import jax, jax.numpy as jnp
        import numpy as np
        N_HEADS = 16
        D_MODEL = 512
        SEQ_LEN = 1024
        BATCH = 4
        *lead, seq_len, d_model = x.shape
        head_dim = d_model // N_HEADS
        qkv = x @ w_qkv
        qkv = qkv.reshape(*qkv.shape[:-1], N_HEADS, 3 * head_dim)
        qkv = jnp.einsum('...Thd->...hTd', qkv)
        q, k, v = jnp.split(qkv, 3, axis=-1)
        scores = jnp.einsum('...hqd,...hkd->...hqk', q, k) / np.sqrt(d_model).astype(x.dtype)
        causal = jnp.tri(seq_len, dtype=bool)
        scores = jnp.where(causal, scores, jnp.asarray(-1e+30, dtype=scores.dtype))
        attn = jax.nn.softmax(scores, axis=-1)
        out = jnp.einsum('...hqk,...hkd->...qhd', attn, v)
        out = out.reshape(*out.shape[:-2], d_model)
        return out @ w_o

    def _L1_ffn_ref(x, shared_w1, shared_b1, shared_w2, shared_b2, router_w, router_b, spec_w1, spec_b1, spec_w2, spec_b2):
        import jax, jax.numpy as jnp
        import numpy as np
        D_MODEL = 512
        D_FF = 2048
        N_EXPERTS = 8
        TOP_K = 2

        def _ffn(x, w1, b1, w2, b2):
            h = jax.nn.gelu(x @ w1.T + b1)
            return h @ w2.T + b2
        B, T, D = x.shape
        xf = x.reshape(-1, D)
        U = xf.shape[0]
        logits = xf @ router_w.T + router_b
        routing = jax.nn.softmax(logits, axis=-1)
        sel_w, sel_idx = jax.lax.top_k(routing, TOP_K)
        sel_w = sel_w / sel_w.sum(axis=-1, keepdims=True)
        comb = jnp.zeros_like(routing).at[jnp.arange(U)[:, None], sel_idx].set(sel_w)
        shared_out = _ffn(xf, shared_w1, shared_b1, shared_w2, shared_b2)

        def body(acc, params):
            w1, b1, w2, b2, we = params
            return (acc + we[:, None] * _ffn(xf, w1, b1, w2, b2), None)
        acc0 = jnp.zeros_like(shared_out)
        acc, _ = jax.lax.scan(body, acc0, (spec_w1, spec_b1, spec_w2, spec_b2, comb.T))
        return (shared_out + acc).reshape(B, T, D)
    x = x + _L0_xattn_ref(_layernorm(x, axis=-1), ctx_1024, ctx_1024, mask_BxS2_ik0, L0_xattn_Wq, L0_xattn_Wk, L0_xattn_Wv, L0_xattn_Wo)
    x = x + _L0_attn_ref(_layernorm(x, axis=-1), L0_attn_A_log, L0_attn_W_B, L0_attn_W_C, L0_attn_D_skip, L0_attn_log_dt, L0_attn_W_in, L0_attn_b_in, L0_attn_W_out, L0_attn_b_out, L0_attn_ln_g, L0_attn_ln_b)
    x = x + _L0_ffn_ref(_layernorm(x, axis=-1), L0_ffn_w_q, L0_ffn_bn_gamma, L0_ffn_bn_beta, L0_ffn_keys, L0_ffn_down_embed, L0_ffn_up_embed)
    x = x + _L1_xattn_ref(_layernorm(x, axis=-1), ctx_1024, ctx_1024, L1_xattn_Wq, L1_xattn_bq, L1_xattn_Wk, L1_xattn_bk, L1_xattn_Wv, L1_xattn_bv, L1_xattn_Wo, L1_xattn_bo, L1_xattn_w1, L1_xattn_b1, L1_xattn_w2, L1_xattn_b2, L1_xattn_w3, L1_xattn_b3)
    x = x + _L1_attn_ref(_layernorm(x, axis=-1), L1_attn_w_qkv, L1_attn_w_o)
    x = x + _L1_ffn_ref(_layernorm(x, axis=-1), L1_ffn_shared_w1, L1_ffn_shared_b1, L1_ffn_shared_w2, L1_ffn_shared_b2, L1_ffn_router_w, L1_ffn_router_b, L1_ffn_spec_w1, L1_ffn_spec_b1, L1_ffn_spec_w2, L1_ffn_spec_b2)
    return x

_drawn_inputs = setup_inputs


def setup_inputs(seed=0):
    import zlib

    import numpy as np

    out = dict(_drawn_inputs(seed))
    spreads = {'L0_attn_D_skip': (1.0, 0.6),
     'L0_attn_ln_g': (1.0, 0.6),
     'L0_attn_ln_b': (0.0, 0.8),
     'L0_ffn_bn_gamma': (1.0, 0.6),
     'L0_ffn_bn_beta': (0.0, 0.8),
     'L1_ffn_shared_b1': (0.0, 0.327),
     'L1_ffn_shared_b2': (0.0, 0.1),
     'L1_ffn_router_b': (0.0, 0.1),
     'L1_ffn_spec_b1': (0.0, 0.477),
     'L1_ffn_spec_b2': (0.0, 0.1)}
    factors = {'L0_attn_A_log': 40.237,
     'L0_attn_W_B': 64.0,
     'L0_attn_W_C': 50.385,
     'L0_attn_log_dt': 8.0,
     'L0_attn_b_in': 8.0,
     'L0_attn_b_out': 4.008,
     'L0_ffn_w_q': 8.0,
     'L0_ffn_keys': 8.0,
     'L0_ffn_down_embed': 8.0,
     'L0_ffn_up_embed': 8.0,
     'L1_xattn_Wq': 4.861,
     'L1_xattn_bq': 8.0,
     'L1_xattn_Wk': 4.644,
     'L1_xattn_bk': 200.0,
     'L1_xattn_bv': 8.0,
     'L1_xattn_bo': 4.726,
     'L1_xattn_w1': 64.0,
     'L1_xattn_b1': 8.0,
     'L1_xattn_w2': 45.752,
     'L1_xattn_b2': 8.0,
     'L1_xattn_w3': 45.752}
    for name, (base, spread) in spreads.items():
        noise = np.random.default_rng([zlib.crc32(name.encode()), seed]).standard_normal(out[name].shape)
        drawn = base * np.exp(spread * noise) if base else spread * noise
        out[name] = jnp.asarray(drawn.astype(out[name].dtype))
    for name, factor in factors.items():
        out[name] = (out[name] * factor).astype(out[name].dtype)
    return out
```

```python
import math
from contextlib import ExitStack

import numpy as np

import concourse.bass as bass
from concourse import mybir

F32 = mybir.dt.float32
F32R = mybir.dt.float32r
I32 = mybir.dt.int32
U32 = mybir.dt.uint32
ALU = mybir.AluOpType
ACT = mybir.ActivationFunctionType
AX = mybir.AxisListType

P = 128
B, S, D = 8, 64, 512
T = B * S
TT = T // P
BT = P // S
DC = D // P
H, DH = 16, 32
HC = P // DH
PAIRS = H // 2
KEYS = 1601
KT = -(-KEYS // P)
CHUNK = 512
NCHUNK = -(-KEYS // CHUNK)
NS = 16
PH, PK, NKEY, PTOP = 8, 128, 128, 8
NEXP = 8
FF = 2048
FC = FF // P
NEG = -1.0e30
LN_EPS = 1e-5
LOG_T_MIN, LOG_T_MAX = math.log(0.1), math.log(10.0)
DT_MIN, DT_MAX = 1e-4, 1.0
LOG_A_MIN, LOG_A_MAX = math.log(1e-8), math.log(1.0 - 1e-8)
BIG = 3.0e38

C_IDENT, C_ONES, C_CAUSAL = 0, P, 2 * P
C_STACK = 3 * P
C_HEAD = C_STACK + S
C_HALF = C_HEAD + HC
C_BAT = C_HALF + 2
C_STATE = C_BAT + B
C_IOTA = C_STATE + NS
C_TIME = C_IOTA + 8
C_TOP = C_TIME + S
C_BOT = C_TOP + P
C_DIAG = C_BOT + P
C_END = C_DIAG + D


def constants():
    c = np.zeros((P, C_END), np.float32)
    p = np.arange(P)
    c[:, C_IDENT:C_IDENT + P] = np.eye(P)
    c[:, C_ONES:C_ONES + P] = 1.0
    same = (p[:, None] // S) == (p[None, :] // S)
    c[:, C_CAUSAL:C_CAUSAL + P] = np.where(same & (p[None, :] <= p[:, None]), 0.0, NEG)
    c[:, C_STACK:C_STACK + S] = np.concatenate([np.eye(S), np.eye(S)])
    c[:, C_HEAD:C_HEAD + HC] = (p[:, None] // DH) == np.arange(HC)
    c[:, C_HALF] = (p < S) / S
    c[:, C_HALF + 1] = (p >= S) / S
    c[:, C_BAT:C_BAT + B] = (p[:, None] // NS) == np.arange(B)
    c[:, C_STATE:C_STATE + NS] = (p[:, None] % NS) == np.arange(NS)
    c[:, C_IOTA:C_IOTA + 8] = np.arange(8)
    c[:, C_TIME:C_TIME + S] = np.arange(S)[::-1]
    c[:, C_TOP:C_TOP + P] = p < S
    c[:, C_BOT:C_BOT + P] = p >= S
    c[:, C_DIAG:C_DIAG + D] = (p[:, None] // S) == (np.arange(D)[None, :] // DH) % 2
    return c


class Chain:

    def __init__(self, eng, sem):
        self.eng, self.sem, self.n, self.at, self.i, self.per = eng, sem, 0, 0, None, 0

    def loop(self, i, per):
        self.i, self.per, self.at = i, per, 0

    def end(self, rounds):
        assert self.at == self.per, f"{self.sem}: {self.at} steps in a round, not {self.per}"
        self.n += rounds * self.per
        self.i, self.at = None, 0

    def inc(self, ins):
        ins.then_inc(self.sem, 1)
        self.at += 1
        if self.i is None:
            self.n, self.at = self.n + 1, 0

    def wait(self):
        if self.i is None:
            self.eng.wait_ge(self.sem, self.n)
        else:
            self.eng.wait_ge(self.sem, self.i * self.per + (self.n + self.at))

    def link(self, ins):
        self.inc(ins)
        self.wait()


class Scope:

    def __init__(self, nc, tag):
        self.nc, self.tag, self.ctx, self.sems = nc, tag, ExitStack(), []

    def __enter__(self):
        return self

    def __exit__(self, *e):
        self.nc.clear_and_free_semaphores(self.sems)
        self.nc.all_engine_barrier()
        return self.ctx.__exit__(*e)

    def sb(self, name, shape, dt=F32):
        return self.ctx.enter_context(self.nc.sbuf_tensor(f"{self.tag}_{name}", shape, dt))

    def ps(self, name, shape):
        return self.ctx.enter_context(self.nc.psum_tensor(f"{self.tag}_{name}", shape, F32))

    def sem(self, name):
        self.sems.append(self.nc.alloc_semaphore(f"{self.tag}_{name}"))
        return self.sems[-1]


class Norm:

    def __init__(self, sc, tag, x, u, uT, ident):
        self.x, self.u, self.uT, self.ident = x, u, uT, ident
        self.stat = sc.sb(tag + "stat", [P, TT, 6])
        self.mv = sc.sb(tag + "mv", [P, TT, 2])
        self.ve = sc.sb(tag + "ve", [P, TT])
        self.sd = sc.sb(tag + "sd", [P, TT])
        self.rs = sc.sb(tag + "rs", [P, TT])
        self.var_ready = sc.sem(tag + "var_ready")
        self.root_ready = sc.sem(tag + "root_ready")
        self.u_ready = sc.sem(tag + "u_ready")
        self.turned = sc.sem(tag + "turned")
        self.uT_ready = sc.sem(tag + "uT_ready")

    def dve_var(self, ch):
        v = ch.eng
        for t in range(TT):
            ch.inc(v.bn_stats(self.stat[:, t, :], self.x[:, t, :]))
        ch.wait()
        for t in range(TT):
            ch.inc(v.bn_aggr(self.mv[:, t, :], self.stat[:, t, :]))
        ch.wait()
        v.tensor_scalar(self.ve[:, :], self.mv[:, :, 1], LN_EPS, None, ALU.add).then_inc(self.var_ready, 1)

    def act_root(self, a):
        a.wait_ge(self.var_ready, 1)
        a.activation(self.sd[:, :], self.ve[:, :], ACT.Sqrt).then_inc(self.root_ready, 1)

    def dve_u(self, ch, gain=None, shift=None):
        v = ch.eng
        v.wait_ge(self.root_ready, 1)
        ch.link(v.reciprocal(self.rs[:, :], self.sd[:, :]))
        for t in range(TT):
            ins = v.tensor_scalar(self.u[:, t, :], self.x[:, t, :], self.mv[:, t, 0:1], self.rs[:, t:t + 1],
                                  ALU.subtract, ALU.mult)
            if gain is not None:
                ch.link(ins)
                ch.link(v.tensor_tensor(self.u[:, t, :], self.u[:, t, :], gain, ALU.mult))
                ins = v.tensor_tensor(self.u[:, t, :], self.u[:, t, :], shift, ALU.add)
            ins.then_inc(self.u_ready, 1)

    def pe_turn(self, pe, banks):
        for t in range(TT):
            pe.wait_ge(self.u_ready, t + 1)
            for d in range(DC):
                ins = pe.transpose(banks[t][:, d * P:(d + 1) * P], self.u[:, t, d * P:(d + 1) * P], self.ident)
            ins.then_inc(self.turned, 1)

    def evac(self, eng, banks, copy):
        for t in range(TT):
            eng.wait_ge(self.turned, t + 1)
            copy(self.uT[:, :, t * P:(t + 1) * P],
                 banks[t][:, :].rearrange("p (d n) -> p d n", d=DC)).then_inc(self.uT_ready, 1)


def product(pe, out, lhs, rhs, n, first=True, last=True):
    for k in range(n):
        ins = pe.matmul(out, lhs(k), rhs(k), start=first and k == 0, stop=last and k == n - 1)
    return ins


def split_product(pe, out, lhs_hi, lhs_lo, rhs_hi, rhs_lo, n, first=True, last=True):
    for k in range(n):
        pe.matmul(out, lhs_hi(k), rhs_hi(k), start=first and k == 0, stop=False)
        pe.matmul(out, lhs_hi(k), rhs_lo(k), start=False, stop=False)
        ins = pe.matmul(out, lhs_lo(k), rhs_hi(k), start=False, stop=last and k == n - 1)
    return ins


def load_and_norm(nc, x_dram, const_dram, const, x):
    with Scope(nc, "ld") as sc:
        done = sc.sem("done")
        with nc.Block() as block:
            @block.sync
            def _(sp):
                sp.dma_start(x[:, :, :], x_dram.rearrange("(i e) t d -> (e t) i d", e=BT)).then_inc(done, 16)
                sp.dma_start(const[:, :], const_dram).then_inc(done, 16)
                sp.wait_ge(done, 32)


def query_stage(nc, tag, const, x, qT, wq_dram, bq_dram):
    with Scope(nc, tag) as sc:
        u = sc.sb("u", [P, TT, D])
        uT = sc.sb("uT", [P, DC, T])
        wq = sc.sb("wq", [P, DC, D])
        bq = sc.sb("bq", [P, DC])
        banks = [sc.ps(f"b{i}", [P, 512]) for i in range(8)]
        norm = Norm(sc, "n", x, u, uT, const[:, C_IDENT:C_IDENT + P])
        w_in, q_done, q_out, dve_step = (sc.sem(n) for n in ("w_in", "q_done", "q_out", "dve_step"))
        with nc.Block() as block:
            @block.sync
            def _(sp):
                sp.dma_start(wq[:, :, :], wq_dram.rearrange("(k p) n -> p k n", p=P)).then_inc(w_in, 16)
                if bq_dram is not None:
                    sp.dma_start(bq[:, :], bq_dram.rearrange("p c -> p c")).then_inc(w_in, 16)

            @block.vector
            def _(v):
                ch = Chain(v, dve_step)
                norm.dve_var(ch)
                norm.dve_u(ch)
                norm.evac(v, banks, v.tensor_copy)

            @block.scalar
            def _(a):
                norm.act_root(a)
                if bq_dram is not None:
                    a.wait_ge(w_in, 32)
                for c in range(DC):
                    a.wait_ge(q_done, c + 1)
                    if bq_dram is not None:
                        a.activation(qT[:, c, :], banks[4 + c][:, :], ACT.Identity, bias=bq[:, c:c + 1]).then_inc(q_out, 1)
                    else:
                        a.activation(qT[:, c, :], banks[4 + c][:, :], ACT.Copy).then_inc(q_out, 1)

            @block.tensor
            def _(pe):
                norm.pe_turn(pe, banks)
                pe.wait_ge(norm.uT_ready, TT)
                pe.wait_ge(w_in, 32 if bq_dram is not None else 16)
                for c in range(DC):
                    product(pe, banks[4 + c][:, :], lambda k: wq[:, k, c * P:(c + 1) * P],
                            lambda k: uT[:, k, :], DC).then_inc(q_done, 1)


def split_buffer(sc, name, shape):
    hi = sc.sb(name + "_hi", shape, F32R)
    at = -(-sc.nc.sbuf_base // 32) * 32
    lo = sc.sb(name + "_lo", shape, F32R)
    raw = sc.nc.alloc_sbuf_tensor_at(f"{sc.tag}_{name}_raw", shape, F32, offset=at)
    return hi, lo, raw


def cross_attention(nc, tag, const, qT, ctx_dram, wk_dram, wv_dram, mask_dram=None, adapt=None):
    NSB = PAIRS if adapt else 3
    scale = float(DH) ** -0.5
    with Scope(nc, tag) as sc:
        sem = sc.sem
        ctx = [split_buffer(sc, f"ctx{s}", [P, DC, CHUNK]) for s in range(2)]
        wk = split_buffer(sc, "wk", [P, DC, D])
        wv = split_buffer(sc, "wv", [P, DC, D])
        kT = sc.sb("kT", [P, DC, KEYS])
        vk = sc.sb("vk", [P, KT, D])
        sco = sc.sb("sco", [P, NSB, KEYS])
        wT = sc.sb("wT", [P, 2, 4, P])
        qbd = sc.sb("qbd", [P, PAIRS, P])
        mx, nmx, rsum, rinv = (sc.sb(n, [P, PAIRS]) for n in ("mx", "nmx", "rsum", "rinv"))
        onorm = sc.sb("onorm", [P, D])
        ps_s = sc.ps("ps_s", [P, 4 * 512])
        ring = [sc.ps(f"ring{i}", [P, 512]) for i in range(2)]
        ps_o = sc.ps("ps_o", [P, 2, 512])
        ps_m = ps_o[:, 1, :]
        if mask_dram is not None:
            mask_i = sc.sb("mask_i", [P, KEYS], I32)
            mask_f = sc.sb("mask_f", [P, KEYS])
        if adapt:
            p1 = sc.sb("p1", [P, KEYS])
            bk, bv = sc.sb("bk", [P, DC]), sc.sb("bv", [P, DC])
            w1T, w2T, w3T = sc.sb("w1T", [3, 64]), sc.sb("w2T", [64, 64]), sc.sb("w3T", [64, 1])
            b12, b3 = sc.sb("b12", [64, 2]), sc.sb("b3", [1, 1])
            kparts = sc.sb("kparts", [P, DC, NCHUNK])
            ksum = sc.sb("ksum", [P, DC])
            stats = sc.sb("stats", [P, PAIRS, 3])
            sums = sc.sb("sums", [P, PAIRS, 2])
            tmp, temp = sc.sb("tmp", [P, PAIRS]), sc.sb("temp", [P, PAIRS])
            featT = sc.sb("featT", [3, H])
            hid = sc.sb("hid", [64, 2, H])
            logt, invt = sc.sb("logt", [1, H]), sc.sb("invt", [1, H])

        w_in = [sem(f"w_in{s}") for s in range(2)]
        small_in, w_hi_ready, w_split = (sem(n) for n in ("small_in", "w_hi_ready", "w_split"))
        ctx_in = [sem(f"ctx_in{s}") for s in range(2)]
        ctx_hi_ready = sem("ctx_hi")
        ctx_split = sem("ctx_split")
        group = sem("group")
        act_evac = sem("act_evac")
        dve_evac = sem("dve_evac")
        q_ready = sem("q_ready")
        scored = sem("scored")
        taken = sem("taken")
        negated = sem("negated")
        probs = sem("probs")
        pv = sem("pv")
        normed = sem("normed")
        o_ready = sem("o_ready")
        mask_in, mask_used = sem("mask_in"), sem("mask_used")
        dve_step = sem("dve_step")
        squared, plain = sem("squared"), sem("plain")
        (ksum_ready, mean_done, stats_ready, feat_done, feat_ready, h1_done, h1_ready, h2_done, h2_ready, t_done,
         t_clip, t_ready, spread, temp_ready) = (sem(n) for n in (
            "ksum_ready", "mean_done", "stats_ready", "feat_done", "feat_ready", "h1_done", "h1_ready", "h2_done",
            "h2_ready", "t_done", "t_clip", "t_ready", "spread", "temp_ready"))
        pool_mark, pe_mark, dve_mark = sem("pool_mark"), sem("pe_mark"), sem("dve_mark")

        widths = [min(CHUNK, KEYS - n * CHUNK) for n in range(NCHUNK)]
        ktiles = [min(P, KEYS - t * P) for t in range(KT)]
        in_chunk = [range(n * CHUNK // P, min(KT, (n + 1) * CHUNK // P)) for n in range(NCHUNK)]
        QUADS = -(-KT // 4)

        uses = []
        for n in range(NCHUNK):
            uses += [("k", n, c, "act") for c in range(DC)]
            uses += [("v", n, t, "dve") for t in in_chunk[n]]
        for p in range(PAIRS):
            uses += [("w", p, g, "act" if (g + p) % 2 else "dve") for g in range(QUADS)]
        uses.append(("o", 0, 0, "dve"))
        PER = len(uses)
        assert PER % 2 == 0, "a round has to keep the banks' parity"
        nth, count = [], {"act": 0, "dve": 0}
        for u in uses:
            count[u[3]] += 1
            nth.append(count[u[3]])
        where = {u[:3]: i for i, u in enumerate(uses)}
        evac_sem = {"act": act_evac, "dve": dve_evac}
        last_of = [where[("v", n, in_chunk[n][-1])] for n in range(NCHUNK)]

        def emptied(eng, b, u, back=0):
            by = uses[u][3]
            eng.wait_ge(evac_sem[by], b * count[by] + ((1 - back) * count[by] + nth[u]))

        def filled(eng, b, u, back=0):
            eng.wait_ge(group, b * PER + ((1 - back) * PER + u + 1))

        with nc.Block() as block:
            @block.sync
            def _(sp):
                for s, (w, src) in enumerate(((wk, wk_dram), (wv, wv_dram))):
                    sp.dma_start(w[2][:, :, :], src.rearrange("(k p) n -> p k n", p=P)).then_inc(w_in[s], 16)
                if adapt:
                    for dst, src in ((bk, "bk"), (bv, "bv"), (w1T, "w1T"), (w2T, "w2T"), (w3T, "w3T"), (b12, "b12"), (b3, "b3")):
                        sp.dma_start(dst[:, :], adapt[src]).then_inc(small_in, 16)
                with sp.Fori(0, B) as b:
                    if mask_dram is not None:
                        sp.wait_ge(mask_used, b + 1)
                        sp.dma_start(mask_i[:, :], mask_dram[bass.ds(b, 1), :].to_broadcast([P, KEYS])).then_inc(mask_in, 16)
                    for n in range(NCHUNK):
                        filled(sp, b, last_of[(n - 2) % NCHUNK], back=int(n < 2))
                        sp.dma_start(ctx[n % 2][2][:, :, 0:widths[n]],
                                     ctx_dram[bass.ds(b, 1), :, n * CHUNK:n * CHUNK + widths[n]].rearrange("o (k p) n -> p (o k) n", p=P)
                                     ).then_inc(ctx_in[n % 2], 16)

            @block.gpsimd
            def _(g):
                with g.Fori(0, B) as b:
                    for n in range(NCHUNK):
                        hi, lo, raw = ctx[n % 2]
                        w = widths[n]
                        g.wait_ge(ctx_in[n % 2], b * (16 * NCHUNK // 2) + 16 * (n // 2 + 1))
                        g.sem_inc(pool_mark, 1)
                        g.tensor_copy(hi[:, :, 0:w], raw[:, :, 0:w]).then_inc(ctx_hi_ready, 1)
                        g.wait_ge(ctx_hi_ready, b * NCHUNK + (n + 1))
                        g.tensor_tensor(lo[:, :, 0:w], raw[:, :, 0:w], hi[:, :, 0:w].bitcast(F32), ALU.subtract).then_inc(ctx_split, 1)

            @block.tensor
            def _(pe):
                pe.sem_inc(group, PER)
                pe.wait_ge(w_split, 2)
                if adapt:
                    pe.wait_ge(small_in, 16 * 7)
                with pe.Fori(0, B) as b:
                    def claim(u):
                        emptied(pe, b, (u - 2) % PER, back=int(u < 2))
                        return ring[u % 2]

                    for n in range(NCHUNK):
                        pe.wait_ge(ctx_split, b * NCHUNK + (n + 1))
                        h, l, _ = ctx[n % 2]
                        w = widths[n] + widths[n] % 2
                        for c in range(DC):
                            split_product(pe, claim(where[("k", n, c)])[:, 0:w],
                                          lambda k: wk[0][:, k, c * P:(c + 1) * P], lambda k: wk[1][:, k, c * P:(c + 1) * P],
                                          lambda k: h[:, k, 0:w], lambda k: l[:, k, 0:w], DC).then_inc(group, 1)
                        for t in in_chunk[n]:
                            o, m = t * P - n * CHUNK, ktiles[t]
                            split_product(pe, claim(where[("v", n, t)])[0:m, :],
                                          lambda k: h[:, k, o:o + m], lambda k: l[:, k, o:o + m],
                                          lambda k: wv[0][:, k, :], lambda k: wv[1][:, k, :], DC).then_inc(group, 1)

                    pe.wait_ge(q_ready, b + 1)
                    emptied(pe, b, where[("k", NCHUNK - 1, DC - 1)])

                    def score(p, n):
                        if n == 0:
                            pe.wait_ge(taken, b * PAIRS + (p + 1))
                        ins = pe.matmul(ps_s[:, n * CHUNK:n * CHUNK + widths[n]], qbd[:, p, :],
                                        kT[:, p // 2, n * CHUNK:n * CHUNK + widths[n]], start=True, stop=True)
                        if n == NCHUNK - 1:
                            ins.then_inc(scored, 1)

                    def turn(p, g):
                        if g == 0:
                            pe.wait_ge(probs, b * PAIRS + (p + 1))
                        bank = claim(where[("w", p, g)])
                        for j in range(4 * g, min(KT, 4 * g + 4)):
                            m = ktiles[j]
                            ins = pe.transpose(bank[0:m, (j % 4) * P:(j % 4) * P + P],
                                               sco[:, p % NSB, j * P:j * P + m], const[:, C_IDENT:C_IDENT + P])
                        ins.then_inc(group, 1)

                    def weigh(p, g):
                        emptied(pe, b, where[("w", p, g)])
                        if g == 0:
                            pe.wait_ge(normed, b * PAIRS + (p + PAIRS - 1))
                        for j in range(4 * g, min(KT, 4 * g + 4)):
                            m = ktiles[j]
                            ins = pe.matmul(ps_o[:, p % 2, 0:P], wT[0:m, g % 2, j % 4, :], vk[0:m, j, P * (p // 2):P * (p // 2) + P],
                                            start=(j == 0), stop=(j == KT - 1), skip_group_check=True)
                        if g == QUADS - 1:
                            ins.then_inc(pv, 1)

                    def pair(p, q):
                        for what, g in (("t", 0), ("t", 1), ("s", 0), ("w", 0), ("t", 2), ("s", 1), ("w", 1), ("t", 3),
                                        ("s", 2), ("s", 3), ("w", 2), ("w", 3)):
                            if what == "s" and p is not None:
                                score(p, g)
                            if what == "t" and q is not None:
                                turn(q, g)
                            if what == "w" and q is not None:
                                weigh(q, g)

                    if not adapt:
                        emptied(pe, b, last_of[-1])
                        for p in range(PAIRS + 2):
                            pair(p if p < PAIRS else None, p - 2 if p >= 2 else None)
                    else:
                        for p in range(PAIRS):
                            pair(p, None)
                        pe.wait_ge(ksum_ready, b + 1)
                        for p in range(PAIRS):
                            ins = pe.matmul(ps_m[:, p:p + 1], qbd[:, p, :], ksum[:, p // 2:p // 2 + 1], start=True, stop=True)
                        ins.then_inc(mean_done, 1)
                        pe.wait_ge(stats_ready, b + 1)
                        for p in range(PAIRS):
                            ins = pe.matmul(ps_m[0:3, 16 + 2 * p:18 + 2 * p], stats[:, p, :], const[:, C_HALF:C_HALF + 2], start=True, stop=True)
                        ins.then_inc(feat_done, 1)
                        pe.wait_ge(feat_ready, b + 1)
                        pe.matmul(ps_m[0:64, 32:48], w1T[:, :], featT[:, :], start=True, stop=True).then_inc(h1_done, 1)
                        pe.wait_ge(h1_ready, b + 1)
                        pe.sem_inc(pe_mark, 1)
                        pe.matmul(ps_m[0:64, 48:64], w2T[:, :], hid[:, 0, :], start=True, stop=True).then_inc(h2_done, 1)
                        pe.wait_ge(h2_ready, b + 1)
                        pe.sem_inc(pe_mark, 1)
                        pe.matmul(ps_m[0:1, 64:80], w3T[:, :], hid[:, 1, :], start=True, stop=True).then_inc(t_done, 1)
                        pe.wait_ge(t_ready, b + 1)
                        iv = invt[0:1, :].rearrange("o (p e) -> o e p", e=2)
                        pe.matmul(ps_m[:, 80:88], const[0:1, C_TOP:C_TOP + P], iv[:, 0, :], start=True, stop=False)
                        pe.matmul(ps_m[:, 80:88], const[0:1, C_BOT:C_BOT + P], iv[:, 1, :], start=False, stop=True).then_inc(spread, 1)
                        emptied(pe, b, last_of[-1])
                        for p in range(PAIRS):
                            pair(None, p)
                    bank = claim(PER - 1)
                    pe.wait_ge(o_ready, b + 2)
                    for c in range(DC):
                        ins = pe.matmul(bank[:, c * S:(c + 1) * S], onorm[:, c * P:(c + 1) * P],
                                        const[:, C_STACK:C_STACK + S], start=True, stop=True)
                    ins.then_inc(group, 1)

            def turned_views(g, bank):
                if 4 * g + 4 <= KT:
                    return wT[:, g % 2, :, :].rearrange("p j n -> p (j n)"), bank[:, :]
                assert KT % 4 == 1
                return wT[0:ktiles[-1], g % 2, 0, :], bank[0:ktiles[-1], 0:P]

            @block.scalar
            def _(a):
                a.sem_inc(act_evac, count["act"])
                for s, w in enumerate((wk, wv)):
                    a.wait_ge(w_in[s], 16)
                    a.activation(w[0][:, :, :], w[2][:, :, :], ACT.Copy).then_inc(w_hi_ready, 1)
                if adapt:
                    a.wait_ge(small_in, 16 * 7)
                with a.Fori(0, B) as b:
                    def turn_evac(p):
                        for g in range(QUADS):
                            u = where[("w", p, g)]
                            if uses[u][3] == "act":
                                filled(a, b, u)
                                dst, src = turned_views(g, ring[u % 2])
                                a.activation(dst, src, ACT.Copy).then_inc(act_evac, 1)

                    for n in range(NCHUNK):
                        for c in range(DC):
                            u = where[("k", n, c)]
                            dst, src = kT[:, c, n * CHUNK:n * CHUNK + widths[n]], ring[u % 2][:, 0:widths[n]]
                            filled(a, b, u)
                            if adapt:
                                a.activation(dst, src, ACT.Identity, bias=bk[:, c:c + 1],
                                             accum_out=kparts[:, c, n:n + 1]).then_inc(act_evac, 1)
                            else:
                                a.activation(dst, src, ACT.Copy).then_inc(act_evac, 1)

                    if not adapt:
                        for p in range(PAIRS + 2):
                            if p >= 2:
                                turn_evac(p - 2)
                            if p < PAIRS:
                                a.wait_ge(negated, b * PAIRS + (p + 1))
                                row = sco[:, p % NSB, :]
                                a.activation(row, row, ACT.Exp, bias=nmx[:, p:p + 1], scale=scale,
                                             accum_out=rsum[:, p:p + 1]).then_inc(probs, 1)
                    else:
                        for p in range(PAIRS):
                            a.wait_ge(negated, b * PAIRS + (p + 1))
                            a.wait_ge(squared, b * PAIRS + (p + 1))
                            a.activation(p1[:, :], sco[:, p, :], ACT.Exp, bias=nmx[:, p:p + 1], scale=scale,
                                         accum_out=sums[:, p, 0:1]).then_inc(plain, 1)
                        a.wait_ge(h1_done, b + 1)
                        a.activation(hid[:, 0, :], ps_m[0:64, 32:48], ACT.Gelu, bias=b12[:, 0:1]).then_inc(h1_ready, 1)
                        a.wait_ge(h2_done, b + 1)
                        a.activation(hid[:, 1, :], ps_m[0:64, 48:64], ACT.Gelu, bias=b12[:, 1:2]).then_inc(h2_ready, 1)
                        a.wait_ge(t_clip, b + 1)
                        a.activation(invt[:, :], logt[:, :], ACT.Exp, scale=-1.0).then_inc(t_ready, 1)
                        a.wait_ge(temp_ready, b + 1)
                        for p in range(PAIRS + 1):
                            if p < PAIRS:
                                row = sco[:, p, :]
                                a.activation(row, row, ACT.Exp, bias=nmx[:, p:p + 1], scale=temp[:, p:p + 1],
                                             accum_out=rsum[:, p:p + 1]).then_inc(probs, 1)
                            if p >= 1:
                                turn_evac(p - 1)

            @block.vector
            def _(v):
                ch = Chain(v, dve_step)
                v.sem_inc(dve_evac, count["dve"])
                for s in (taken, o_ready, squared, mask_used):
                    v.sem_inc(s, 1)
                v.sem_inc(normed, PAIRS)
                for s, w in enumerate((wk, wv)):
                    v.wait_ge(w_hi_ready, s + 1)
                    v.tensor_tensor(w[1][:, :, :], w[2][:, :, :], w[0][:, :, :].bitcast(F32), ALU.subtract).then_inc(w_split, 1)
                with v.Fori(0, B) as b:
                    ch.loop(b, PAIRS + (6 if adapt else 1))

                    def take(p):
                        v.wait_ge(scored, b * PAIRS + (p + 1))
                        if mask_dram is not None:
                            if p >= NSB:
                                filled(v, b, where[("w", p - NSB, QUADS - 1)])
                            v.sem_inc(dve_mark, 1)
                            v.tensor_tensor_reduce(sco[:, p % NSB, :], ps_s[:, 0:KEYS], mask_f[:, :], 1.0, -BIG,
                                                   ALU.add, ALU.max, mx[:, p:p + 1]).then_inc(taken, 1)
                        else:
                            v.tensor_scalar(sco[:, p % NSB, :], ps_s[:, 0:KEYS], 1.0, -BIG, ALU.mult, ALU.max,
                                            accum_out=mx[:, p:p + 1]).then_inc(taken, 1)
                        v.wait_ge(taken, b * PAIRS + (p + 2))
                        v.tensor_scalar(nmx[:, p:p + 1], mx[:, p:p + 1], -scale, None, ALU.mult).then_inc(negated, 1)

                    def turn_evac(p):
                        for g in range(QUADS):
                            u = where[("w", p, g)]
                            if uses[u][3] == "dve":
                                filled(v, b, u)
                                v.tensor_copy(*turned_views(g, ring[u % 2])).then_inc(dve_evac, 1)

                    def norm(p):
                        v.wait_ge(pv, b * PAIRS + (p + 1))
                        ch.link(v.reciprocal(rinv[:, p:p + 1], rsum[:, p:p + 1]))
                        v.tensor_scalar(onorm[:, 64 * p:64 * p + 64], ps_o[:, p % 2, 64 * (p % 2):64 * (p % 2) + 64],
                                        rinv[:, p:p + 1], None, ALU.mult).then_inc(normed, 1)

                    def square(p):
                        v.wait_ge(plain, b * PAIRS + (p + 1))
                        v.tensor_tensor_reduce(p1[:, :], p1[:, :], p1[:, :], 1.0, 0.0, ALU.mult, ALU.add,
                                               sums[:, p, 1:2]).then_inc(squared, 1)

                    for p in range(PAIRS):
                        for e in range(2):
                            h = 2 * (p % 2) + e
                            ins = v.tensor_scalar(qbd[:, p, e * S:(e + 1) * S], qT[:, p // 2, bass.ds(b * S, S)],
                                                  const[:, C_HEAD + h:C_HEAD + h + 1], None, ALU.mult)
                    ins.then_inc(q_ready, 1)
                    if mask_dram is not None:
                        v.wait_ge(mask_in, b * 16 + 16)
                        ch.link(v.tensor_scalar(mask_f[:, :], mask_i[:, :], 0.0, NEG, ALU.is_equal, ALU.mult))
                        v.sem_inc(mask_used, 1)
                    for n in range(NCHUNK):
                        for t in in_chunk[n]:
                            u = where[("v", n, t)]
                            filled(v, b, u)
                            v.tensor_copy(vk[0:ktiles[t], t, :], ring[u % 2][0:ktiles[t], :]).then_inc(dve_evac, 1)

                    if not adapt:
                        for p in range(PAIRS + 2):
                            if p >= 3:
                                norm(p - 3)
                            if p >= 2:
                                turn_evac(p - 2)
                            if p < PAIRS:
                                take(p)
                        norm(PAIRS - 1)
                    else:
                        emptied(v, b, where[("k", NCHUNK - 1, DC - 1)])
                        v.tensor_reduce(ksum[:, :], kparts[:, :, :], AX.X, ALU.add).then_inc(ksum_ready, 1)
                        for p in range(PAIRS + 1):
                            if p < PAIRS:
                                take(p)
                            if p >= 1:
                                v.wait_ge(plain, b * PAIRS + p)
                                square(p - 1)
                        v.wait_ge(squared, b * PAIRS + (PAIRS + 1))
                        ch.link(v.reciprocal(rinv[:, :], sums[:, :, 0]))
                        ch.link(v.tensor_tensor(tmp[:, :], rinv[:, :], rinv[:, :], ALU.mult))
                        ch.link(v.tensor_tensor(tmp[:, :], tmp[:, :], sums[:, :, 1], ALU.mult))
                        v.tensor_scalar(stats[:, :, 1], mx[:, :], scale, None, ALU.mult)
                        v.tensor_scalar(stats[:, :, 2], tmp[:, :], -1.0 / KEYS, 1.0 / (KEYS - 1), ALU.add, ALU.mult)
                        v.wait_ge(mean_done, b + 1)
                        v.tensor_scalar(stats[:, :, 0], ps_m[:, 0:PAIRS], scale / KEYS, None, ALU.mult).then_inc(stats_ready, 1)
                        v.wait_ge(feat_done, b + 1)
                        v.tensor_copy(featT[:, :], ps_m[0:3, 16:32]).then_inc(feat_ready, 1)
                        v.wait_ge(t_done, b + 1)
                        ch.link(v.tensor_scalar(logt[:, :], ps_m[0:1, 64:80], b3[:, 0:1], LOG_T_MAX, ALU.add, ALU.min))
                        v.tensor_scalar(logt[:, :], logt[:, :], LOG_T_MIN, None, ALU.max).then_inc(t_clip, 1)
                        v.wait_ge(spread, b + 1)
                        ch.link(v.tensor_scalar(temp[:, :], ps_m[:, 80:88], 0.5, None, ALU.mult))
                        ch.link(v.tensor_tensor(nmx[:, :], mx[:, :], temp[:, :], ALU.mult))
                        v.tensor_scalar(nmx[:, :], nmx[:, :], -1.0, None, ALU.mult).then_inc(temp_ready, 1)
                        for p in range(PAIRS):
                            turn_evac(p)
                            if p >= 1:
                                norm(p - 1)
                        norm(PAIRS - 1)
                    v.wait_ge(normed, b * PAIRS + 2 * PAIRS)
                    v.tensor_tensor(onorm[:, :], onorm[:, :], const[:, C_DIAG:C_DIAG + D], ALU.mult).then_inc(o_ready, 1)
                    filled(v, b, PER - 1)
                    v.sem_inc(dve_mark, 1)
                    v.tensor_copy(qT[:, :, bass.ds(b * S, S)],
                                  ring[(PER - 1) % 2][:, 0:DC * S].rearrange("p (c n) -> p c n", c=DC)).then_inc(dve_evac, 1)
                ch.end(B)
                if adapt:
                    v.wait_ge(small_in, 16 * 7)
                    v.wait_ge(dve_evac, (B + 1) * count["dve"])
                    for c in range(DC):
                        v.tensor_scalar(qT[:, c, :], qT[:, c, :], bv[:, c:c + 1], None, ALU.add)


def output_stage(nc, tag, x, aT, wo_dram, bo_dram=None):
    with Scope(nc, tag) as sc:
        wo = sc.sb("wo", [P, DC, D])
        bo = sc.sb("bo", [P, D])
        banks = [sc.ps(f"b{i}", [P, 512]) for i in range(TT)]
        w_in, done, added, step = (sc.sem(n) for n in ("w_in", "done", "added", "step"))
        with nc.Block() as block:
            @block.sync
            def _(sp):
                sp.dma_start(wo[:, :, :], wo_dram.rearrange("(k p) n -> p k n", p=P)).then_inc(w_in, 16)
                if bo_dram is not None:
                    sp.dma_start(bo[:, :], bo_dram.to_broadcast([P, D])).then_inc(w_in, 16)

            @block.tensor
            def _(pe):
                pe.wait_ge(w_in, 16 if bo_dram is None else 32)
                for t in range(TT):
                    product(pe, banks[t][:, :], lambda k: aT[:, k, t * P:(t + 1) * P], lambda k: wo[:, k, :], DC).then_inc(done, 1)

            @block.vector
            def _(v):
                ch = Chain(v, step)
                if bo_dram is not None:
                    v.wait_ge(w_in, 32)
                    for t in range(TT):
                        ch.inc(v.tensor_tensor(x[:, t, :], x[:, t, :], bo[:, :], ALU.add))
                    ch.wait()
                for t in range(TT):
                    v.wait_ge(done, t + 1)
                    v.tensor_tensor(x[:, t, :], x[:, t, :], banks[t][:, :], ALU.add)


def store(nc, out_dram, x):
    with Scope(nc, "st") as sc:
        done = sc.sem("done")
        with nc.Block() as block:
            @block.sync
            def _(sp):
                sp.dma_start(out_dram.rearrange("(i e) t d -> (e t) i d", e=BT), x[:, :, :]).then_inc(done, 16)
                sp.wait_ge(done, 16)


def mixer_stage(nc, const, x, a):
    with Scope(nc, "mx") as sc:
        sb, sem = sc.sb, sc.sem
        u, xn = sb("u", [P, TT, D]), sb("xn", [P, TT, D])
        xnT = sb("xnT", [P, DC, T])
        xp, z = sb("xp", [P, DC, T]), sb("z", [P, DC, T])
        w_in, w_out = sb("w_in", [P, DC, 2 * D]), sb("w_out", [P, DC, D])
        gain, shift, b_out = sb("gain", [P, D]), sb("shift", [P, D]), sb("b_out", [P, D])
        wc = sb("wc", [P, D])
        W_PAD = (B - 1) * NS
        wb = sb("wb", [P, DC, 2 * W_PAD + NS])
        b_in, d_skip, dt = sb("b_in", [P, 2 * DC]), sb("d_skip", [P, DC]), sb("dt", [P, DC])
        la = sb("la", [P, DC, NS])
        ea = sb("ea", [P, DC, NS])
        ex = sb("ex", [P, DC, NS * S])
        amean = sb("amean", [P, S])
        sel = sb("sel", [P, NS, S])
        dtm = sb("dtm", [P, 1])
        bp = sb("bp", [P, 2 * S - 1])
        conv = sb("conv", [P, S, S])
        xm = sb("xm", [P, S])
        xmx = sb("xmx", [P, B, S])
        y = sb("y", [P, DC, T])
        bank = [sc.ps(f"b{i}", [P, 512]) for i in range(8)]
        outer = Norm(sc, "no", x, u, None, None)
        inner = Norm(sc, "ni", u, xn, xnT, const[:, C_IDENT:C_IDENT + P])
        (big_in, small_in, dt_exp, al_ready, ea_ready, tl_ready, ex_ready, dt_ready, a_sum, xz_done, xp_ready,
         z_ready, wb_ready, b_done, xm_ready, y_sum, y_ready, out_done, step) = (sem(n) for n in (
            "big_in", "small_in", "dt_exp", "al_ready", "ea_ready", "tl_ready", "ex_ready", "dt_ready", "a_sum",
            "xz_done", "xp_ready", "z_ready", "wb_ready", "b_done", "xm_ready", "y_sum", "y_ready", "out_done", "step"))
        wb_in = sem("wb_in")
        SMALL = 5 + B
        with nc.Block() as block:
            @block.sync
            def _(sp):
                sp.dma_start(la[:, :, :], a["A_log"].rearrange("(k p) s -> p k s", p=P)).then_inc(small_in, 16)
                for dst, src in ((dt, "log_dt"), (d_skip, "D_skip"), (b_in, "b_in")):
                    sp.dma_start(dst[:, :], a[src]).then_inc(small_in, 16)
                for b in range(B):
                    sp.dma_start(wc[b * NS:(b + 1) * NS, :], a["W_CT"]).then_inc(small_in, 16)
                sp.dma_start(b_out[:, :], a["b_out"].to_broadcast([P, D])).then_inc(small_in, 16)
                for dst, src in ((gain, "ln_g"), (shift, "ln_b")):
                    sp.dma_start(dst[:, :], a[src].to_broadcast([P, D])).then_inc(big_in, 16)
                sp.dma_start(w_in[:, :, :], a["W_inT"].rearrange("(k p) n -> p k n", p=P)).then_inc(big_in, 16)
                sp.dma_start(w_out[:, :, :], a["W_outT"].rearrange("(k p) n -> p k n", p=P)).then_inc(big_in, 16)
                sp.wait_ge(wb_ready, 1)
                sp.dma_start(wb[:, :, W_PAD:W_PAD + NS], a["W_BT"].rearrange("(k p) s -> p k s", p=P)).then_inc(wb_in, 16)

            @block.gpsimd
            def _(g):
                g.memset(bp[:, 0:S - 1], 0.0)
                g.memset(wb[:, :, :], 0.0).then_inc(wb_ready, 1)

            @block.scalar
            def _(s):
                outer.act_root(s)
                inner.act_root(s)
                s.wait_ge(small_in, 16 * SMALL)
                s.activation(dt[:, :], dt[:, :], ACT.Exp).then_inc(dt_exp, 1)
                s.wait_ge(al_ready, 1)
                s.activation(ea[:, :, :], la[:, :, :], ACT.Exp).then_inc(ea_ready, 1)
                for k in range(DC):
                    s.wait_ge(tl_ready, k + 1)
                    s.activation(ex[:, k, :], ex[:, k, :], ACT.Exp).then_inc(ex_ready, 1)
                for g in range(DC):
                    s.wait_ge(xz_done, g + 1)
                    s.activation(xp[:, g, :], bank[g][:, :], ACT.Identity, bias=b_in[:, g:g + 1]).then_inc(xp_ready, 1)
                for g in range(DC, 2 * DC):
                    s.wait_ge(xz_done, g + 1)
                    s.activation(z[:, g - DC, :], bank[g - DC][:, :], ACT.Silu, bias=b_in[:, g:g + 1]).then_inc(z_ready, 1)

            @block.tensor
            def _(pe):
                inner.pe_turn(pe, bank)
                pe.wait_ge(ex_ready, DC)
                for half in range(2):
                    product(pe, bank[4 + half][:, :], lambda k: const[:, C_ONES:C_ONES + P],
                            lambda k: ex[:, k, half * 512:(half + 1) * 512], DC)
                pe.wait_ge(dt_ready, 1)
                pe.matmul(bank[6][:, 0:DC], const[:, C_ONES:C_ONES + P], dt[:, :], start=True, stop=True).then_inc(a_sum, 1)
                pe.wait_ge(inner.uT_ready, TT)
                pe.wait_ge(big_in, 16 * 4)
                for g in range(2 * DC):
                    if g >= DC:
                        pe.wait_ge(xp_ready, g - DC + 1)
                    product(pe, bank[g % 4][:, :], lambda k: w_in[:, k, g * P:(g + 1) * P], lambda k: xnT[:, k, :], DC).then_inc(xz_done, 1)
                pe.wait_ge(wb_in, 16)
                pe.wait_ge(xp_ready, DC)
                for b in range(B):
                    for k in range(DC):
                        at = W_PAD - b * NS
                        ins = pe.matmul(bank[7][:, 0:S], wb[:, k, at:at + P], xp[:, k, b * S:(b + 1) * S],
                                        start=(b == 0 and k == 0), stop=(b == B - 1 and k == DC - 1))
                ins.then_inc(b_done, 1)
                pe.wait_ge(xm_ready, 1)
                pe.wait_ge(z_ready, DC)
                for k in range(DC):
                    pe.matmul(bank[k][:, :], wc[:, k * P:(k + 1) * P], xmx[:, :, :].rearrange("p b t -> p (b t)"),
                              start=True, stop=True).then_inc(y_sum, 1)
                pe.wait_ge(y_ready, DC)
                for t in range(TT):
                    product(pe, bank[4 + t][:, :], lambda k: y[:, k, t * P:(t + 1) * P], lambda k: w_out[:, k, :], DC).then_inc(out_done, 1)

            @block.vector
            def _(v):
                ch = Chain(v, step)
                v.wait_ge(small_in, 16 * SMALL)
                v.tensor_scalar(la[:, :, :], la[:, :, :], 80.0, None, ALU.min).then_inc(al_ready, 1)
                outer.dve_var(ch)
                outer.dve_u(ch)
                v.wait_ge(outer.u_ready, TT)
                inner.dve_var(ch)
                v.wait_ge(dt_exp, 1)
                v.tensor_scalar(dt[:, :], dt[:, :], DT_MIN, DT_MAX, ALU.max, ALU.min).then_inc(dt_ready, 1)
                v.wait_ge(ea_ready, 1)
                v.wait_ge(dt_ready, 1)
                ch.link(v.tensor_tensor(la[:, :, :], ea[:, :, :], dt[:, :].unsqueeze(2).to_broadcast([P, DC, NS]), ALU.mult))
                ch.link(v.tensor_scalar(la[:, :, :], la[:, :, :], -1.0, LOG_A_MIN, ALU.mult, ALU.max))
                ch.link(v.tensor_scalar(la[:, :, :], la[:, :, :], LOG_A_MAX, None, ALU.min))
                for k in range(DC):
                    v.tensor_tensor(ex[:, k, :].rearrange("p (s t) -> p s t", s=NS),
                                    la[:, k, :].unsqueeze(2).to_broadcast([P, NS, S]),
                                    const[:, C_TIME:C_TIME + S].unsqueeze(1).to_broadcast([P, NS, S]), ALU.mult).then_inc(tl_ready, 1)
                v.wait_ge(big_in, 16 * 4)
                inner.dve_u(ch, gain[:, :], shift[:, :])
                inner.evac(v, bank, v.tensor_copy)
                v.wait_ge(a_sum, 1)
                for half in range(2):
                    n = NS // 2
                    ch.inc(v.tensor_tensor(sel[:, half * n:(half + 1) * n, :], bank[4 + half][:, :].rearrange("p (s t) -> p s t", s=n),
                                           const[:, C_STATE + half * n:C_STATE + (half + 1) * n].unsqueeze(2).to_broadcast([P, n, S]), ALU.mult))
                ch.link(v.tensor_reduce(dtm[:, :], bank[6][:, 0:DC], AX.X, ALU.add))
                ch.link(v.tensor_reduce(amean[:, :], sel[:, :, :].rearrange("p s t -> p t s"), AX.X, ALU.add))
                ch.link(v.tensor_scalar(dtm[:, :], dtm[:, :], 1.0 / D, None, ALU.mult))
                v.wait_ge(b_done, 1)
                v.wait_ge(wb_ready, 1)
                ch.link(v.tensor_scalar(bp[:, S - 1:2 * S - 1], bank[7][:, 0:S], dtm[:, 0:1], 1.0 / D, ALU.mult, ALU.mult))
                windows = bass.AP(tensor=bp[:, :].tensor, offset=0, ap=[[2 * S - 1, P], [1, S], [1, S]])
                ch.link(v.tensor_tensor(conv[:, :, :], windows, amean[:, :].unsqueeze(1).to_broadcast([P, S, S]), ALU.mult))
                ch.link(v.tensor_reduce(xm[:, :], conv[:, :, :], AX.X, ALU.add))
                v.tensor_tensor(xmx[:, :, :], xm[:, :].unsqueeze(1).to_broadcast([P, B, S]),
                                const[:, C_BAT:C_BAT + B].unsqueeze(2).to_broadcast([P, B, S]), ALU.mult).then_inc(xm_ready, 1)
                v.wait_ge(z_ready, DC)
                for k in range(DC):
                    v.wait_ge(y_sum, k + 1)
                    ch.link(v.scalar_tensor_tensor(y[:, k, :], xp[:, k, :], d_skip[:, k:k + 1], bank[k][:, :], ALU.mult, ALU.add))
                    v.tensor_tensor(y[:, k, :], y[:, k, :], z[:, k, :], ALU.mult).then_inc(y_ready, 1)
                for t in range(TT):
                    ch.inc(v.tensor_tensor(x[:, t, :], x[:, t, :], u[:, t, :], ALU.add))
                ch.wait()
                for t in range(TT):
                    ch.inc(v.tensor_tensor(x[:, t, :], x[:, t, :], b_out[:, :], ALU.add))
                ch.wait()
                for t in range(TT):
                    v.wait_ge(out_done, t + 1)
                    v.tensor_tensor(x[:, t, :], x[:, t, :], bank[4 + t][:, :], ALU.add)


def retrieval_stage(nc, const, x, a):
    with Scope(nc, "rt") as outer:
        u = outer.sb("u", [P, TT, D])
        idx = outer.sb("idx", [P, TT, PH * PTOP], I32)
        weight = outer.sb("weight", [P, TT, PH * PTOP])
        choose_experts(nc, const, x, u, idx, weight, a)
        apply_experts(nc, x, u, idx, weight, a["embed"])


def choose_experts(nc, const, x, u, idx, weight, a):
    G = 2 * PH
    with Scope(nc, "ch") as sc:
        sb, sem = sc.sb, sc.sem
        uT = sb("uT", [P, DC, T])
        wq = sb("wq", [P, DC, G * PK])
        keys = sb("keys", [P, G * NKEY])
        q = sb("q", [P, G, T])
        gamma, beta = sb("gamma", [P, G]), sb("beta", [P, G])
        stat, mv = sb("stat", [P, G, 6]), sb("mv", [P, G, 2])
        ve, sd, gs, sh = (sb(n, [P, G]) for n in ("ve", "sd", "gs", "sh"))
        s8 = sb("s8", [P, G, PTOP])
        i8 = sb("i8", [P, G, PTOP], U32)
        i8f = sb("i8f", [P, G, PTOP])
        sums = sb("sums", [P, PH, PTOP, PTOP])
        t8 = sb("t8", [P, PH, PTOP])
        pk = sb("pk", [P, PH, PTOP], U32)
        pki = sb("pki", [P, 2, PH, PTOP], U32)
        pkf = sb("pkf", [P, 2, PH, PTOP])
        eq = sb("eq", [P, PH, PTOP, PTOP])
        ixy = sb("ixy", [P, 2, PH, PTOP])
        e8 = sb("e8", [P, PH, PTOP])
        tot = sb("tot", [P, PH])
        bank = [sc.ps(f"b{i}", [P, 512]) for i in range(8)]
        norm = Norm(sc, "n", x, u, uT, const[:, C_IDENT:C_IDENT + P])
        (w_in, small_in, q_done, q_out, q_root, q_var, q_normed, sim_done, sim_used, shifted, e_ready, step) = (
            sem(n) for n in ("w_in", "small_in", "q_done", "q_out", "q_root", "q_var", "q_normed", "sim_done",
                             "sim_used", "shifted", "e_ready", "step"))
        with nc.Block() as block:
            @block.sync
            def _(sp):
                sp.dma_start(wq[:, :, :], a["w_q"].rearrange("(k p) n -> p k n", p=P)).then_inc(w_in, 16)
                sp.dma_start(keys[:, :], a["pkeys"]).then_inc(small_in, 16)
                sp.dma_start(gamma[:, :], a["bn_gamma"]).then_inc(small_in, 16)
                sp.dma_start(beta[:, :], a["bn_beta"]).then_inc(small_in, 16)

            @block.tensor
            def _(pe):
                norm.pe_turn(pe, bank)
                pe.wait_ge(norm.uT_ready, TT)
                pe.wait_ge(w_in, 16)
                for g in range(G):
                    if g >= 8:
                        pe.wait_ge(q_out, g - 7)
                    product(pe, bank[g % 8][:, :], lambda k: wq[:, k, g * PK:(g + 1) * PK], lambda k: uT[:, k, :], DC).then_inc(q_done, 1)
                pe.wait_ge(small_in, 48)
                pe.wait_ge(q_normed, G)
                for t in range(TT):
                    if t >= 2:
                        pe.wait_ge(sim_used, t - 1)
                    for g in range(G):
                        ins = pe.matmul(bank[t % 2 * 4 + g // 4][:, g % 4 * NKEY:(g % 4 + 1) * NKEY],
                                        q[:, g, t * P:(t + 1) * P], keys[:, g * NKEY:(g + 1) * NKEY], start=True, stop=True)
                    ins.then_inc(sim_done, 1)

            @block.scalar
            def _(s):
                norm.act_root(s)
                for g in range(G):
                    s.wait_ge(q_done, g + 1)
                    s.activation(q[:, g, :], bank[g % 8][:, :], ACT.Copy).then_inc(q_out, 1)
                s.wait_ge(q_var, 1)
                s.activation(sd[:, :], ve[:, :], ACT.Sqrt).then_inc(q_root, 1)
                for t in range(TT):
                    s.wait_ge(shifted, t + 1)
                    s.activation(e8[:, :, :], e8[:, :, :], ACT.Exp).then_inc(e_ready, 1)

            @block.vector
            def _(v):
                ch = Chain(v, step)
                norm.dve_var(ch)
                norm.dve_u(ch)
                norm.evac(v, bank, v.tensor_copy)
                for g in range(G):
                    v.wait_ge(q_out, g + 1)
                    ch.inc(v.bn_stats(stat[:, g, :], q[:, g, :]))
                ch.wait()
                for g in range(G):
                    ch.inc(v.bn_aggr(mv[:, g, :], stat[:, g, :]))
                ch.wait()
                v.tensor_scalar(ve[:, :], mv[:, :, 1], LN_EPS, None, ALU.add).then_inc(q_var, 1)
                v.wait_ge(q_root, 1)
                v.wait_ge(small_in, 48)
                ch.link(v.reciprocal(gs[:, :], sd[:, :]))
                ch.link(v.tensor_tensor(gs[:, :], gs[:, :], gamma[:, :], ALU.mult))
                ch.link(v.tensor_tensor(sh[:, :], mv[:, :, 0], gs[:, :], ALU.mult))
                ch.link(v.tensor_tensor(sh[:, :], beta[:, :], sh[:, :], ALU.subtract))
                for g in range(G):
                    v.tensor_scalar(q[:, g, :], q[:, g, :], gs[:, g:g + 1], sh[:, g:g + 1], ALU.mult, ALU.add).then_inc(q_normed, 1)
                iota = const[:, C_IOTA:C_IOTA + 8]
                shape = [P, PH, PTOP, PTOP]
                for t in range(TT):
                    v.wait_ge(sim_done, t + 1)
                    sims = [bank[t % 2 * 4 + g // 4][:, g % 4 * NKEY:(g % 4 + 1) * NKEY] for g in range(G)]
                    for g in range(G):
                        ch.inc(v.max(out=s8[:, g, :], in_=sims[g]))
                    ch.wait()
                    for g in range(G):
                        ins = v.max_index(out=i8[:, g, :], in_max=s8[:, g, :], in_values=sims[g])
                    ins.then_inc(sim_used, 1)
                    ch.link(v.tensor_tensor(sums[:, :, :, :], s8[:, 0:PH, :].unsqueeze(3).to_broadcast(shape),
                                            s8[:, PH:G, :].unsqueeze(2).to_broadcast(shape), ALU.add))
                    flat = sums[:, :, :, :].rearrange("p h i j -> p h (i j)")
                    for h in range(PH):
                        ch.inc(v.max(out=t8[:, h, :], in_=flat[:, h, :]))
                    ch.wait()
                    for h in range(PH):
                        ch.inc(v.max_index(out=pk[:, h, :], in_max=t8[:, h, :], in_values=flat[:, h, :]))
                    v.tensor_tensor(e8[:, :, :], t8[:, :, :], t8[:, :, 0:1].to_broadcast([P, PH, PTOP]), ALU.subtract).then_inc(shifted, 1)
                    v.wait_ge(sim_used, t + 1)
                    ch.inc(v.tensor_copy(i8f[:, :, :], i8[:, :, :]))
                    ch.wait()
                    ch.inc(v.tensor_single_scalar(pki[:, 0, :, :], pk[:, :, :], 3, ALU.logical_shift_right))
                    ch.link(v.tensor_single_scalar(pki[:, 1, :, :], pk[:, :, :], 7, ALU.bitwise_and))
                    ch.link(v.tensor_copy(pkf[:, :, :, :], pki[:, :, :, :]))
                    for side in range(2):
                        ch.link(v.tensor_tensor(eq[:, :, :, :], pkf[:, side, :, :].unsqueeze(3).to_broadcast(shape),
                                                iota.unsqueeze(1).unsqueeze(1).to_broadcast(shape), ALU.is_equal))
                        ch.link(v.tensor_tensor(eq[:, :, :, :], eq[:, :, :, :],
                                                i8f[:, side * PH:(side + 1) * PH, :].unsqueeze(2).to_broadcast(shape), ALU.mult))
                        ch.link(v.tensor_reduce(ixy[:, side, :, :], eq[:, :, :, :], AX.X, ALU.add))
                    ch.inc(v.scalar_tensor_tensor(idx[:, t, :], ixy[:, 0, :, :].rearrange("p h k -> p (h k)"), float(NKEY),
                                                  ixy[:, 1, :, :].rearrange("p h k -> p (h k)"), ALU.mult, ALU.add))
                    v.wait_ge(e_ready, t + 1)
                    ch.link(v.tensor_reduce(tot[:, :], e8[:, :, :], AX.X, ALU.add))
                    ch.link(v.reciprocal(tot[:, :], tot[:, :]))
                    ch.link(v.tensor_tensor(weight[:, t, :].rearrange("p (h k) -> p h k", h=PH), e8[:, :, :],
                                            tot[:, :].unsqueeze(2).to_broadcast([P, PH, PTOP]), ALU.mult))


def apply_experts(nc, x, u, idx, weight, embed):
    N = PTOP
    RING = 4
    with Scope(nc, "ap") as sc:
        sb, sem = sc.sb, sc.sem
        rows = sb("rows", [P, RING, N, 2 * D])
        idx_c = sb("idx_c", [P, 2, PH * PTOP], I32)
        uc, acc, wc = sb("uc", [P, D]), sb("acc", [P, D]), sb("wc", [P, PH * PTOP])
        dot, act, coef = (sb(n, [P, 2, N]) for n in ("dot", "act", "coef"))
        landed = [sem(f"landed{r}") for r in range(RING)]
        used, idx_ready, dots, gelus, step, mark, pool_mark = (
            sem(n) for n in ("used", "idx_ready", "dots", "gelus", "step", "mark", "pool_mark"))
        with nc.Block() as block:
            @block.gpsimd
            def _(g):
                with g.Fori(0, TT // 2) as i:
                    for e in range(2):
                        g.tensor_copy(idx_c[:, e, :], idx[:, bass.ds(2 * i + e, 1), :].rearrange("p o n -> p (o n)")).then_inc(idx_ready, 1)
                        g.wait_ge(idx_ready, 2 * i + (e + 1))
                        for h in range(PH):
                            g.wait_ge(used, i * (2 * PH) + (e * PH + h + 1))
                            g.sem_inc(pool_mark, 1)
                            for k in range(N):
                                g.indirect_dma_start(rows[:, h % RING, k, :], None, embed,
                                                     bass.IndirectOffsetOnAxis(ap=idx_c[:, e, h * N + k:h * N + k + 1], axis=0)
                                                     ).then_inc(landed[h % RING], 16)

            @block.scalar
            def _(s):
                with s.Fori(0, TT // 2) as i:
                    for n in range(2 * PH):
                        s.wait_ge(dots, i * (2 * PH) + (n + 1))
                        s.activation(act[:, n % 2, :], dot[:, n % 2, :], ACT.Gelu_apprx_tanh).then_inc(gelus, 1)

            @block.vector
            def _(v):
                ch = Chain(v, step)
                v.sem_inc(used, RING)
                with v.Fori(0, TT // 2) as i:
                    ch.loop(i, 2 * (2 + PH * (1 + N)))

                    def add_up(e, h):
                        n = e * PH + h
                        v.wait_ge(gelus, i * (2 * PH) + (n + 1))
                        ch.link(v.tensor_tensor(coef[:, n % 2, :], act[:, n % 2, :], wc[:, h * N:(h + 1) * N], ALU.mult))
                        for k in range(N):
                            ch.link(v.scalar_tensor_tensor(acc[:, :], rows[:, h % RING, k, D:2 * D], coef[:, n % 2, k:k + 1],
                                                           acc[:, :], ALU.mult, ALU.add))
                        v.sem_inc(used, 1)

                    for e in range(2):
                        tile = bass.ds(2 * i + e, 1)
                        v.tensor_copy(uc[:, :], u[:, tile, :].rearrange("p o n -> p (o n)"))
                        v.tensor_copy(wc[:, :], weight[:, tile, :].rearrange("p o n -> p (o n)"))
                        ch.link(v.tensor_copy(acc[:, :], x[:, tile, :].rearrange("p o n -> p (o n)")))
                        for h in range(PH + 1):
                            if h < PH:
                                n = e * PH + h
                                v.wait_ge(landed[h % RING], i * (16 * N * 2 * PH // RING) + 16 * N * (n // RING + 1))
                                for k in range(N):
                                    down = rows[:, h % RING, k, 0:D]
                                    ins = v.tensor_tensor_reduce(down, uc[:, :], down, 1.0, 0.0,
                                                                 ALU.mult, ALU.add, dot[:, n % 2, k:k + 1])
                                ins.then_inc(dots, 1)
                            if h >= 1:
                                add_up(e, h - 1)
                        ch.link(v.tensor_copy(x[:, tile, :].rearrange("p o n -> p (o n)"), acc[:, :]))
                ch.end(TT // 2)


def self_attention(nc, const, x, a):
    scale = float(D) ** -0.5
    with Scope(nc, "sa") as sc:
        sb, sem = sc.sb, sc.sem
        u, uT = sb("u", [P, TT, D]), sb("uT", [P, DC, T])
        wq, wk, wv, wo = (sb(n, [P, DC, D]) for n in ("wq", "wk", "wv", "wo"))
        qT, kT = sb("qT", [P, DC, T]), sb("kT", [P, DC, T])
        vt = sb("vt", [P, TT, D])
        s_sb = sb("s", [P, 2, H, P])
        mx, tot = sb("mx", [P, 2, H]), sb("tot", [P, 2, H])
        wT = sb("wT", [P, H, P])
        o = sb("o", [P, 2, D])
        oT = sb("oT", [P, DC, P])
        pa = sc.ps("pa", [P, 4, 512])
        pb = sc.ps("pb", [P, 4, 512])
        banks = [pa[:, i, :] for i in range(4)] + [pb[:, i, :] for i in range(4)]
        norm = Norm(sc, "n", x, u, uT, const[:, C_IDENT:C_IDENT + P])
        (w_in, wo_in, q_done, q_out, v_out, scored, taken, shifted, probs, turned, wT_ready, pv, o_ready, o_turned,
         oT_ready, done, added, step) = (sem(n) for n in (
            "w_in", "wo_in", "q_done", "q_out", "v_out", "scored", "taken", "shifted", "probs", "turned",
            "wT_ready", "pv", "o_ready", "o_turned", "oT_ready", "done", "added", "step"))
        with nc.Block() as block:
            @block.sync
            def _(sp):
                for w, n in ((wq, "sa_q"), (wk, "sa_k"), (wv, "sa_v")):
                    sp.dma_start(w[:, :, :], a[n].rearrange("(k p) n -> p k n", p=P)).then_inc(w_in, 16)
                sp.dma_start(wo[:, :, :], a["sa_o"].rearrange("(k p) n -> p k n", p=P)).then_inc(wo_in, 16)

            @block.tensor
            def _(pe):
                norm.pe_turn(pe, banks)
                pe.wait_ge(norm.uT_ready, TT)
                pe.wait_ge(w_in, 48)
                for c in range(DC):
                    product(pe, banks[c], lambda k: wq[:, k, c * P:(c + 1) * P], lambda k: uT[:, k, :], DC).then_inc(q_done, 1)
                for c in range(DC):
                    product(pe, banks[4 + c], lambda k: wk[:, k, c * P:(c + 1) * P], lambda k: uT[:, k, :], DC).then_inc(q_done, 1)
                for t in range(TT):
                    pe.wait_ge(q_out, t + 1)
                    product(pe, banks[t], lambda k: uT[:, k, t * P:(t + 1) * P], lambda k: wv[:, k, :], DC).then_inc(q_done, 1)
                pe.wait_ge(wo_in, 16)
                pe.wait_ge(q_out, 2 * DC)
                pe.wait_ge(v_out, TT)

                def scores(t):
                    for h in range(H):
                        c, i = h // HC, h % HC
                        ins = pe.matmul(pa[:, i, c * P:(c + 1) * P], qT[i * DH:(i + 1) * DH, c, t * P:(t + 1) * P],
                                        kT[i * DH:(i + 1) * DH, c, t * P:(t + 1) * P], start=True, stop=True)
                    ins.then_inc(scored, 1)

                scores(0)
                for t in range(TT):
                    pe.wait_ge(taken, HC * (t + 1))
                    if t + 1 < TT:
                        scores(t + 1)
                    pe.wait_ge(probs, t + 1)
                    if t >= 1:
                        pe.wait_ge(added, t)
                    for h in range(H):
                        ins = pe.transpose(pb[:, h // 4, (h % 4) * P:(h % 4 + 1) * P], s_sb[:, t % 2, h, :], const[:, C_IDENT:C_IDENT + P])
                        if h % 4 == 3:
                            ins.then_inc(turned, 1)
                    for h in range(H):
                        if h % 4 == 0:
                            pe.wait_ge(wT_ready, 4 * t + h // 4 + 1)
                        ins = pe.matmul(pb[:, h // 4, (h % 4) * P:(h % 4 + 1) * P], wT[:, h, :],
                                        vt[:, t, (h // HC) * P:(h // HC + 1) * P], start=True, stop=True)
                    ins.then_inc(pv, 1)
                    pe.wait_ge(o_ready, DC * (t + 1))
                    for c in range(DC):
                        ins = pe.transpose(pb[:, 0, c * P:(c + 1) * P], o[:, t % 2, c * P:(c + 1) * P], const[:, C_IDENT:C_IDENT + P])
                    ins.then_inc(o_turned, 1)
                    pe.wait_ge(oT_ready, t + 1)
                    product(pe, pb[:, 1, :], lambda k: oT[:, k, :], lambda k: wo[:, k, :], DC).then_inc(done, 1)

            @block.scalar
            def _(s):
                norm.act_root(s)
                for c in range(DC):
                    s.wait_ge(q_done, c + 1)
                    s.activation(qT[:, c, :], banks[c], ACT.Copy).then_inc(q_out, 1)
                for c in range(DC):
                    s.wait_ge(q_done, DC + c + 1)
                    s.activation(kT[:, c, :], banks[4 + c], ACT.Copy).then_inc(q_out, 1)
                for t in range(TT):
                    s.wait_ge(shifted, t + 1)
                    s.activation(s_sb[:, t % 2, :, :], s_sb[:, t % 2, :, :], ACT.Exp).then_inc(probs, 1)
                    for g in range(4):
                        s.wait_ge(turned, 4 * t + g + 1)
                        if g == 0 and t >= 1:
                            s.wait_ge(pv, t)
                        s.activation(wT[:, 4 * g:4 * g + 4, :].rearrange("p h n -> p (h n)"), pb[:, g, :], ACT.Copy).then_inc(wT_ready, 1)

            @block.vector
            def _(v):
                ch = Chain(v, step)
                norm.dve_var(ch)
                norm.dve_u(ch)
                norm.evac(v, banks, v.tensor_copy)
                for t in range(TT):
                    v.wait_ge(q_done, 2 * DC + t + 1)
                    v.tensor_copy(vt[:, t, :], banks[t]).then_inc(v_out, 1)

                def soften(t):
                    v.wait_ge(scored, t + 1)
                    if t >= 2:
                        v.wait_ge(turned, 4 * (t - 1))
                    s = s_sb[:, t % 2, :, :]
                    for i in range(HC):
                        v.scalar_tensor_tensor(s.rearrange("p (c i) n -> p i c n", i=HC)[:, i, :, :],
                                               pa[:, i, :].rearrange("p (c n) -> p c n", n=P), scale,
                                               const[:, C_CAUSAL:C_CAUSAL + P].unsqueeze(1).to_broadcast([P, DC, P]),
                                               ALU.mult, ALU.add).then_inc(taken, 1)
                    v.wait_ge(taken, HC * (t + 1))
                    ch.link(v.tensor_reduce(mx[:, t % 2, :], s, AX.X, ALU.max))
                    v.tensor_tensor(s, s, mx[:, t % 2, :].unsqueeze(2).to_broadcast([P, H, P]), ALU.subtract).then_inc(shifted, 1)

                soften(0)
                for t in range(TT):
                    v.wait_ge(probs, t + 1)
                    ch.link(v.tensor_reduce(tot[:, t % 2, :], s_sb[:, t % 2, :, :], AX.X, ALU.add))
                    ch.link(v.reciprocal(tot[:, t % 2, :], tot[:, t % 2, :]))
                    if t + 1 < TT:
                        soften(t + 1)
                    v.wait_ge(pv, t + 1)
                    for c in range(DC):
                        own = bass.AP(tensor=pb[:, :, :].tensor, offset=512 * c, ap=[[4 * 512, P], [P + DH, HC], [1, DH]])
                        v.tensor_tensor(o[:, t % 2, c * P:(c + 1) * P].rearrange("p (i n) -> p i n", i=HC), own,
                                        tot[:, t % 2, c * HC:(c + 1) * HC].unsqueeze(2).to_broadcast([P, HC, DH]),
                                        ALU.mult).then_inc(o_ready, 1)
                    v.wait_ge(o_turned, t + 1)
                    v.tensor_copy(oT[:, :, :].rearrange("p c n -> p (c n)"), pb[:, 0, :]).then_inc(oT_ready, 1)
                    v.wait_ge(done, t + 1)
                    v.tensor_tensor(x[:, t, :], x[:, t, :], pb[:, 1, :], ALU.add).then_inc(added, 1)


def expert_stage(nc, const, x, a):
    E = 1 + NEXP
    RING, HRING, AHEAD = 4, 4, 2
    with Scope(nc, "ex") as sc:
        sb, sem = sc.sb, sc.sem
        u, uT = sb("u", [P, TT, D]), sb("uT", [P, DC, T])
        u_hi, u_lo = sb("u_hi", [P, DC, T], F32R), sb("u_lo", [P, DC, T], F32R)
        w = [split_buffer(sc, f"w{r}", [P, 2 * D]) for r in range(RING)]
        b1, b2 = sb("b1", [P, E * FC]), sb("b2", [E, D])
        rw, rb = sb("rw", [P, DC, NEXP]), sb("rb", [P, NEXP])
        lg, m8, i8f = sb("lg", [P, TT, NEXP]), sb("m8", [P, TT, 8]), sb("i8f", [P, TT, 8])
        i8 = sb("i8", [P, TT, 8], U32)
        e2, tot = sb("e2", [P, TT, 2]), sb("tot", [P, TT])
        pick = sb("pick", [P, TT, 2, NEXP])
        share = sb("share", [P, TT, E])
        shareT = sb("shareT", [E, T])
        shares = sb("shares", [P, E, T])
        g_sb, gs = sb("g", [P, 2, T]), sb("gs", [P, 2, T])
        h_hi, h_lo = ([sb(f"h_{n}{r}", [P, T], F32R) for r in range(2)] for n in ("hi", "lo"))
        py = [sc.ps(f"py{t}", [P, 512]) for t in range(TT)]
        ph = [sc.ps(f"ph{r}", [P, 512]) for r in range(HRING)]
        norm = Norm(sc, "n", x, u, uT, const[:, C_IDENT:C_IDENT + P])
        landed = [sem(f"landed{r}") for r in range(RING)]
        (small_in, u_hi_ready, u_lo_ready, routed, shifted, e_ready, share_ready, share_turned, shareT_ready, spread,
         spread_out, w_hi_ready, w_lo_ready, inner, gelus, scaled, h_hi_ready, h_lo_ready, used, step) = (sem(n) for n in (
            "small_in", "u_hi_ready", "u_lo_ready", "routed", "shifted", "e_ready", "share_ready", "share_turned",
            "shareT_ready", "spread", "spread_out", "w_hi_ready", "w_lo_ready", "inner", "gelus", "scaled",
            "h_hi_ready", "h_lo_ready", "used", "step"))


        def networks(eng, body):
            body(0)
            with eng.Fori(1, E - 1) as e:
                body(e)
            body(E - 1)

        def until(eng, s, e, f, back):
            if isinstance(e, int) and e * FC + f - back < 0:
                return
            if isinstance(e, int):
                eng.wait_ge(s, e * FC + f - back + 1)
            else:
                eng.wait_ge(s, e * FC + (f - back + 1))

        with nc.Block() as block:
            @block.sync
            def _(sp):
                sp.dma_start(rw[:, :, :], a["router_wT"].rearrange("(k p) n -> p k n", p=P)).then_inc(small_in, 16)
                sp.dma_start(rb[:, :], a["router_b"].to_broadcast([P, NEXP])).then_inc(small_in, 16)
                sp.dma_start(b1[:, :], a["b1"]).then_inc(small_in, 16)
                sp.dma_start(b2[:, :], a["b2"]).then_inc(small_in, 16)

                def load(e):
                    for f in range(FC):
                        until(sp, used, e, f, RING)
                        if isinstance(e, int):
                            src = a["w12"][(e * FC + f) * P:(e * FC + f + 1) * P, :]
                        else:
                            src = a["w12"][bass.ds(e * (FC * P) + f * P, P), :]
                        sp.dma_start(w[f % RING][2][:, :], src).then_inc(landed[f % RING], 16)
                networks(sp, load)

            @block.gpsimd
            def _(g):
                def low(e):
                    for f in range(FC):
                        hi, lo, raw = w[f % RING]
                        until(g, w_hi_ready, e, f, 0)
                        g.tensor_tensor(lo[:, :], raw[:, :], hi[:, :].bitcast(F32), ALU.subtract).then_inc(w_lo_ready, 1)
                networks(g, low)

            @block.tensor
            def _(pe):
                norm.pe_turn(pe, py)
                pe.wait_ge(norm.uT_ready, TT)
                pe.wait_ge(small_in, 64)
                for t in range(TT):
                    ins = product(pe, ph[0][:, t * NEXP:(t + 1) * NEXP], lambda k: uT[:, k, t * P:(t + 1) * P], lambda k: rw[:, k, :], DC)
                ins.then_inc(routed, 1)
                pe.wait_ge(share_ready, 1)
                for t in range(TT):
                    ins = pe.transpose(ph[1][0:E, t * P:(t + 1) * P], share[:, t, :], const[:, C_IDENT:C_IDENT + P])
                ins.then_inc(share_turned, 1)
                pe.wait_ge(shareT_ready, 1)
                for e in range(E):
                    if e >= 2:
                        pe.wait_ge(spread_out, e - 1)
                    pe.matmul(ph[2 + e % 2][:, :], const[0:E, C_IDENT + e:C_IDENT + e + 1].to_broadcast([E, P]), shareT[:, :],
                              start=True, stop=True).then_inc(spread, 1)
                for t in range(TT):
                    pe.matmul(py[t][:, :], shareT[:, t * P:(t + 1) * P], b2[:, :], start=True, stop=False)
                pe.wait_ge(u_lo_ready, 1)
                pe.wait_ge(spread_out, E)

                def first(e, f):
                    until(pe, w_lo_ready, e, f, 0)
                    until(pe, gelus, e, f, HRING)
                    hi, lo, _ = w[f % RING]
                    split_product(pe, ph[f % HRING][:, :],
                                  lambda k: hi[:, k * P:(k + 1) * P], lambda k: lo[:, k * P:(k + 1) * P],
                                  lambda k: u_hi[:, k, :], lambda k: u_lo[:, k, :], DC).then_inc(inner, 1)

                def second(e, f, last=False):
                    until(pe, h_lo_ready, e, f, 0)
                    hi, lo, _ = w[f % RING]
                    hh, hl = h_hi[f % 2], h_lo[f % 2]
                    for t in range(TT):
                        ins = split_product(pe, py[t][:, :], lambda k: hh[:, t * P:(t + 1) * P], lambda k: hl[:, t * P:(t + 1) * P],
                                            lambda k: hi[:, D:2 * D], lambda k: lo[:, D:2 * D], 1, first=False, last=last)
                    ins.then_inc(used, 1)

                def network(e):
                    for f in range(FC):
                        first(e, f)
                        if not (isinstance(e, int) and e * FC + f == 0):
                            second(e, f - 1)
                networks(pe, network)
                second(E - 1, FC - 1, last=True)

            @block.scalar
            def _(s):
                norm.act_root(s)
                s.wait_ge(norm.uT_ready, TT)
                s.activation(u_hi[:, :, :], uT[:, :, :], ACT.Copy).then_inc(u_hi_ready, 1)
                s.wait_ge(shifted, 1)
                s.activation(e2[:, :, :], e2[:, :, :], ACT.Exp).then_inc(e_ready, 1)
                for e in range(E):
                    s.wait_ge(spread, e + 1)
                    s.activation(shares[:, e, :], ph[2 + e % 2][:, :], ACT.Copy).then_inc(spread_out, 1)

                def high(e, f):
                    if isinstance(e, int):
                        if e * FC + f >= E * FC:
                            return
                        s.wait_ge(landed[f % RING], 16 * ((e * FC + f) // RING + 1))
                    else:
                        s.wait_ge(landed[f % RING], e * (16 * FC // RING) + 16 * (f // RING + 1))
                    s.activation(w[f % RING][0][:, :], w[f % RING][2][:, :], ACT.Copy).then_inc(w_hi_ready, 1)

                for f in range(AHEAD):
                    high(0, f)

                def network(e):
                    for f in range(FC):
                        until(s, inner, e, f, 0)
                        until(s, scaled, e, f, 2)
                        bias = b1[:, e * FC + f:e * FC + f + 1] if isinstance(e, int) else b1[:, bass.ds(e * FC + f, 1)]
                        s.activation(g_sb[:, f % 2, :], ph[f % HRING][:, :], ACT.Gelu_apprx_tanh, bias=bias).then_inc(gelus, 1)
                        high(e, f + AHEAD)
                        until(s, scaled, e, f, 0)
                        until(s, used, e, f, 2)
                        s.activation(h_hi[f % 2][:, :], gs[:, f % 2, :], ACT.Copy).then_inc(h_hi_ready, 1)
                networks(s, network)

            @block.vector
            def _(v):
                ch = Chain(v, step)
                norm.dve_var(ch)
                norm.dve_u(ch)
                norm.evac(v, py, v.tensor_copy)
                v.wait_ge(u_hi_ready, 1)
                v.tensor_tensor(u_lo[:, :, :], uT[:, :, :], u_hi[:, :, :].bitcast(F32), ALU.subtract).then_inc(u_lo_ready, 1)
                v.wait_ge(routed, 1)
                v.wait_ge(small_in, 64)
                ch.link(v.tensor_tensor(lg[:, :, :], ph[0][:, 0:TT * NEXP].rearrange("p (t e) -> p t e", t=TT),
                                        rb[:, :].unsqueeze(1).to_broadcast([P, TT, NEXP]), ALU.add))
                for t in range(TT):
                    ch.inc(v.max(out=m8[:, t, :], in_=lg[:, t, :]))
                ch.wait()
                for t in range(TT):
                    ch.inc(v.max_index(out=i8[:, t, :], in_max=m8[:, t, :], in_values=lg[:, t, :]))
                v.tensor_tensor(e2[:, :, :], m8[:, :, 0:2], m8[:, :, 0:1].to_broadcast([P, TT, 2]), ALU.subtract).then_inc(shifted, 1)
                ch.wait()
                ch.inc(v.tensor_copy(i8f[:, :, :], i8[:, :, :]))
                v.wait_ge(e_ready, 1)
                ch.link(v.tensor_reduce(tot[:, :], e2[:, :, :], AX.X, ALU.add))
                ch.link(v.reciprocal(tot[:, :], tot[:, :]))
                ch.link(v.tensor_tensor(e2[:, :, :], e2[:, :, :], tot[:, :].unsqueeze(2).to_broadcast([P, TT, 2]), ALU.mult))
                ch.inc(v.memset(share[:, :, 0], 1.0))
                for t in range(TT):
                    for k in range(2):
                        ch.inc(v.tensor_scalar(pick[:, t, k, :], const[:, C_IOTA:C_IOTA + NEXP], i8f[:, t, k:k + 1], e2[:, t, k:k + 1],
                                               ALU.is_equal, ALU.mult))
                ch.wait()
                v.tensor_tensor(share[:, :, 1:E], pick[:, :, 0, :], pick[:, :, 1, :], ALU.add).then_inc(share_ready, 1)
                v.wait_ge(share_turned, 1)
                v.tensor_copy(shareT[:, :], ph[1][0:E, :]).then_inc(shareT_ready, 1)
                v.wait_ge(spread_out, E)

                def network(e):
                    for f in range(FC):
                        until(v, gelus, e, f, 0)
                        until(v, h_lo_ready, e, f, 2)
                        mine = shares[:, e, :] if isinstance(e, int) else shares[:, bass.ds(e, 1), :].rearrange("p o n -> p (o n)")
                        v.tensor_tensor(gs[:, f % 2, :], g_sb[:, f % 2, :], mine, ALU.mult).then_inc(scaled, 1)
                        until(v, h_hi_ready, e, f, 0)
                        v.tensor_tensor(h_lo[f % 2][:, :], gs[:, f % 2, :], h_hi[f % 2][:, :].bitcast(F32), ALU.subtract).then_inc(h_lo_ready, 1)
                networks(v, network)
                v.wait_ge(used, E * FC)
                for t in range(TT):
                    v.tensor_tensor(x[:, t, :], x[:, t, :], py[t][:, :], ALU.add)


def build(nc, a, out):
    with ExitStack() as ctx:
        x = ctx.enter_context(nc.sbuf_tensor("x", [P, TT, D], F32))
        const = ctx.enter_context(nc.sbuf_tensor("const", [P, C_END], F32))
        load_and_norm(nc, a["x"], a["constants"], const, x)
        with nc.sbuf_tensor("qT0", [P, DC, T], F32) as qT:
            query_stage(nc, "q0", const, x, qT, a["L0_xattn_Wq"], None)
            cross_attention(nc, "c0", const, qT, a["ctxT"], a["L0_xattn_Wk"], a["L0_xattn_Wv"], mask_dram=a["mask"])
            output_stage(nc, "o0", x, qT, a["L0_xattn_Wo"])
        mixer_stage(nc, const, x, a)
        retrieval_stage(nc, const, x, a)
        with nc.sbuf_tensor("qT1", [P, DC, T], F32) as qT:
            query_stage(nc, "q1", const, x, qT, a["L1_WqT"], a["L1_bqT"])
            cross_attention(nc, "c1", const, qT, a["ctxT"], a["L1_WkT"], a["L1_WvT"], adapt=a)
            output_stage(nc, "o1", x, qT, a["L1_WoT"], a["L1_bo"])
        self_attention(nc, const, x, a)
        expert_stage(nc, const, x, a)
        store(nc, out, x)


def kernel(**i):
    import concourse.bacc as _bacc
    from concourse.bass_utils import run_bass_kernel_spmd as _run

    def col(v):
        return np.ascontiguousarray(np.asarray(v).reshape(-1, P).T)

    def t(w):
        return np.ascontiguousarray(np.asarray(w).T)

    arrays = {
        "x": np.asarray(i["x"]),
        "constants": constants(),
        "ctxT": np.ascontiguousarray(np.asarray(i["ctx_1024"]).transpose(0, 2, 1)),
        "mask": np.asarray(i["mask_BxS2_ik0"]),
        "L0_xattn_Wq": np.asarray(i["L0_xattn_Wq"]), "L0_xattn_Wk": np.asarray(i["L0_xattn_Wk"]),
        "L0_xattn_Wv": np.asarray(i["L0_xattn_Wv"]), "L0_xattn_Wo": np.asarray(i["L0_xattn_Wo"]),
    }
    arrays.update({
        "A_log": np.asarray(i["L0_attn_A_log"]), "W_BT": t(i["L0_attn_W_B"]), "W_CT": t(i["L0_attn_W_C"]),
        "W_inT": t(i["L0_attn_W_in"]), "W_outT": t(i["L0_attn_W_out"]), "b_out": np.asarray(i["L0_attn_b_out"]).reshape(1, D),
        "D_skip": col(i["L0_attn_D_skip"]), "log_dt": col(i["L0_attn_log_dt"]), "b_in": col(i["L0_attn_b_in"]),
        "ln_g": np.asarray(i["L0_attn_ln_g"]).reshape(1, D), "ln_b": np.asarray(i["L0_attn_ln_b"]).reshape(1, D),
    })
    arrays.update({
        "w_q": np.asarray(i["L0_ffn_w_q"]), "bn_gamma": col(i["L0_ffn_bn_gamma"]), "bn_beta": col(i["L0_ffn_bn_beta"]),
        "pkeys": np.ascontiguousarray(np.asarray(i["L0_ffn_keys"]).transpose(3, 2, 0, 1).reshape(PK, 2 * PH * NKEY)),
        "embed": np.concatenate([np.asarray(i["L0_ffn_down_embed"]), np.asarray(i["L0_ffn_up_embed"])], axis=1),
    })
    arrays.update({
        "L1_WqT": t(i["L1_xattn_Wq"]), "L1_WkT": t(i["L1_xattn_Wk"]), "L1_WvT": t(i["L1_xattn_Wv"]), "L1_WoT": t(i["L1_xattn_Wo"]),
        "L1_bqT": col(i["L1_xattn_bq"]), "bk": col(i["L1_xattn_bk"]), "bv": col(i["L1_xattn_bv"]), "L1_bo": np.asarray(i["L1_xattn_bo"]).reshape(1, D),
        "w1T": t(i["L1_xattn_w1"]), "w2T": t(i["L1_xattn_w2"]), "w3T": t(i["L1_xattn_w3"]),
        "b12": np.stack([np.asarray(i["L1_xattn_b1"]), np.asarray(i["L1_xattn_b2"])], axis=1), "b3": np.asarray(i["L1_xattn_b3"]).reshape(1, 1),
    })
    qkv = np.asarray(i["L1_attn_w_qkv"]).reshape(D, H, 3, DH)
    arrays.update({n: np.ascontiguousarray(qkv[:, :, k].reshape(D, D)) for k, n in enumerate(("sa_q", "sa_k", "sa_v"))})
    arrays["sa_o"] = np.asarray(i["L1_attn_w_o"])
    w1 = np.concatenate([np.asarray(i["L1_ffn_shared_w1"])[None], np.asarray(i["L1_ffn_spec_w1"])])
    w2 = np.concatenate([np.asarray(i["L1_ffn_shared_w2"])[None], np.asarray(i["L1_ffn_spec_w2"])])
    b1 = np.concatenate([np.asarray(i["L1_ffn_shared_b1"])[None], np.asarray(i["L1_ffn_spec_b1"])])
    b2 = np.concatenate([np.asarray(i["L1_ffn_shared_b2"])[None], np.asarray(i["L1_ffn_spec_b2"])])
    n = 1 + NEXP
    w1 = w1.reshape(n, FC, P, DC, P).transpose(0, 1, 4, 3, 2).reshape(n * FC * P, D)
    w2 = w2.transpose(0, 2, 1).reshape(n * FC * P, D)
    arrays.update({
        "w12": np.ascontiguousarray(np.concatenate([w1, w2], axis=1)),
        "b1": np.ascontiguousarray(b1.reshape(n * FC, P).T), "b2": b2,
        "router_wT": t(i["L1_ffn_router_w"]), "router_b": np.asarray(i["L1_ffn_router_b"]).reshape(1, NEXP),
    })

    nc = _bacc.Bacc("TRN2", target_bir_lowering=False, num_devices=1)
    a = {n: nc.dram_tensor(f"in_{n}", v.shape, mybir.dt.from_np(v.dtype), kind="ExternalInput").ap() for n, v in arrays.items()}
    out = nc.dram_tensor("out_x", (B, S, D), F32, kind="ExternalOutput").ap()
    build(nc, a, out)
    r = _run(nc, [{f"in_{n}": v for n, v in arrays.items()}], core_ids=[0])
    return r.results[0]["out_x"]
```

```python
import math
from contextlib import ExitStack

import numpy as np

import concourse.bass as bass
from concourse import mybir

F32 = mybir.dt.float32
F32R = mybir.dt.float32r
I32 = mybir.dt.int32
U32 = mybir.dt.uint32
ALU = mybir.AluOpType
ACT = mybir.ActivationFunctionType
AX = mybir.AxisListType

P = 128
B, S, D = 8, 64, 512
T = B * S
TT = T // P
BT = P // S
DC = D // P
H, DH = 16, 32
HC = P // DH
PAIRS = H // 2
KEYS = 1601
KT = -(-KEYS // P)
CHUNK = 512
NCHUNK = -(-KEYS // CHUNK)
NS = 16
PH, PK, NKEY, PTOP = 8, 128, 128, 8
NEXP = 8
FF = 2048
FC = FF // P
NEG = -1.0e30
LN_EPS = 1e-5
LOG_T_MIN, LOG_T_MAX = math.log(0.1), math.log(10.0)
DT_MIN, DT_MAX = 1e-4, 1.0
LOG_A_MIN, LOG_A_MAX = math.log(1e-8), math.log(1.0 - 1e-8)
BIG = 3.0e38

C_IDENT, C_ONES, C_CAUSAL = 0, P, 2 * P
C_STACK = 3 * P
C_HEAD = C_STACK + S
C_HALF = C_HEAD + HC
C_BAT = C_HALF + 2
C_STATE = C_BAT + B
C_IOTA = C_STATE + NS
C_TIME = C_IOTA + 8
C_TOP = C_TIME + S
C_BOT = C_TOP + P
C_DIAG = C_BOT + P
C_END = C_DIAG + D


def constants():
    c = np.zeros((P, C_END), np.float32)
    p = np.arange(P)
    c[:, C_IDENT:C_IDENT + P] = np.eye(P)
    c[:, C_ONES:C_ONES + P] = 1.0
    same = (p[:, None] // S) == (p[None, :] // S)
    c[:, C_CAUSAL:C_CAUSAL + P] = np.where(same & (p[None, :] <= p[:, None]), 0.0, NEG)
    c[:, C_STACK:C_STACK + S] = np.concatenate([np.eye(S), np.eye(S)])
    c[:, C_HEAD:C_HEAD + HC] = (p[:, None] // DH) == np.arange(HC)
    c[:, C_HALF] = (p < S) / S
    c[:, C_HALF + 1] = (p >= S) / S
    c[:, C_BAT:C_BAT + B] = (p[:, None] // NS) == np.arange(B)
    c[:, C_STATE:C_STATE + NS] = (p[:, None] % NS) == np.arange(NS)
    c[:, C_IOTA:C_IOTA + 8] = np.arange(8)
    c[:, C_TIME:C_TIME + S] = np.arange(S)[::-1]
    c[:, C_TOP:C_TOP + P] = p < S
    c[:, C_BOT:C_BOT + P] = p >= S
    c[:, C_DIAG:C_DIAG + D] = (p[:, None] // S) == (np.arange(D)[None, :] // DH) % 2
    return c


class Chain:

    def __init__(self, eng, sem):
        self.eng, self.sem, self.n, self.at, self.i, self.per = eng, sem, 0, 0, None, 0

    def loop(self, i, per):
        self.i, self.per, self.at = i, per, 0

    def end(self, rounds):
        assert self.at == self.per, f"{self.sem}: {self.at} steps in a round, not {self.per}"
        self.n += rounds * self.per
        self.i, self.at = None, 0

    def inc(self, ins):
        ins.then_inc(self.sem, 1)
        self.at += 1
        if self.i is None:
            self.n, self.at = self.n + 1, 0

    def wait(self):
        if self.i is None:
            self.eng.wait_ge(self.sem, self.n)
        else:
            self.eng.wait_ge(self.sem, self.i * self.per + (self.n + self.at))

    def link(self, ins):
        self.inc(ins)
        self.wait()


class Scope:

    def __init__(self, nc, tag):
        self.nc, self.tag, self.ctx, self.sems = nc, tag, ExitStack(), []

    def __enter__(self):
        return self

    def __exit__(self, *e):
        self.nc.clear_and_free_semaphores(self.sems)
        self.nc.all_engine_barrier()
        return self.ctx.__exit__(*e)

    def sb(self, name, shape, dt=F32):
        return self.ctx.enter_context(self.nc.sbuf_tensor(f"{self.tag}_{name}", shape, dt))

    def ps(self, name, shape):
        return self.ctx.enter_context(self.nc.psum_tensor(f"{self.tag}_{name}", shape, F32))

    def sem(self, name):
        self.sems.append(self.nc.alloc_semaphore(f"{self.tag}_{name}"))
        return self.sems[-1]


class Norm:

    def __init__(self, sc, tag, x, u, uT, ident):
        self.x, self.u, self.uT, self.ident = x, u, uT, ident
        self.stat = sc.sb(tag + "stat", [P, TT, 6])
        self.mv = sc.sb(tag + "mv", [P, TT, 2])
        self.ve = sc.sb(tag + "ve", [P, TT])
        self.sd = sc.sb(tag + "sd", [P, TT])
        self.rs = sc.sb(tag + "rs", [P, TT])
        self.var_ready = sc.sem(tag + "var_ready")
        self.root_ready = sc.sem(tag + "root_ready")
        self.u_ready = sc.sem(tag + "u_ready")
        self.turned = sc.sem(tag + "turned")
        self.uT_ready = sc.sem(tag + "uT_ready")

    def dve_var(self, ch):
        v = ch.eng
        for t in range(TT):
            ch.inc(v.bn_stats(self.stat[:, t, :], self.x[:, t, :]))
        ch.wait()
        for t in range(TT):
            ch.inc(v.bn_aggr(self.mv[:, t, :], self.stat[:, t, :]))
        ch.wait()
        v.tensor_scalar(self.ve[:, :], self.mv[:, :, 1], LN_EPS, None, ALU.add).then_inc(self.var_ready, 1)

    def act_root(self, a):
        a.wait_ge(self.var_ready, 1)
        a.activation(self.sd[:, :], self.ve[:, :], ACT.Sqrt).then_inc(self.root_ready, 1)

    def dve_u(self, ch, gain=None, shift=None):
        v = ch.eng
        v.wait_ge(self.root_ready, 1)
        ch.link(v.reciprocal(self.rs[:, :], self.sd[:, :]))
        for t in range(TT):
            ins = v.tensor_scalar(self.u[:, t, :], self.x[:, t, :], self.mv[:, t, 0:1], self.rs[:, t:t + 1],
                                  ALU.subtract, ALU.mult)
            if gain is not None:
                ch.link(ins)
                ch.link(v.tensor_tensor(self.u[:, t, :], self.u[:, t, :], gain, ALU.mult))
                ins = v.tensor_tensor(self.u[:, t, :], self.u[:, t, :], shift, ALU.add)
            ins.then_inc(self.u_ready, 1)

    def pe_turn(self, pe, banks):
        for t in range(TT):
            pe.wait_ge(self.u_ready, t + 1)
            for d in range(DC):
                ins = pe.transpose(banks[t][:, d * P:(d + 1) * P], self.u[:, t, d * P:(d + 1) * P], self.ident)
            ins.then_inc(self.turned, 1)

    def evac(self, eng, banks, copy):
        for t in range(TT):
            eng.wait_ge(self.turned, t + 1)
            copy(self.uT[:, :, t * P:(t + 1) * P],
                 banks[t][:, :].rearrange("p (d n) -> p d n", d=DC)).then_inc(self.uT_ready, 1)


def product(pe, out, lhs, rhs, n, first=True, last=True):
    for k in range(n):
        ins = pe.matmul(out, lhs(k), rhs(k), start=first and k == 0, stop=last and k == n - 1)
    return ins


def split_product(pe, out, lhs_hi, lhs_lo, rhs_hi, rhs_lo, n, first=True, last=True):
    for k in range(n):
        pe.matmul(out, lhs_hi(k), rhs_hi(k), start=first and k == 0, stop=False)
        pe.matmul(out, lhs_hi(k), rhs_lo(k), start=False, stop=False)
        ins = pe.matmul(out, lhs_lo(k), rhs_hi(k), start=False, stop=last and k == n - 1)
    return ins


def load_and_norm(nc, x_dram, const_dram, const, x):
    with Scope(nc, "ld") as sc:
        done = sc.sem("done")
        with nc.Block() as block:
            @block.sync
            def _(sp):
                sp.dma_start(x[:, :, :], x_dram.rearrange("(i e) t d -> (e t) i d", e=BT)).then_inc(done, 16)
                sp.dma_start(const[:, :], const_dram).then_inc(done, 16)
                sp.wait_ge(done, 32)


def query_stage(nc, tag, const, x, qT, wq_dram, bq_dram):
    with Scope(nc, tag) as sc:
        u = sc.sb("u", [P, TT, D])
        uT = sc.sb("uT", [P, DC, T])
        wq = sc.sb("wq", [P, DC, D])
        bq = sc.sb("bq", [P, DC])
        banks = [sc.ps(f"b{i}", [P, 512]) for i in range(8)]
        norm = Norm(sc, "n", x, u, uT, const[:, C_IDENT:C_IDENT + P])
        w_in, q_done, q_out, dve_step = (sc.sem(n) for n in ("w_in", "q_done", "q_out", "dve_step"))
        with nc.Block() as block:
            @block.sync
            def _(sp):
                sp.dma_start(wq[:, :, :], wq_dram.rearrange("(k p) n -> p k n", p=P)).then_inc(w_in, 16)
                if bq_dram is not None:
                    sp.dma_start(bq[:, :], bq_dram.rearrange("p c -> p c")).then_inc(w_in, 16)

            @block.vector
            def _(v):
                ch = Chain(v, dve_step)
                norm.dve_var(ch)
                norm.dve_u(ch)
                norm.evac(v, banks, v.tensor_copy)

            @block.scalar
            def _(a):
                norm.act_root(a)
                if bq_dram is not None:
                    a.wait_ge(w_in, 32)
                for c in range(DC):
                    a.wait_ge(q_done, c + 1)
                    if bq_dram is not None:
                        a.activation(qT[:, c, :], banks[4 + c][:, :], ACT.Identity, bias=bq[:, c:c + 1]).then_inc(q_out, 1)
                    else:
                        a.activation(qT[:, c, :], banks[4 + c][:, :], ACT.Copy).then_inc(q_out, 1)

            @block.tensor
            def _(pe):
                norm.pe_turn(pe, banks)
                pe.wait_ge(norm.uT_ready, TT)
                pe.wait_ge(w_in, 32 if bq_dram is not None else 16)
                for c in range(DC):
                    product(pe, banks[4 + c][:, :], lambda k: wq[:, k, c * P:(c + 1) * P],
                            lambda k: uT[:, k, :], DC).then_inc(q_done, 1)


def split_buffer(sc, name, shape):
    hi = sc.sb(name + "_hi", shape, F32R)
    at = -(-sc.nc.sbuf_base // 32) * 32
    lo = sc.sb(name + "_lo", shape, F32R)
    raw = sc.nc.alloc_sbuf_tensor_at(f"{sc.tag}_{name}_raw", shape, F32, offset=at)
    return hi, lo, raw


KW = -(-KEYS // KT) + (-(-KEYS // KT)) % 2
CHUNK_TILES = [4, 3, 3, 3]
assert sum(CHUNK_TILES) == KT and len(CHUNK_TILES) == NCHUNK
TILE_KEYS = [min(KW, KEYS - t * KW) for t in range(KT)]
CHUNK_AT = [KW * sum(CHUNK_TILES[:n]) for n in range(NCHUNK)]
CHUNK_KEYS = [min(KEYS - CHUNK_AT[n], KW * CHUNK_TILES[n]) for n in range(NCHUNK)]
CHUNK_OF = [n for n in range(NCHUNK) for _ in range(CHUNK_TILES[n])]
CW = max(CHUNK_KEYS)
SCORE_KEYS = [min(512, KEYS - n * 512) for n in range(4)]
QUADS = -(-KT // 4)


def attention_order(adapt, last):
    v = [("v", t) for t in range(KT)]
    k = [] if last else [("k", n, c) for n in range(NCHUNK) for c in range(DC)]
    order = []
    for p, before in enumerate((2, 1, 1, 2, 1, 2, 1, 1)):
        order += v[:before] + [("s", p)]
        del v[:before]
    order += v

    def next_k(n=1):
        order.extend(k[:n])
        del k[:n]

    if adapt:
        for step, n in (("mean", 0), ("feat", 1), ("h1", 1), ("h2", 1), ("t", 1), ("spread", 3)):
            order.append((step,))
            next_k(n)
    order.extend([("t", 0, 0), ("t", 0, 1)])
    for p in range(PAIRS):
        if not adapt:
            next_k()
        order.extend([("w", p, 0), ("t", p, 2), ("w", p, 1), ("t", p, 3)])
        if p < PAIRS - 1:
            next_k()
        order.append(("w", p, 2))
        if p < PAIRS - 1:
            order.append(("t", p + 1, 0))
        order.append(("w", p, 3))
        if p < PAIRS - 1:
            order.append(("t", p + 1, 1))
    next_k(len(k))
    order.append(("o",))
    return order


class Round:

    def __init__(self, order):
        self.order = order
        self.uses = [i for i in order if (i[0] in "kvo") or (i[0] == "t" and len(i) == 3)]
        self.by, self.nth, self.count = [], [], {"act": 0, "dve": 0}
        for i in self.uses:
            by = "act" if i[0] == "k" or (i[0] == "t" and (i[1] + i[2]) % 2) else "dve"
            self.count[by] += 1
            self.by.append(by)
            self.nth.append(self.count[by])
        self.at = {i: n for n, i in enumerate(self.uses)}


def cross_attention(nc, tag, const, qT, ctx_dram, wk_dram, wv_dram, mask_dram=None, adapt=None):
    scale = float(DH) ** -0.5
    with Scope(nc, tag) as sc:
        sem = sc.sem
        ctx = [split_buffer(sc, f"ctx{s}", [P, DC, CW + CW % 2]) for s in range(2)]
        wk = split_buffer(sc, "wk", [P, DC, D])
        wv = split_buffer(sc, "wv", [P, DC, D])
        kT = sc.sb("kT", [P, DC, KEYS])
        vk = sc.sb("vk", [P, KT, D])
        sco = sc.sb("sco", [P, PAIRS, KEYS])
        wT = sc.sb("wT", [P, 2, 4, P])
        qbd = sc.sb("qbd", [P, PAIRS, P])
        mx, nmx, rsum, rinv = (sc.sb(n, [P, PAIRS]) for n in ("mx", "nmx", "rsum", "rinv"))
        onorm = sc.sb("onorm", [P, D])
        ps_s = sc.ps("ps_s", [P, 4 * 512])
        ring = [sc.ps(f"ring{i}", [P, 512]) for i in range(2)]
        ps_o = sc.ps("ps_o", [P, 2, 512])
        ps_m = ps_o[:, 1, :]
        if mask_dram is not None:
            mask = sc.sb("mask", [P, KEYS])
        if adapt:
            p1 = sc.sb("p1", [P, KEYS])
            bk, bv = sc.sb("bk", [P, DC]), sc.sb("bv", [P, DC])
            w1T, w2T, w3T = sc.sb("w1T", [3, 64]), sc.sb("w2T", [64, 64]), sc.sb("w3T", [64, 1])
            b12, b3 = sc.sb("b12", [64, 2]), sc.sb("b3", [1, 1])
            kparts = sc.sb("kparts", [P, DC, NCHUNK])
            ksum = sc.sb("ksum", [P, DC])
            stats = sc.sb("stats", [P, PAIRS, 3])
            sums = sc.sb("sums", [P, PAIRS, 2])
            tmp, temp = sc.sb("tmp", [P, PAIRS]), sc.sb("temp", [P, PAIRS])
            featT = sc.sb("featT", [3, H])
            hid = sc.sb("hid", [64, 2, H])
            logt, invt = sc.sb("logt", [1, H]), sc.sb("invt", [1, H])

        w_in = [sem(f"w_in{s}") for s in range(2)]
        small_in, w_hi_ready, w_split = (sem(n) for n in ("small_in", "w_hi_ready", "w_split"))
        ctx_in = [sem(f"ctx_in{s}") for s in range(2)]
        ctx_hi_ready = sem("ctx_hi")
        ctx_split = sem("ctx_split")
        first_k = sem("first_k")
        first_evac = sem("first_evac")
        group = sem("group")
        act_evac = sem("act_evac")
        dve_evac = sem("dve_evac")
        q_ready = sem("q_ready")
        scored = sem("scored")
        taken = sem("taken")
        negated = sem("negated")
        probs = sem("probs")
        pv = sem("pv")
        normed = sem("normed")
        o_ready = sem("o_ready")
        mask_in = sem("mask_in")
        dve_step = sem("dve_step")
        pool_mark, pe_mark, dve_mark = sem("pool_mark"), sem("pe_mark"), sem("dve_mark")
        if adapt:
            (squared, plain, ksum_ready, mean_done, stats_ready, feat_done, feat_ready, h1_done, h1_ready, h2_done,
             h2_ready, t_done, t_clip, t_ready, spread, temp_ready) = (sem(n) for n in (
                "squared", "plain", "ksum_ready", "mean_done", "stats_ready", "feat_done", "feat_ready", "h1_done",
                "h1_ready", "h2_done", "h2_ready", "t_done", "t_clip", "t_ready", "spread", "temp_ready"))

        full, final = (Round(attention_order(adapt, last)) for last in (False, True))
        PER = len(full.uses)
        assert PER % 2 == 0, "a round has to keep the banks' parity"
        evac_sem = {"act": act_evac, "dve": dve_evac}
        CHUNKS = 2 * NCHUNK
        last_v = [max(u for i, u in full.at.items() if i[0] == "v" and CHUNK_OF[i[1]] == n) for n in range(NCHUNK)]
        last_k = [full.at[("k", n, DC - 1)] for n in range(NCHUNK)]
        through = last_v + last_k

        def emptied(eng, b, r, u):
            if u < 0:
                u += PER
                by = full.by[u]
                eng.wait_ge(evac_sem[by], b * full.count[by] + full.nth[u])
            else:
                by = r.by[u]
                eng.wait_ge(evac_sem[by], b * full.count[by] + (full.count[by] + r.nth[u]))

        def filled(eng, b, u):
            eng.wait_ge(group, b * PER + (PER + u + 1))

        def rounds(eng, body):
            with eng.Fori(0, B - 1) as b:
                body(b, full)
            body(B - 1, final)

        with nc.Block() as block:
            @block.sync
            def _(sp):
                def load(s, b, n):
                    sp.dma_start(ctx[s][2][:, :, 0:CHUNK_KEYS[n]],
                                 ctx_dram[bass.ds(b, 1), :, CHUNK_AT[n]:CHUNK_AT[n] + CHUNK_KEYS[n]].rearrange("o (k p) n -> p (o k) n", p=P)
                                 ).then_inc(ctx_in[s], 16)

                def load_weights(s, w, src):
                    sp.dma_start(w[2][:, :, :], src.rearrange("(k p) n -> p k n", p=P)).then_inc(w_in[s], 16)

                load_weights(0, wk, wk_dram)
                load(0, 0, 0)
                if adapt:
                    for dst, src in ((bk, "bk"), (bv, "bv"), (w1T, "w1T"), (w2T, "w2T"), (w3T, "w3T"), (b12, "b12"), (b3, "b3")):
                        sp.dma_start(dst[:, :], adapt[src]).then_inc(small_in, 16)
                load(1, 0, 1)
                load_weights(1, wv, wv_dram)
                for n in range(2, NCHUNK):
                    sp.wait_ge(first_k, (n - 1) * DC)
                    load(n % 2, 0, n)
                sp.wait_ge(first_k, NCHUNK * DC)

                def body(b, r):
                    if mask_dram is not None:
                        sp.wait_ge(taken, b * PAIRS + 1)
                        sp.dma_start(mask[:, :].bitcast(I32), mask_dram[bass.ds(b, 1), :].to_broadcast([P, KEYS])).then_inc(mask_in, 16)
                    for i in range(CHUNKS if r is full else NCHUNK):
                        filled(sp, b, through[i - 2] - (PER if i < 2 else 0))
                        load(i % 2, b + i // NCHUNK, i % NCHUNK)

                rounds(sp, body)

            @block.gpsimd
            def _(g):
                def split(s, n, arrived, at):
                    hi, lo, raw = ctx[s]
                    w = CHUNK_KEYS[n]
                    g.wait_ge(ctx_in[s], arrived)
                    g.sem_inc(pool_mark, 1)
                    g.tensor_copy(hi[:, :, 0:w], raw[:, :, 0:w]).then_inc(ctx_hi_ready, 1)
                    g.wait_ge(ctx_hi_ready, at)
                    g.tensor_tensor(lo[:, :, 0:w], raw[:, :, 0:w], hi[:, :, 0:w].bitcast(F32), ALU.subtract).then_inc(ctx_split, 1)

                for n in range(NCHUNK):
                    split(n % 2, n, 16 * (n // 2 + 1), n + 1)

                def body(b, r):
                    for i in range(CHUNKS if r is full else NCHUNK):
                        split(i % 2, i % NCHUNK, b * (8 * CHUNKS) + 16 * (NCHUNK // 2 + i // 2 + 1),
                              b * CHUNKS + (NCHUNK + i + 1))

                rounds(g, body)

            @block.tensor
            def _(pe):
                def project_k(bank, s, n, c):
                    w = CHUNK_KEYS[n] + CHUNK_KEYS[n] % 2
                    return split_product(pe, bank[:, 0:w],
                                         lambda k: wk[0][:, k, c * P:(c + 1) * P], lambda k: wk[1][:, k, c * P:(c + 1) * P],
                                         lambda k: ctx[s][0][:, k, 0:w], lambda k: ctx[s][1][:, k, 0:w], DC)

                pe.wait_ge(w_split, 1)
                for n in range(NCHUNK):
                    pe.wait_ge(ctx_split, n + 1)
                    for c in range(DC):
                        if n or c >= 2:
                            pe.wait_ge(first_evac, n * DC + c - 1)
                        project_k(ring[c % 2], n % 2, n, c).then_inc(first_k, 1)
                pe.sem_inc(group, PER)
                pe.wait_ge(first_evac, NCHUNK * DC)
                pe.wait_ge(w_split, 2)
                if adapt:
                    pe.wait_ge(small_in, 16 * 7)

                def body(b, r):
                    def claim(item):
                        u = r.at[item]
                        emptied(pe, b, r, u - 2)
                        return ring[u % 2]

                    for item in r.order:
                        what, i = item[0], item[1:]
                        if what == "v":
                            t, n = i[0], CHUNK_OF[i[0]]
                            o, m, s = t * KW - CHUNK_AT[n], TILE_KEYS[t], n % 2
                            if o == 0:
                                pe.wait_ge(ctx_split, b * CHUNKS + (NCHUNK + n + 1))
                            split_product(pe, claim(item)[0:m, :],
                                          lambda k: ctx[s][0][:, k, o:o + m], lambda k: ctx[s][1][:, k, o:o + m],
                                          lambda k: wv[0][:, k, :], lambda k: wv[1][:, k, :], DC).then_inc(group, 1)
                        elif what == "k":
                            n, c = i
                            if c == 0:
                                pe.wait_ge(ctx_split, b * CHUNKS + (2 * NCHUNK + n + 1))
                            if adapt and n == 0 and c == 0:
                                pe.wait_ge(ksum_ready, b + 1)
                            project_k(claim(item), n % 2, n, c).then_inc(group, 1)
                        elif what == "s":
                            p = i[0]
                            if p == 0:
                                pe.wait_ge(q_ready, b + 1)
                                emptied(pe, b, r, last_k[-1] - PER)
                            pe.wait_ge(taken, b * PAIRS + (p + 1))
                            for n, w in enumerate(SCORE_KEYS):
                                ins = pe.matmul(ps_s[:, n * 512:n * 512 + w], qbd[:, p, :],
                                                kT[:, p // 2, n * 512:n * 512 + w], start=True, stop=True)
                            ins.then_inc(scored, 1)
                        elif what == "t" and i:
                            p, g = i
                            if g == 0:
                                pe.wait_ge(probs, b * PAIRS + (p + 1))
                            bank = claim(item)
                            for j in range(4 * g, min(KT, 4 * g + 4)):
                                m = TILE_KEYS[j]
                                ins = pe.transpose(bank[0:m, (j % 4) * P:(j % 4) * P + P],
                                                   sco[:, p, j * KW:j * KW + m], const[:, C_IDENT:C_IDENT + P])
                            ins.then_inc(group, 1)
                        elif what == "w":
                            p, g = i
                            emptied(pe, b, r, r.at[("t", p, g)])
                            if p == 0 and g == 0:
                                emptied(pe, b, r, r.at[("v", KT - 1)])
                            if g == 0:
                                pe.wait_ge(normed, b * PAIRS + (p + PAIRS - 1))
                            for j in range(4 * g, min(KT, 4 * g + 4)):
                                m = TILE_KEYS[j]
                                ins = pe.matmul(ps_o[:, p % 2, 0:P], wT[0:m, g % 2, j % 4, :], vk[0:m, j, P * (p // 2):P * (p // 2) + P],
                                                start=(j == 0), stop=(j == KT - 1), skip_group_check=True)
                            if g == QUADS - 1:
                                ins.then_inc(pv, 1)
                        elif what == "o":
                            bank = claim(item)
                            pe.wait_ge(o_ready, b + 1)
                            for c in range(DC):
                                ins = pe.matmul(bank[:, c * S:(c + 1) * S], onorm[:, c * P:(c + 1) * P],
                                                const[:, C_STACK:C_STACK + S], start=True, stop=True)
                            ins.then_inc(group, 1)
                        elif what == "mean":
                            pe.wait_ge(ksum_ready, b + 1)
                            for p in range(PAIRS):
                                ins = pe.matmul(ps_m[:, p:p + 1], qbd[:, p, :], ksum[:, p // 2:p // 2 + 1], start=True, stop=True)
                            ins.then_inc(mean_done, 1)
                        elif what == "feat":
                            pe.wait_ge(stats_ready, b + 1)
                            for p in range(PAIRS):
                                ins = pe.matmul(ps_m[0:3, 16 + 2 * p:18 + 2 * p], stats[:, p, :], const[:, C_HALF:C_HALF + 2], start=True, stop=True)
                            ins.then_inc(feat_done, 1)
                        elif what == "h1":
                            pe.wait_ge(feat_ready, b + 1)
                            pe.matmul(ps_m[0:64, 32:48], w1T[:, :], featT[:, :], start=True, stop=True).then_inc(h1_done, 1)
                        elif what == "h2":
                            pe.wait_ge(h1_ready, b + 1)
                            pe.sem_inc(pe_mark, 1)
                            pe.matmul(ps_m[0:64, 48:64], w2T[:, :], hid[:, 0, :], start=True, stop=True).then_inc(h2_done, 1)
                        elif what == "t":
                            pe.wait_ge(h2_ready, b + 1)
                            pe.sem_inc(pe_mark, 1)
                            pe.matmul(ps_m[0:1, 64:80], w3T[:, :], hid[:, 1, :], start=True, stop=True).then_inc(t_done, 1)
                        elif what == "spread":
                            pe.wait_ge(t_ready, b + 1)
                            iv = invt[0:1, :].rearrange("o (p e) -> o e p", e=2)
                            pe.matmul(ps_m[:, 80:88], const[0:1, C_TOP:C_TOP + P], iv[:, 0, :], start=True, stop=False)
                            pe.matmul(ps_m[:, 80:88], const[0:1, C_BOT:C_BOT + P], iv[:, 1, :], start=False, stop=True).then_inc(spread, 1)

                rounds(pe, body)

            def turned_views(g, bank):
                if 4 * g + 4 <= KT:
                    return wT[0:KW, g % 2, :, :].rearrange("p j n -> p (j n)"), bank[0:KW, :]
                assert KT % 4 == 1
                return wT[0:TILE_KEYS[-1], g % 2, 0, :], bank[0:TILE_KEYS[-1], 0:P]

            @block.scalar
            def _(a):
                a.sem_inc(act_evac, full.count["act"])
                for s, w in enumerate((wk, wv)):
                    a.wait_ge(w_in[s], 16)
                    a.activation(w[0][:, :, :], w[2][:, :, :], ACT.Copy).then_inc(w_hi_ready, 1)
                if adapt:
                    a.wait_ge(small_in, 16 * 7)

                def take_k(bank, n, c):
                    w = CHUNK_KEYS[n]
                    dst, src = kT[:, c, CHUNK_AT[n]:CHUNK_AT[n] + w], bank[:, 0:w]
                    if adapt:
                        return a.activation(dst, src, ACT.Identity, bias=bk[:, c:c + 1], accum_out=kparts[:, c, n:n + 1])
                    return a.activation(dst, src, ACT.Copy)

                for n in range(NCHUNK):
                    for c in range(DC):
                        a.wait_ge(first_k, n * DC + c + 1)
                        take_k(ring[c % 2], n, c).then_inc(first_evac, 1)

                def body(b, r):
                    def weights(p):
                        row = sco[:, p, :]
                        a.activation(row, row, ACT.Exp, bias=nmx[:, p:p + 1], scale=temp[:, p:p + 1] if adapt else scale,
                                     accum_out=rsum[:, p:p + 1]).then_inc(probs, 1)

                    for item in r.order:
                        what, i = item[0], item[1:]
                        if what == "s":
                            p = i[0]
                            a.wait_ge(negated, b * PAIRS + (p + 1))
                            if adapt:
                                a.wait_ge(squared, b * PAIRS + (p + 1))
                                a.activation(p1[:, :], sco[:, p, :], ACT.Exp, bias=nmx[:, p:p + 1], scale=scale,
                                             accum_out=sums[:, p, 0:1]).then_inc(plain, 1)
                            else:
                                weights(p)
                        elif what == "h1":
                            a.wait_ge(h1_done, b + 1)
                            a.activation(hid[:, 0, :], ps_m[0:64, 32:48], ACT.Gelu, bias=b12[:, 0:1]).then_inc(h1_ready, 1)
                        elif what == "h2":
                            a.wait_ge(h2_done, b + 1)
                            a.activation(hid[:, 1, :], ps_m[0:64, 48:64], ACT.Gelu, bias=b12[:, 1:2]).then_inc(h2_ready, 1)
                        elif what == "t" and not i:
                            a.wait_ge(t_clip, b + 1)
                            a.activation(invt[:, :], logt[:, :], ACT.Exp, scale=-1.0).then_inc(t_ready, 1)
                        elif what == "spread":
                            a.wait_ge(temp_ready, b + 1)
                            weights(0)
                        elif what == "k":
                            filled(a, b, r.at[item])
                            take_k(ring[r.at[item] % 2], *i).then_inc(act_evac, 1)
                        elif what == "t" and r.by[r.at[item]] == "act":
                            filled(a, b, r.at[item])
                            dst, src = turned_views(i[1], ring[r.at[item] % 2])
                            a.activation(dst, src, ACT.Copy).then_inc(act_evac, 1)
                        elif what == "w" and i[1] == 0 and adapt and i[0] + 1 < PAIRS:
                            weights(i[0] + 1)

                rounds(a, body)

            @block.vector
            def _(v):
                ch = Chain(v, dve_step)
                v.sem_inc(dve_evac, full.count["dve"])
                v.sem_inc(taken, 1)
                if adapt:
                    v.sem_inc(squared, 1)
                v.sem_inc(normed, PAIRS)
                for s, w in enumerate((wk, wv)):
                    v.wait_ge(w_hi_ready, s + 1)
                    v.tensor_tensor(w[1][:, :, :], w[2][:, :, :], w[0][:, :, :].bitcast(F32), ALU.subtract).then_inc(w_split, 1)
                v.wait_ge(first_evac, NCHUNK * DC)

                def body(b, r):
                    def square(p):
                        v.wait_ge(plain, b * PAIRS + (p + 1))
                        v.tensor_tensor_reduce(p1[:, :], p1[:, :], p1[:, :], 1.0, 0.0, ALU.mult, ALU.add,
                                               sums[:, p, 1:2]).then_inc(squared, 1)

                    def norm(p):
                        v.wait_ge(pv, b * PAIRS + (p + 1))
                        ch.link(v.reciprocal(rinv[:, p:p + 1], rsum[:, p:p + 1]))
                        v.tensor_scalar(onorm[:, 64 * p:64 * p + 64], ps_o[:, p % 2, 64 * (p % 2):64 * (p % 2) + 64],
                                        rinv[:, p:p + 1], None, ALU.mult).then_inc(normed, 1)

                    for p in range(PAIRS):
                        for e in range(2):
                            h = 2 * (p % 2) + e
                            ins = v.tensor_scalar(qbd[:, p, e * S:(e + 1) * S], qT[:, p // 2, bass.ds(b * S, S)],
                                                  const[:, C_HEAD + h:C_HEAD + h + 1], None, ALU.mult)
                    ins.then_inc(q_ready, 1)
                    if mask_dram is not None:
                        v.wait_ge(mask_in, b * 16 + 16)
                        ch.link(v.tensor_scalar(mask[:, :], mask[:, :].bitcast(I32), 0.0, NEG, ALU.is_equal, ALU.mult))
                    if adapt:
                        emptied(v, b, r, last_k[-1] - PER)
                        v.tensor_reduce(ksum[:, :], kparts[:, :, :], AX.X, ALU.add).then_inc(ksum_ready, 1)

                    for item in r.order:
                        what, i = item[0], item[1:]
                        if what == "v":
                            t, u = i[0], r.at[item]
                            filled(v, b, u)
                            v.tensor_copy(vk[0:TILE_KEYS[t], t, :], ring[u % 2][0:TILE_KEYS[t], :]).then_inc(dve_evac, 1)
                        elif what == "s":
                            p = i[0]
                            v.wait_ge(scored, b * PAIRS + (p + 1))
                            if mask_dram is not None:
                                v.sem_inc(dve_mark, 1)
                                v.tensor_tensor_reduce(sco[:, p, :], ps_s[:, 0:KEYS], mask[:, :], 1.0, -BIG,
                                                       ALU.add, ALU.max, mx[:, p:p + 1]).then_inc(taken, 1)
                            else:
                                v.tensor_scalar(sco[:, p, :], ps_s[:, 0:KEYS], 1.0, -BIG, ALU.mult, ALU.max,
                                                accum_out=mx[:, p:p + 1]).then_inc(taken, 1)
                            v.wait_ge(taken, b * PAIRS + (p + 2))
                            v.tensor_scalar(nmx[:, p:p + 1], mx[:, p:p + 1], -scale, None, ALU.mult).then_inc(negated, 1)
                            if adapt and p:
                                square(p - 1)
                        elif what == "mean":
                            square(PAIRS - 1)
                            v.wait_ge(squared, b * PAIRS + (PAIRS + 1))
                            ch.link(v.reciprocal(rinv[:, :], sums[:, :, 0]))
                            ch.link(v.tensor_tensor(tmp[:, :], rinv[:, :], rinv[:, :], ALU.mult))
                            ch.link(v.tensor_tensor(tmp[:, :], tmp[:, :], sums[:, :, 1], ALU.mult))
                            v.tensor_scalar(stats[:, :, 1], mx[:, :], scale, None, ALU.mult)
                            v.tensor_scalar(stats[:, :, 2], tmp[:, :], -1.0 / KEYS, 1.0 / (KEYS - 1), ALU.add, ALU.mult)
                            v.wait_ge(mean_done, b + 1)
                            v.tensor_scalar(stats[:, :, 0], ps_m[:, 0:PAIRS], scale / KEYS, None, ALU.mult).then_inc(stats_ready, 1)
                        elif what == "feat":
                            v.wait_ge(feat_done, b + 1)
                            v.tensor_copy(featT[:, :], ps_m[0:3, 16:32]).then_inc(feat_ready, 1)
                        elif what == "t" and not i:
                            v.wait_ge(t_done, b + 1)
                            ch.link(v.tensor_scalar(logt[:, :], ps_m[0:1, 64:80], b3[:, 0:1], LOG_T_MAX, ALU.add, ALU.min))
                            v.tensor_scalar(logt[:, :], logt[:, :], LOG_T_MIN, None, ALU.max).then_inc(t_clip, 1)
                        elif what == "spread":
                            v.wait_ge(spread, b + 1)
                            ch.link(v.tensor_scalar(temp[:, :], ps_m[:, 80:88], 0.5, None, ALU.mult))
                            ch.link(v.tensor_tensor(nmx[:, :], mx[:, :], temp[:, :], ALU.mult))
                            v.tensor_scalar(nmx[:, :], nmx[:, :], -1.0, None, ALU.mult).then_inc(temp_ready, 1)
                        elif what == "t" and r.by[r.at[item]] == "dve":
                            filled(v, b, r.at[item])
                            v.tensor_copy(*turned_views(i[1], ring[r.at[item] % 2])).then_inc(dve_evac, 1)
                        elif what == "w" and i[1] == 1 and i[0]:
                            norm(i[0] - 1)
                        elif what == "o":
                            norm(PAIRS - 1)
                            v.wait_ge(normed, b * PAIRS + 2 * PAIRS)
                            v.tensor_tensor(onorm[:, :], onorm[:, :], const[:, C_DIAG:C_DIAG + D], ALU.mult).then_inc(o_ready, 1)
                            filled(v, b, r.at[item])
                            v.sem_inc(dve_mark, 1)
                            v.tensor_copy(qT[:, :, bass.ds(b * S, S)],
                                          ring[r.at[item] % 2][:, 0:DC * S].rearrange("p (c n) -> p c n", c=DC)).then_inc(dve_evac, 1)

                PER_STEPS = PAIRS + (6 if adapt else 1)
                with v.Fori(0, B - 1) as b:
                    ch.loop(b, PER_STEPS)
                    body(b, full)
                ch.end(B - 1)
                body(B - 1, final)
                if adapt:
                    v.wait_ge(small_in, 16 * 7)
                    v.wait_ge(dve_evac, B * full.count["dve"] + final.count["dve"])
                    for c in range(DC):
                        v.tensor_scalar(qT[:, c, :], qT[:, c, :], bv[:, c:c + 1], None, ALU.add)


def output_stage(nc, tag, x, aT, wo_dram, bo_dram=None):
    with Scope(nc, tag) as sc:
        wo = sc.sb("wo", [P, DC, D])
        bo = sc.sb("bo", [P, D])
        banks = [sc.ps(f"b{i}", [P, 512]) for i in range(TT)]
        w_in, done, added, step = (sc.sem(n) for n in ("w_in", "done", "added", "step"))
        with nc.Block() as block:
            @block.sync
            def _(sp):
                sp.dma_start(wo[:, :, :], wo_dram.rearrange("(k p) n -> p k n", p=P)).then_inc(w_in, 16)
                if bo_dram is not None:
                    sp.dma_start(bo[:, :], bo_dram.to_broadcast([P, D])).then_inc(w_in, 16)

            @block.tensor
            def _(pe):
                pe.wait_ge(w_in, 16 if bo_dram is None else 32)
                for t in range(TT):
                    product(pe, banks[t][:, :], lambda k: aT[:, k, t * P:(t + 1) * P], lambda k: wo[:, k, :], DC).then_inc(done, 1)

            @block.vector
            def _(v):
                ch = Chain(v, step)
                if bo_dram is not None:
                    v.wait_ge(w_in, 32)
                    for t in range(TT):
                        ch.inc(v.tensor_tensor(x[:, t, :], x[:, t, :], bo[:, :], ALU.add))
                    ch.wait()
                for t in range(TT):
                    v.wait_ge(done, t + 1)
                    v.tensor_tensor(x[:, t, :], x[:, t, :], banks[t][:, :], ALU.add)


def store(nc, out_dram, x):
    with Scope(nc, "st") as sc:
        done = sc.sem("done")
        with nc.Block() as block:
            @block.sync
            def _(sp):
                sp.dma_start(out_dram.rearrange("(i e) t d -> (e t) i d", e=BT), x[:, :, :]).then_inc(done, 16)
                sp.wait_ge(done, 16)


def mixer_stage(nc, const, x, a):
    with Scope(nc, "mx") as sc:
        sb, sem = sc.sb, sc.sem
        u, xn = sb("u", [P, TT, D]), sb("xn", [P, TT, D])
        xnT = sb("xnT", [P, DC, T])
        xp, z = sb("xp", [P, DC, T]), sb("z", [P, DC, T])
        w_in, w_out = sb("w_in", [P, DC, 2 * D]), sb("w_out", [P, DC, D])
        gain, shift, b_out = sb("gain", [P, D]), sb("shift", [P, D]), sb("b_out", [P, D])
        wc = sb("wc", [P, D])
        W_PAD = (B - 1) * NS
        wb = sb("wb", [P, DC, 2 * W_PAD + NS])
        b_in, d_skip, dt = sb("b_in", [P, 2 * DC]), sb("d_skip", [P, DC]), sb("dt", [P, DC])
        la = sb("la", [P, DC, NS])
        ea = sb("ea", [P, DC, NS])
        ex = sb("ex", [P, DC, NS * S])
        amean = sb("amean", [P, S])
        sel = sb("sel", [P, NS, S])
        dtm = sb("dtm", [P, 1])
        bp = sb("bp", [P, 2 * S - 1])
        conv = sb("conv", [P, S, S])
        xm = sb("xm", [P, S])
        xmx = sb("xmx", [P, B, S])
        y = sb("y", [P, DC, T])
        bank = [sc.ps(f"b{i}", [P, 512]) for i in range(8)]
        outer = Norm(sc, "no", x, u, None, None)
        inner = Norm(sc, "ni", u, xn, xnT, const[:, C_IDENT:C_IDENT + P])
        (big_in, small_in, dt_exp, al_ready, ea_ready, tl_ready, ex_ready, dt_ready, a_sum, xz_done, xp_ready,
         z_ready, wb_ready, b_done, xm_ready, y_sum, y_ready, out_done, step) = (sem(n) for n in (
            "big_in", "small_in", "dt_exp", "al_ready", "ea_ready", "tl_ready", "ex_ready", "dt_ready", "a_sum",
            "xz_done", "xp_ready", "z_ready", "wb_ready", "b_done", "xm_ready", "y_sum", "y_ready", "out_done", "step"))
        wb_in = sem("wb_in")
        SMALL = 5 + B
        with nc.Block() as block:
            @block.sync
            def _(sp):
                sp.dma_start(la[:, :, :], a["A_log"].rearrange("(k p) s -> p k s", p=P)).then_inc(small_in, 16)
                for dst, src in ((dt, "log_dt"), (d_skip, "D_skip"), (b_in, "b_in")):
                    sp.dma_start(dst[:, :], a[src]).then_inc(small_in, 16)
                for b in range(B):
                    sp.dma_start(wc[b * NS:(b + 1) * NS, :], a["W_CT"]).then_inc(small_in, 16)
                sp.dma_start(b_out[:, :], a["b_out"].to_broadcast([P, D])).then_inc(small_in, 16)
                for dst, src in ((gain, "ln_g"), (shift, "ln_b")):
                    sp.dma_start(dst[:, :], a[src].to_broadcast([P, D])).then_inc(big_in, 16)
                sp.dma_start(w_in[:, :, :], a["W_inT"].rearrange("(k p) n -> p k n", p=P)).then_inc(big_in, 16)
                sp.dma_start(w_out[:, :, :], a["W_outT"].rearrange("(k p) n -> p k n", p=P)).then_inc(big_in, 16)
                sp.wait_ge(wb_ready, 1)
                sp.dma_start(wb[:, :, W_PAD:W_PAD + NS], a["W_BT"].rearrange("(k p) s -> p k s", p=P)).then_inc(wb_in, 16)

            @block.gpsimd
            def _(g):
                g.memset(bp[:, 0:S - 1], 0.0)
                g.memset(wb[:, :, :], 0.0).then_inc(wb_ready, 1)

            @block.scalar
            def _(s):
                outer.act_root(s)
                inner.act_root(s)
                s.wait_ge(small_in, 16 * SMALL)
                s.activation(dt[:, :], dt[:, :], ACT.Exp).then_inc(dt_exp, 1)
                s.wait_ge(al_ready, 1)
                s.activation(ea[:, :, :], la[:, :, :], ACT.Exp).then_inc(ea_ready, 1)
                for k in range(DC):
                    s.wait_ge(tl_ready, k + 1)
                    s.activation(ex[:, k, :], ex[:, k, :], ACT.Exp).then_inc(ex_ready, 1)
                for g in range(DC):
                    s.wait_ge(xz_done, g + 1)
                    s.activation(xp[:, g, :], bank[g][:, :], ACT.Identity, bias=b_in[:, g:g + 1]).then_inc(xp_ready, 1)
                for g in range(DC, 2 * DC):
                    s.wait_ge(xz_done, g + 1)
                    s.activation(z[:, g - DC, :], bank[g - DC][:, :], ACT.Silu, bias=b_in[:, g:g + 1]).then_inc(z_ready, 1)

            @block.tensor
            def _(pe):
                inner.pe_turn(pe, bank)
                pe.wait_ge(ex_ready, DC)
                for half in range(2):
                    product(pe, bank[4 + half][:, :], lambda k: const[:, C_ONES:C_ONES + P],
                            lambda k: ex[:, k, half * 512:(half + 1) * 512], DC)
                pe.wait_ge(dt_ready, 1)
                pe.matmul(bank[6][:, 0:DC], const[:, C_ONES:C_ONES + P], dt[:, :], start=True, stop=True).then_inc(a_sum, 1)
                pe.wait_ge(inner.uT_ready, TT)
                pe.wait_ge(big_in, 16 * 4)
                for g in range(2 * DC):
                    if g >= DC:
                        pe.wait_ge(xp_ready, g - DC + 1)
                    product(pe, bank[g % 4][:, :], lambda k: w_in[:, k, g * P:(g + 1) * P], lambda k: xnT[:, k, :], DC).then_inc(xz_done, 1)
                pe.wait_ge(wb_in, 16)
                pe.wait_ge(xp_ready, DC)
                for b in range(B):
                    for k in range(DC):
                        at = W_PAD - b * NS
                        ins = pe.matmul(bank[7][:, 0:S], wb[:, k, at:at + P], xp[:, k, b * S:(b + 1) * S],
                                        start=(b == 0 and k == 0), stop=(b == B - 1 and k == DC - 1))
                ins.then_inc(b_done, 1)
                pe.wait_ge(xm_ready, 1)
                pe.wait_ge(z_ready, DC)
                for k in range(DC):
                    pe.matmul(bank[k][:, :], wc[:, k * P:(k + 1) * P], xmx[:, :, :].rearrange("p b t -> p (b t)"),
                              start=True, stop=True).then_inc(y_sum, 1)
                pe.wait_ge(y_ready, DC)
                for t in range(TT):
                    product(pe, bank[4 + t][:, :], lambda k: y[:, k, t * P:(t + 1) * P], lambda k: w_out[:, k, :], DC).then_inc(out_done, 1)

            @block.vector
            def _(v):
                ch = Chain(v, step)
                v.wait_ge(small_in, 16 * SMALL)
                v.tensor_scalar(la[:, :, :], la[:, :, :], 80.0, None, ALU.min).then_inc(al_ready, 1)
                outer.dve_var(ch)
                outer.dve_u(ch)
                v.wait_ge(outer.u_ready, TT)
                inner.dve_var(ch)
                v.wait_ge(dt_exp, 1)
                v.tensor_scalar(dt[:, :], dt[:, :], DT_MIN, DT_MAX, ALU.max, ALU.min).then_inc(dt_ready, 1)
                v.wait_ge(ea_ready, 1)
                v.wait_ge(dt_ready, 1)
                ch.link(v.tensor_tensor(la[:, :, :], ea[:, :, :], dt[:, :].unsqueeze(2).to_broadcast([P, DC, NS]), ALU.mult))
                ch.link(v.tensor_scalar(la[:, :, :], la[:, :, :], -1.0, LOG_A_MIN, ALU.mult, ALU.max))
                ch.link(v.tensor_scalar(la[:, :, :], la[:, :, :], LOG_A_MAX, None, ALU.min))
                for k in range(DC):
                    v.tensor_tensor(ex[:, k, :].rearrange("p (s t) -> p s t", s=NS),
                                    la[:, k, :].unsqueeze(2).to_broadcast([P, NS, S]),
                                    const[:, C_TIME:C_TIME + S].unsqueeze(1).to_broadcast([P, NS, S]), ALU.mult).then_inc(tl_ready, 1)
                v.wait_ge(big_in, 16 * 4)
                inner.dve_u(ch, gain[:, :], shift[:, :])
                inner.evac(v, bank, v.tensor_copy)
                v.wait_ge(a_sum, 1)
                for half in range(2):
                    n = NS // 2
                    ch.inc(v.tensor_tensor(sel[:, half * n:(half + 1) * n, :], bank[4 + half][:, :].rearrange("p (s t) -> p s t", s=n),
                                           const[:, C_STATE + half * n:C_STATE + (half + 1) * n].unsqueeze(2).to_broadcast([P, n, S]), ALU.mult))
                ch.link(v.tensor_reduce(dtm[:, :], bank[6][:, 0:DC], AX.X, ALU.add))
                ch.link(v.tensor_reduce(amean[:, :], sel[:, :, :].rearrange("p s t -> p t s"), AX.X, ALU.add))
                ch.link(v.tensor_scalar(dtm[:, :], dtm[:, :], 1.0 / D, None, ALU.mult))
                v.wait_ge(b_done, 1)
                v.wait_ge(wb_ready, 1)
                ch.link(v.tensor_scalar(bp[:, S - 1:2 * S - 1], bank[7][:, 0:S], dtm[:, 0:1], 1.0 / D, ALU.mult, ALU.mult))
                windows = bass.AP(tensor=bp[:, :].tensor, offset=0, ap=[[2 * S - 1, P], [1, S], [1, S]])
                ch.link(v.tensor_tensor(conv[:, :, :], windows, amean[:, :].unsqueeze(1).to_broadcast([P, S, S]), ALU.mult))
                ch.link(v.tensor_reduce(xm[:, :], conv[:, :, :], AX.X, ALU.add))
                v.tensor_tensor(xmx[:, :, :], xm[:, :].unsqueeze(1).to_broadcast([P, B, S]),
                                const[:, C_BAT:C_BAT + B].unsqueeze(2).to_broadcast([P, B, S]), ALU.mult).then_inc(xm_ready, 1)
                v.wait_ge(z_ready, DC)
                for k in range(DC):
                    v.wait_ge(y_sum, k + 1)
                    ch.link(v.scalar_tensor_tensor(y[:, k, :], xp[:, k, :], d_skip[:, k:k + 1], bank[k][:, :], ALU.mult, ALU.add))
                    v.tensor_tensor(y[:, k, :], y[:, k, :], z[:, k, :], ALU.mult).then_inc(y_ready, 1)
                for t in range(TT):
                    ch.inc(v.tensor_tensor(x[:, t, :], x[:, t, :], u[:, t, :], ALU.add))
                ch.wait()
                for t in range(TT):
                    ch.inc(v.tensor_tensor(x[:, t, :], x[:, t, :], b_out[:, :], ALU.add))
                ch.wait()
                for t in range(TT):
                    v.wait_ge(out_done, t + 1)
                    v.tensor_tensor(x[:, t, :], x[:, t, :], bank[4 + t][:, :], ALU.add)


def retrieval_stage(nc, const, x, a):
    with Scope(nc, "rt") as outer:
        u = outer.sb("u", [P, TT, D])
        idx = outer.sb("idx", [P, TT, PH * PTOP], I32)
        weight = outer.sb("weight", [P, TT, PH * PTOP])
        choose_experts(nc, const, x, u, idx, weight, a)
        apply_experts(nc, x, u, idx, weight, a["embed"])


def choose_experts(nc, const, x, u, idx, weight, a):
    G = 2 * PH
    with Scope(nc, "ch") as sc:
        sb, sem = sc.sb, sc.sem
        uT = sb("uT", [P, DC, T])
        wq = sb("wq", [P, DC, G * PK])
        keys = sb("keys", [P, G * NKEY])
        q = sb("q", [P, G, T])
        gamma, beta = sb("gamma", [P, G]), sb("beta", [P, G])
        stat, mv = sb("stat", [P, G, 6]), sb("mv", [P, G, 2])
        ve, sd, gs, sh = (sb(n, [P, G]) for n in ("ve", "sd", "gs", "sh"))
        s8 = sb("s8", [P, G, PTOP])
        i8 = sb("i8", [P, G, PTOP], U32)
        i8f = sb("i8f", [P, G, PTOP])
        sums = sb("sums", [P, PH, PTOP, PTOP])
        t8 = sb("t8", [P, PH, PTOP])
        pk = sb("pk", [P, PH, PTOP], U32)
        pki = sb("pki", [P, 2, PH, PTOP], U32)
        pkf = sb("pkf", [P, 2, PH, PTOP])
        eq = sb("eq", [P, PH, PTOP, PTOP])
        ixy = sb("ixy", [P, 2, PH, PTOP])
        e8 = sb("e8", [P, PH, PTOP])
        tot = sb("tot", [P, PH])
        bank = [sc.ps(f"b{i}", [P, 512]) for i in range(8)]
        norm = Norm(sc, "n", x, u, uT, const[:, C_IDENT:C_IDENT + P])
        (w_in, small_in, q_done, q_out, q_root, q_var, q_normed, sim_done, sim_used, shifted, e_ready, step) = (
            sem(n) for n in ("w_in", "small_in", "q_done", "q_out", "q_root", "q_var", "q_normed", "sim_done",
                             "sim_used", "shifted", "e_ready", "step"))
        with nc.Block() as block:
            @block.sync
            def _(sp):
                sp.dma_start(wq[:, :, :], a["w_q"].rearrange("(k p) n -> p k n", p=P)).then_inc(w_in, 16)
                sp.dma_start(keys[:, :], a["pkeys"]).then_inc(small_in, 16)
                sp.dma_start(gamma[:, :], a["bn_gamma"]).then_inc(small_in, 16)
                sp.dma_start(beta[:, :], a["bn_beta"]).then_inc(small_in, 16)

            @block.tensor
            def _(pe):
                norm.pe_turn(pe, bank)
                pe.wait_ge(norm.uT_ready, TT)
                pe.wait_ge(w_in, 16)
                for g in range(G):
                    if g >= 8:
                        pe.wait_ge(q_out, g - 7)
                    product(pe, bank[g % 8][:, :], lambda k: wq[:, k, g * PK:(g + 1) * PK], lambda k: uT[:, k, :], DC).then_inc(q_done, 1)
                pe.wait_ge(small_in, 48)
                pe.wait_ge(q_normed, G)
                for t in range(TT):
                    if t >= 2:
                        pe.wait_ge(sim_used, t - 1)
                    for g in range(G):
                        ins = pe.matmul(bank[t % 2 * 4 + g // 4][:, g % 4 * NKEY:(g % 4 + 1) * NKEY],
                                        q[:, g, t * P:(t + 1) * P], keys[:, g * NKEY:(g + 1) * NKEY], start=True, stop=True)
                    ins.then_inc(sim_done, 1)

            @block.scalar
            def _(s):
                norm.act_root(s)
                for g in range(G):
                    s.wait_ge(q_done, g + 1)
                    s.activation(q[:, g, :], bank[g % 8][:, :], ACT.Copy).then_inc(q_out, 1)
                s.wait_ge(q_var, 1)
                s.activation(sd[:, :], ve[:, :], ACT.Sqrt).then_inc(q_root, 1)
                for t in range(TT):
                    s.wait_ge(shifted, t + 1)
                    s.activation(e8[:, :, :], e8[:, :, :], ACT.Exp).then_inc(e_ready, 1)

            @block.vector
            def _(v):
                ch = Chain(v, step)
                norm.dve_var(ch)
                norm.dve_u(ch)
                norm.evac(v, bank, v.tensor_copy)
                for g in range(G):
                    v.wait_ge(q_out, g + 1)
                    ch.inc(v.bn_stats(stat[:, g, :], q[:, g, :]))
                ch.wait()
                for g in range(G):
                    ch.inc(v.bn_aggr(mv[:, g, :], stat[:, g, :]))
                ch.wait()
                v.tensor_scalar(ve[:, :], mv[:, :, 1], LN_EPS, None, ALU.add).then_inc(q_var, 1)
                v.wait_ge(q_root, 1)
                v.wait_ge(small_in, 48)
                ch.link(v.reciprocal(gs[:, :], sd[:, :]))
                ch.link(v.tensor_tensor(gs[:, :], gs[:, :], gamma[:, :], ALU.mult))
                ch.link(v.tensor_tensor(sh[:, :], mv[:, :, 0], gs[:, :], ALU.mult))
                ch.link(v.tensor_tensor(sh[:, :], beta[:, :], sh[:, :], ALU.subtract))
                for g in range(G):
                    v.tensor_scalar(q[:, g, :], q[:, g, :], gs[:, g:g + 1], sh[:, g:g + 1], ALU.mult, ALU.add).then_inc(q_normed, 1)
                iota = const[:, C_IOTA:C_IOTA + 8]
                shape = [P, PH, PTOP, PTOP]
                for t in range(TT):
                    v.wait_ge(sim_done, t + 1)
                    sims = [bank[t % 2 * 4 + g // 4][:, g % 4 * NKEY:(g % 4 + 1) * NKEY] for g in range(G)]
                    for g in range(G):
                        ch.inc(v.max(out=s8[:, g, :], in_=sims[g]))
                    ch.wait()
                    for g in range(G):
                        ins = v.max_index(out=i8[:, g, :], in_max=s8[:, g, :], in_values=sims[g])
                    ins.then_inc(sim_used, 1)
                    ch.link(v.tensor_tensor(sums[:, :, :, :], s8[:, 0:PH, :].unsqueeze(3).to_broadcast(shape),
                                            s8[:, PH:G, :].unsqueeze(2).to_broadcast(shape), ALU.add))
                    flat = sums[:, :, :, :].rearrange("p h i j -> p h (i j)")
                    for h in range(PH):
                        ch.inc(v.max(out=t8[:, h, :], in_=flat[:, h, :]))
                    ch.wait()
                    for h in range(PH):
                        ch.inc(v.max_index(out=pk[:, h, :], in_max=t8[:, h, :], in_values=flat[:, h, :]))
                    v.tensor_tensor(e8[:, :, :], t8[:, :, :], t8[:, :, 0:1].to_broadcast([P, PH, PTOP]), ALU.subtract).then_inc(shifted, 1)
                    v.wait_ge(sim_used, t + 1)
                    ch.inc(v.tensor_copy(i8f[:, :, :], i8[:, :, :]))
                    ch.wait()
                    ch.inc(v.tensor_single_scalar(pki[:, 0, :, :], pk[:, :, :], 3, ALU.logical_shift_right))
                    ch.link(v.tensor_single_scalar(pki[:, 1, :, :], pk[:, :, :], 7, ALU.bitwise_and))
                    ch.link(v.tensor_copy(pkf[:, :, :, :], pki[:, :, :, :]))
                    for side in range(2):
                        ch.link(v.tensor_tensor(eq[:, :, :, :], pkf[:, side, :, :].unsqueeze(3).to_broadcast(shape),
                                                iota.unsqueeze(1).unsqueeze(1).to_broadcast(shape), ALU.is_equal))
                        ch.link(v.tensor_tensor(eq[:, :, :, :], eq[:, :, :, :],
                                                i8f[:, side * PH:(side + 1) * PH, :].unsqueeze(2).to_broadcast(shape), ALU.mult))
                        ch.link(v.tensor_reduce(ixy[:, side, :, :], eq[:, :, :, :], AX.X, ALU.add))
                    ch.inc(v.scalar_tensor_tensor(idx[:, t, :], ixy[:, 0, :, :].rearrange("p h k -> p (h k)"), float(NKEY),
                                                  ixy[:, 1, :, :].rearrange("p h k -> p (h k)"), ALU.mult, ALU.add))
                    v.wait_ge(e_ready, t + 1)
                    ch.link(v.tensor_reduce(tot[:, :], e8[:, :, :], AX.X, ALU.add))
                    ch.link(v.reciprocal(tot[:, :], tot[:, :]))
                    ch.link(v.tensor_tensor(weight[:, t, :].rearrange("p (h k) -> p h k", h=PH), e8[:, :, :],
                                            tot[:, :].unsqueeze(2).to_broadcast([P, PH, PTOP]), ALU.mult))


def apply_experts(nc, x, u, idx, weight, embed):
    N = PTOP
    RING = 4
    with Scope(nc, "ap") as sc:
        sb, sem = sc.sb, sc.sem
        rows = sb("rows", [P, RING, N, 2 * D])
        idx_c = sb("idx_c", [P, 2, PH * PTOP], I32)
        uc, acc, wc = sb("uc", [P, D]), sb("acc", [P, D]), sb("wc", [P, PH * PTOP])
        dot, act, coef = (sb(n, [P, 2, N]) for n in ("dot", "act", "coef"))
        landed = [sem(f"landed{r}") for r in range(RING)]
        used, idx_ready, dots, gelus, step, mark, pool_mark = (
            sem(n) for n in ("used", "idx_ready", "dots", "gelus", "step", "mark", "pool_mark"))
        with nc.Block() as block:
            @block.gpsimd
            def _(g):
                with g.Fori(0, TT // 2) as i:
                    for e in range(2):
                        g.tensor_copy(idx_c[:, e, :], idx[:, bass.ds(2 * i + e, 1), :].rearrange("p o n -> p (o n)")).then_inc(idx_ready, 1)
                        g.wait_ge(idx_ready, 2 * i + (e + 1))
                        for h in range(PH):
                            g.wait_ge(used, i * (2 * PH) + (e * PH + h + 1))
                            g.sem_inc(pool_mark, 1)
                            for k in range(N):
                                g.indirect_dma_start(rows[:, h % RING, k, :], None, embed,
                                                     bass.IndirectOffsetOnAxis(ap=idx_c[:, e, h * N + k:h * N + k + 1], axis=0)
                                                     ).then_inc(landed[h % RING], 16)

            @block.scalar
            def _(s):
                with s.Fori(0, TT // 2) as i:
                    for n in range(2 * PH):
                        s.wait_ge(dots, i * (2 * PH) + (n + 1))
                        s.activation(act[:, n % 2, :], dot[:, n % 2, :], ACT.Gelu_apprx_tanh).then_inc(gelus, 1)

            @block.vector
            def _(v):
                ch = Chain(v, step)
                v.sem_inc(used, RING)
                with v.Fori(0, TT // 2) as i:
                    ch.loop(i, 2 * (2 + PH * (1 + N)))

                    def add_up(e, h):
                        n = e * PH + h
                        v.wait_ge(gelus, i * (2 * PH) + (n + 1))
                        ch.link(v.tensor_tensor(coef[:, n % 2, :], act[:, n % 2, :], wc[:, h * N:(h + 1) * N], ALU.mult))
                        for k in range(N):
                            ch.link(v.scalar_tensor_tensor(acc[:, :], rows[:, h % RING, k, D:2 * D], coef[:, n % 2, k:k + 1],
                                                           acc[:, :], ALU.mult, ALU.add))
                        v.sem_inc(used, 1)

                    for e in range(2):
                        tile = bass.ds(2 * i + e, 1)
                        v.tensor_copy(uc[:, :], u[:, tile, :].rearrange("p o n -> p (o n)"))
                        v.tensor_copy(wc[:, :], weight[:, tile, :].rearrange("p o n -> p (o n)"))
                        ch.link(v.tensor_copy(acc[:, :], x[:, tile, :].rearrange("p o n -> p (o n)")))
                        for h in range(PH + 1):
                            if h < PH:
                                n = e * PH + h
                                v.wait_ge(landed[h % RING], i * (16 * N * 2 * PH // RING) + 16 * N * (n // RING + 1))
                                for k in range(N):
                                    down = rows[:, h % RING, k, 0:D]
                                    ins = v.tensor_tensor_reduce(down, uc[:, :], down, 1.0, 0.0,
                                                                 ALU.mult, ALU.add, dot[:, n % 2, k:k + 1])
                                ins.then_inc(dots, 1)
                            if h >= 1:
                                add_up(e, h - 1)
                        ch.link(v.tensor_copy(x[:, tile, :].rearrange("p o n -> p (o n)"), acc[:, :]))
                ch.end(TT // 2)


def self_attention(nc, const, x, a):
    scale = float(D) ** -0.5
    with Scope(nc, "sa") as sc:
        sb, sem = sc.sb, sc.sem
        u, uT = sb("u", [P, TT, D]), sb("uT", [P, DC, T])
        wq, wk, wv, wo = (sb(n, [P, DC, D]) for n in ("wq", "wk", "wv", "wo"))
        qT, kT = sb("qT", [P, DC, T]), sb("kT", [P, DC, T])
        vt = sb("vt", [P, TT, D])
        s_sb = sb("s", [P, 2, H, P])
        mx, tot = sb("mx", [P, 2, H]), sb("tot", [P, 2, H])
        wT = sb("wT", [P, H, P])
        o = sb("o", [P, 2, D])
        oT = sb("oT", [P, DC, P])
        pa = sc.ps("pa", [P, 4, 512])
        pb = sc.ps("pb", [P, 4, 512])
        banks = [pa[:, i, :] for i in range(4)] + [pb[:, i, :] for i in range(4)]
        norm = Norm(sc, "n", x, u, uT, const[:, C_IDENT:C_IDENT + P])
        (w_in, wo_in, q_done, q_out, v_out, scored, taken, shifted, probs, turned, wT_ready, pv, o_ready, o_turned,
         oT_ready, done, added, step) = (sem(n) for n in (
            "w_in", "wo_in", "q_done", "q_out", "v_out", "scored", "taken", "shifted", "probs", "turned",
            "wT_ready", "pv", "o_ready", "o_turned", "oT_ready", "done", "added", "step"))
        with nc.Block() as block:
            @block.sync
            def _(sp):
                for w, n in ((wq, "sa_q"), (wk, "sa_k"), (wv, "sa_v")):
                    sp.dma_start(w[:, :, :], a[n].rearrange("(k p) n -> p k n", p=P)).then_inc(w_in, 16)
                sp.dma_start(wo[:, :, :], a["sa_o"].rearrange("(k p) n -> p k n", p=P)).then_inc(wo_in, 16)

            @block.tensor
            def _(pe):
                norm.pe_turn(pe, banks)
                pe.wait_ge(norm.uT_ready, TT)
                pe.wait_ge(w_in, 48)
                for c in range(DC):
                    product(pe, banks[c], lambda k: wq[:, k, c * P:(c + 1) * P], lambda k: uT[:, k, :], DC).then_inc(q_done, 1)
                for c in range(DC):
                    product(pe, banks[4 + c], lambda k: wk[:, k, c * P:(c + 1) * P], lambda k: uT[:, k, :], DC).then_inc(q_done, 1)
                for t in range(TT):
                    pe.wait_ge(q_out, t + 1)
                    product(pe, banks[t], lambda k: uT[:, k, t * P:(t + 1) * P], lambda k: wv[:, k, :], DC).then_inc(q_done, 1)
                pe.wait_ge(wo_in, 16)
                pe.wait_ge(q_out, 2 * DC)
                pe.wait_ge(v_out, TT)

                def scores(t):
                    for h in range(H):
                        c, i = h // HC, h % HC
                        ins = pe.matmul(pa[:, i, c * P:(c + 1) * P], qT[i * DH:(i + 1) * DH, c, t * P:(t + 1) * P],
                                        kT[i * DH:(i + 1) * DH, c, t * P:(t + 1) * P], start=True, stop=True)
                    ins.then_inc(scored, 1)

                scores(0)
                for t in range(TT):
                    pe.wait_ge(taken, HC * (t + 1))
                    if t + 1 < TT:
                        scores(t + 1)
                    pe.wait_ge(probs, t + 1)
                    if t >= 1:
                        pe.wait_ge(added, t)
                    for h in range(H):
                        ins = pe.transpose(pb[:, h // 4, (h % 4) * P:(h % 4 + 1) * P], s_sb[:, t % 2, h, :], const[:, C_IDENT:C_IDENT + P])
                        if h % 4 == 3:
                            ins.then_inc(turned, 1)
                    for h in range(H):
                        if h % 4 == 0:
                            pe.wait_ge(wT_ready, 4 * t + h // 4 + 1)
                        ins = pe.matmul(pb[:, h // 4, (h % 4) * P:(h % 4 + 1) * P], wT[:, h, :],
                                        vt[:, t, (h // HC) * P:(h // HC + 1) * P], start=True, stop=True)
                    ins.then_inc(pv, 1)
                    pe.wait_ge(o_ready, DC * (t + 1))
                    for c in range(DC):
                        ins = pe.transpose(pb[:, 0, c * P:(c + 1) * P], o[:, t % 2, c * P:(c + 1) * P], const[:, C_IDENT:C_IDENT + P])
                    ins.then_inc(o_turned, 1)
                    pe.wait_ge(oT_ready, t + 1)
                    product(pe, pb[:, 1, :], lambda k: oT[:, k, :], lambda k: wo[:, k, :], DC).then_inc(done, 1)

            @block.scalar
            def _(s):
                norm.act_root(s)
                for c in range(DC):
                    s.wait_ge(q_done, c + 1)
                    s.activation(qT[:, c, :], banks[c], ACT.Copy).then_inc(q_out, 1)
                for c in range(DC):
                    s.wait_ge(q_done, DC + c + 1)
                    s.activation(kT[:, c, :], banks[4 + c], ACT.Copy).then_inc(q_out, 1)
                for t in range(TT):
                    s.wait_ge(shifted, t + 1)
                    s.activation(s_sb[:, t % 2, :, :], s_sb[:, t % 2, :, :], ACT.Exp).then_inc(probs, 1)
                    for g in range(4):
                        s.wait_ge(turned, 4 * t + g + 1)
                        if g == 0 and t >= 1:
                            s.wait_ge(pv, t)
                        s.activation(wT[:, 4 * g:4 * g + 4, :].rearrange("p h n -> p (h n)"), pb[:, g, :], ACT.Copy).then_inc(wT_ready, 1)

            @block.vector
            def _(v):
                ch = Chain(v, step)
                norm.dve_var(ch)
                norm.dve_u(ch)
                norm.evac(v, banks, v.tensor_copy)
                for t in range(TT):
                    v.wait_ge(q_done, 2 * DC + t + 1)
                    v.tensor_copy(vt[:, t, :], banks[t]).then_inc(v_out, 1)

                def soften(t):
                    v.wait_ge(scored, t + 1)
                    if t >= 2:
                        v.wait_ge(turned, 4 * (t - 1))
                    s = s_sb[:, t % 2, :, :]
                    for i in range(HC):
                        v.scalar_tensor_tensor(s.rearrange("p (c i) n -> p i c n", i=HC)[:, i, :, :],
                                               pa[:, i, :].rearrange("p (c n) -> p c n", n=P), scale,
                                               const[:, C_CAUSAL:C_CAUSAL + P].unsqueeze(1).to_broadcast([P, DC, P]),
                                               ALU.mult, ALU.add).then_inc(taken, 1)
                    v.wait_ge(taken, HC * (t + 1))
                    ch.link(v.tensor_reduce(mx[:, t % 2, :], s, AX.X, ALU.max))
                    v.tensor_tensor(s, s, mx[:, t % 2, :].unsqueeze(2).to_broadcast([P, H, P]), ALU.subtract).then_inc(shifted, 1)

                soften(0)
                for t in range(TT):
                    v.wait_ge(probs, t + 1)
                    ch.link(v.tensor_reduce(tot[:, t % 2, :], s_sb[:, t % 2, :, :], AX.X, ALU.add))
                    ch.link(v.reciprocal(tot[:, t % 2, :], tot[:, t % 2, :]))
                    if t + 1 < TT:
                        soften(t + 1)
                    v.wait_ge(pv, t + 1)
                    for c in range(DC):
                        own = bass.AP(tensor=pb[:, :, :].tensor, offset=512 * c, ap=[[4 * 512, P], [P + DH, HC], [1, DH]])
                        v.tensor_tensor(o[:, t % 2, c * P:(c + 1) * P].rearrange("p (i n) -> p i n", i=HC), own,
                                        tot[:, t % 2, c * HC:(c + 1) * HC].unsqueeze(2).to_broadcast([P, HC, DH]),
                                        ALU.mult).then_inc(o_ready, 1)
                    v.wait_ge(o_turned, t + 1)
                    v.tensor_copy(oT[:, :, :].rearrange("p c n -> p (c n)"), pb[:, 0, :]).then_inc(oT_ready, 1)
                    v.wait_ge(done, t + 1)
                    v.tensor_tensor(x[:, t, :], x[:, t, :], pb[:, 1, :], ALU.add).then_inc(added, 1)


def expert_stage(nc, const, x, a):
    E = 1 + NEXP
    RING, HRING, AHEAD = 4, 4, 2
    with Scope(nc, "ex") as sc:
        sb, sem = sc.sb, sc.sem
        u, uT = sb("u", [P, TT, D]), sb("uT", [P, DC, T])
        u_hi, u_lo = sb("u_hi", [P, DC, T], F32R), sb("u_lo", [P, DC, T], F32R)
        w = [split_buffer(sc, f"w{r}", [P, 2 * D]) for r in range(RING)]
        b1, b2 = sb("b1", [P, E * FC]), sb("b2", [E, D])
        rw, rb = sb("rw", [P, DC, NEXP]), sb("rb", [P, NEXP])
        lg, m8, i8f = sb("lg", [P, TT, NEXP]), sb("m8", [P, TT, 8]), sb("i8f", [P, TT, 8])
        i8 = sb("i8", [P, TT, 8], U32)
        e2, tot = sb("e2", [P, TT, 2]), sb("tot", [P, TT])
        pick = sb("pick", [P, TT, 2, NEXP])
        share = sb("share", [P, TT, E])
        shareT = sb("shareT", [E, T])
        shares = sb("shares", [P, E, T])
        g_sb, gs = sb("g", [P, 2, T]), sb("gs", [P, 2, T])
        h_hi, h_lo = ([sb(f"h_{n}{r}", [P, T], F32R) for r in range(2)] for n in ("hi", "lo"))
        py = [sc.ps(f"py{t}", [P, 512]) for t in range(TT)]
        ph = [sc.ps(f"ph{r}", [P, 512]) for r in range(HRING)]
        norm = Norm(sc, "n", x, u, uT, const[:, C_IDENT:C_IDENT + P])
        landed = [sem(f"landed{r}") for r in range(RING)]
        (small_in, u_hi_ready, u_lo_ready, routed, shifted, e_ready, share_ready, share_turned, shareT_ready, spread,
         spread_out, w_hi_ready, w_lo_ready, inner, gelus, scaled, h_hi_ready, h_lo_ready, used, step) = (sem(n) for n in (
            "small_in", "u_hi_ready", "u_lo_ready", "routed", "shifted", "e_ready", "share_ready", "share_turned",
            "shareT_ready", "spread", "spread_out", "w_hi_ready", "w_lo_ready", "inner", "gelus", "scaled",
            "h_hi_ready", "h_lo_ready", "used", "step"))


        def networks(eng, body):
            body(0)
            with eng.Fori(1, E - 1) as e:
                body(e)
            body(E - 1)

        def until(eng, s, e, f, back):
            if isinstance(e, int) and e * FC + f - back < 0:
                return
            if isinstance(e, int):
                eng.wait_ge(s, e * FC + f - back + 1)
            else:
                eng.wait_ge(s, e * FC + (f - back + 1))

        with nc.Block() as block:
            @block.sync
            def _(sp):
                sp.dma_start(rw[:, :, :], a["router_wT"].rearrange("(k p) n -> p k n", p=P)).then_inc(small_in, 16)
                sp.dma_start(rb[:, :], a["router_b"].to_broadcast([P, NEXP])).then_inc(small_in, 16)
                sp.dma_start(b1[:, :], a["b1"]).then_inc(small_in, 16)
                sp.dma_start(b2[:, :], a["b2"]).then_inc(small_in, 16)

                def load(e):
                    for f in range(FC):
                        until(sp, used, e, f, RING)
                        if isinstance(e, int):
                            src = a["w12"][(e * FC + f) * P:(e * FC + f + 1) * P, :]
                        else:
                            src = a["w12"][bass.ds(e * (FC * P) + f * P, P), :]
                        sp.dma_start(w[f % RING][2][:, :], src).then_inc(landed[f % RING], 16)
                networks(sp, load)

            @block.gpsimd
            def _(g):
                def low(e):
                    for f in range(FC):
                        hi, lo, raw = w[f % RING]
                        until(g, w_hi_ready, e, f, 0)
                        g.tensor_tensor(lo[:, :], raw[:, :], hi[:, :].bitcast(F32), ALU.subtract).then_inc(w_lo_ready, 1)
                networks(g, low)

            @block.tensor
            def _(pe):
                norm.pe_turn(pe, py)
                pe.wait_ge(norm.uT_ready, TT)
                pe.wait_ge(small_in, 64)
                for t in range(TT):
                    ins = product(pe, ph[0][:, t * NEXP:(t + 1) * NEXP], lambda k: uT[:, k, t * P:(t + 1) * P], lambda k: rw[:, k, :], DC)
                ins.then_inc(routed, 1)
                pe.wait_ge(share_ready, 1)
                for t in range(TT):
                    ins = pe.transpose(ph[1][0:E, t * P:(t + 1) * P], share[:, t, :], const[:, C_IDENT:C_IDENT + P])
                ins.then_inc(share_turned, 1)
                pe.wait_ge(shareT_ready, 1)
                for e in range(E):
                    if e >= 2:
                        pe.wait_ge(spread_out, e - 1)
                    pe.matmul(ph[2 + e % 2][:, :], const[0:E, C_IDENT + e:C_IDENT + e + 1].to_broadcast([E, P]), shareT[:, :],
                              start=True, stop=True).then_inc(spread, 1)
                for t in range(TT):
                    pe.matmul(py[t][:, :], shareT[:, t * P:(t + 1) * P], b2[:, :], start=True, stop=False)
                pe.wait_ge(u_lo_ready, 1)
                pe.wait_ge(spread_out, E)

                def first(e, f):
                    until(pe, w_lo_ready, e, f, 0)
                    until(pe, gelus, e, f, HRING)
                    hi, lo, _ = w[f % RING]
                    split_product(pe, ph[f % HRING][:, :],
                                  lambda k: hi[:, k * P:(k + 1) * P], lambda k: lo[:, k * P:(k + 1) * P],
                                  lambda k: u_hi[:, k, :], lambda k: u_lo[:, k, :], DC).then_inc(inner, 1)

                def second(e, f, last=False):
                    until(pe, h_lo_ready, e, f, 0)
                    hi, lo, _ = w[f % RING]
                    hh, hl = h_hi[f % 2], h_lo[f % 2]
                    for t in range(TT):
                        ins = split_product(pe, py[t][:, :], lambda k: hh[:, t * P:(t + 1) * P], lambda k: hl[:, t * P:(t + 1) * P],
                                            lambda k: hi[:, D:2 * D], lambda k: lo[:, D:2 * D], 1, first=False, last=last)
                    ins.then_inc(used, 1)

                def network(e):
                    for f in range(FC):
                        first(e, f)
                        if not (isinstance(e, int) and e * FC + f == 0):
                            second(e, f - 1)
                networks(pe, network)
                second(E - 1, FC - 1, last=True)

            @block.scalar
            def _(s):
                norm.act_root(s)
                s.wait_ge(norm.uT_ready, TT)
                s.activation(u_hi[:, :, :], uT[:, :, :], ACT.Copy).then_inc(u_hi_ready, 1)
                s.wait_ge(shifted, 1)
                s.activation(e2[:, :, :], e2[:, :, :], ACT.Exp).then_inc(e_ready, 1)
                for e in range(E):
                    s.wait_ge(spread, e + 1)
                    s.activation(shares[:, e, :], ph[2 + e % 2][:, :], ACT.Copy).then_inc(spread_out, 1)

                def high(e, f):
                    if isinstance(e, int):
                        if e * FC + f >= E * FC:
                            return
                        s.wait_ge(landed[f % RING], 16 * ((e * FC + f) // RING + 1))
                    else:
                        s.wait_ge(landed[f % RING], e * (16 * FC // RING) + 16 * (f // RING + 1))
                    s.activation(w[f % RING][0][:, :], w[f % RING][2][:, :], ACT.Copy).then_inc(w_hi_ready, 1)

                for f in range(AHEAD):
                    high(0, f)

                def network(e):
                    for f in range(FC):
                        until(s, inner, e, f, 0)
                        until(s, scaled, e, f, 2)
                        bias = b1[:, e * FC + f:e * FC + f + 1] if isinstance(e, int) else b1[:, bass.ds(e * FC + f, 1)]
                        s.activation(g_sb[:, f % 2, :], ph[f % HRING][:, :], ACT.Gelu_apprx_tanh, bias=bias).then_inc(gelus, 1)
                        high(e, f + AHEAD)
                        until(s, scaled, e, f, 0)
                        until(s, used, e, f, 2)
                        s.activation(h_hi[f % 2][:, :], gs[:, f % 2, :], ACT.Copy).then_inc(h_hi_ready, 1)
                networks(s, network)

            @block.vector
            def _(v):
                ch = Chain(v, step)
                norm.dve_var(ch)
                norm.dve_u(ch)
                norm.evac(v, py, v.tensor_copy)
                v.wait_ge(u_hi_ready, 1)
                v.tensor_tensor(u_lo[:, :, :], uT[:, :, :], u_hi[:, :, :].bitcast(F32), ALU.subtract).then_inc(u_lo_ready, 1)
                v.wait_ge(routed, 1)
                v.wait_ge(small_in, 64)
                ch.link(v.tensor_tensor(lg[:, :, :], ph[0][:, 0:TT * NEXP].rearrange("p (t e) -> p t e", t=TT),
                                        rb[:, :].unsqueeze(1).to_broadcast([P, TT, NEXP]), ALU.add))
                for t in range(TT):
                    ch.inc(v.max(out=m8[:, t, :], in_=lg[:, t, :]))
                ch.wait()
                for t in range(TT):
                    ch.inc(v.max_index(out=i8[:, t, :], in_max=m8[:, t, :], in_values=lg[:, t, :]))
                v.tensor_tensor(e2[:, :, :], m8[:, :, 0:2], m8[:, :, 0:1].to_broadcast([P, TT, 2]), ALU.subtract).then_inc(shifted, 1)
                ch.wait()
                ch.inc(v.tensor_copy(i8f[:, :, :], i8[:, :, :]))
                v.wait_ge(e_ready, 1)
                ch.link(v.tensor_reduce(tot[:, :], e2[:, :, :], AX.X, ALU.add))
                ch.link(v.reciprocal(tot[:, :], tot[:, :]))
                ch.link(v.tensor_tensor(e2[:, :, :], e2[:, :, :], tot[:, :].unsqueeze(2).to_broadcast([P, TT, 2]), ALU.mult))
                ch.inc(v.memset(share[:, :, 0], 1.0))
                for t in range(TT):
                    for k in range(2):
                        ch.inc(v.tensor_scalar(pick[:, t, k, :], const[:, C_IOTA:C_IOTA + NEXP], i8f[:, t, k:k + 1], e2[:, t, k:k + 1],
                                               ALU.is_equal, ALU.mult))
                ch.wait()
                v.tensor_tensor(share[:, :, 1:E], pick[:, :, 0, :], pick[:, :, 1, :], ALU.add).then_inc(share_ready, 1)
                v.wait_ge(share_turned, 1)
                v.tensor_copy(shareT[:, :], ph[1][0:E, :]).then_inc(shareT_ready, 1)
                v.wait_ge(spread_out, E)

                def network(e):
                    for f in range(FC):
                        until(v, gelus, e, f, 0)
                        until(v, h_lo_ready, e, f, 2)
                        mine = shares[:, e, :] if isinstance(e, int) else shares[:, bass.ds(e, 1), :].rearrange("p o n -> p (o n)")
                        v.tensor_tensor(gs[:, f % 2, :], g_sb[:, f % 2, :], mine, ALU.mult).then_inc(scaled, 1)
                        until(v, h_hi_ready, e, f, 0)
                        v.tensor_tensor(h_lo[f % 2][:, :], gs[:, f % 2, :], h_hi[f % 2][:, :].bitcast(F32), ALU.subtract).then_inc(h_lo_ready, 1)
                networks(v, network)
                v.wait_ge(used, E * FC)
                for t in range(TT):
                    v.tensor_tensor(x[:, t, :], x[:, t, :], py[t][:, :], ALU.add)


def build(nc, a, out):
    with ExitStack() as ctx:
        x = ctx.enter_context(nc.sbuf_tensor("x", [P, TT, D], F32))
        const = ctx.enter_context(nc.sbuf_tensor("const", [P, C_END], F32))
        load_and_norm(nc, a["x"], a["constants"], const, x)
        with nc.sbuf_tensor("qT0", [P, DC, T], F32) as qT:
            query_stage(nc, "q0", const, x, qT, a["L0_xattn_Wq"], None)
            cross_attention(nc, "c0", const, qT, a["ctxT"], a["L0_xattn_Wk"], a["L0_xattn_Wv"], mask_dram=a["mask"])
            output_stage(nc, "o0", x, qT, a["L0_xattn_Wo"])
        mixer_stage(nc, const, x, a)
        retrieval_stage(nc, const, x, a)
        with nc.sbuf_tensor("qT1", [P, DC, T], F32) as qT:
            query_stage(nc, "q1", const, x, qT, a["L1_WqT"], a["L1_bqT"])
            cross_attention(nc, "c1", const, qT, a["ctxT"], a["L1_WkT"], a["L1_WvT"], adapt=a)
            output_stage(nc, "o1", x, qT, a["L1_WoT"], a["L1_bo"])
        self_attention(nc, const, x, a)
        expert_stage(nc, const, x, a)
        store(nc, out, x)


def kernel(**i):
    import concourse.bacc as _bacc
    from concourse.bass_utils import run_bass_kernel_spmd as _run

    def col(v):
        return np.ascontiguousarray(np.asarray(v).reshape(-1, P).T)

    def t(w):
        return np.ascontiguousarray(np.asarray(w).T)

    arrays = {
        "x": np.asarray(i["x"]),
        "constants": constants(),
        "ctxT": np.ascontiguousarray(np.asarray(i["ctx_1024"]).transpose(0, 2, 1)),
        "mask": np.asarray(i["mask_BxS2_ik0"]),
        "L0_xattn_Wq": np.asarray(i["L0_xattn_Wq"]), "L0_xattn_Wk": np.asarray(i["L0_xattn_Wk"]),
        "L0_xattn_Wv": np.asarray(i["L0_xattn_Wv"]), "L0_xattn_Wo": np.asarray(i["L0_xattn_Wo"]),
    }
    arrays.update({
        "A_log": np.asarray(i["L0_attn_A_log"]), "W_BT": t(i["L0_attn_W_B"]), "W_CT": t(i["L0_attn_W_C"]),
        "W_inT": t(i["L0_attn_W_in"]), "W_outT": t(i["L0_attn_W_out"]), "b_out": np.asarray(i["L0_attn_b_out"]).reshape(1, D),
        "D_skip": col(i["L0_attn_D_skip"]), "log_dt": col(i["L0_attn_log_dt"]), "b_in": col(i["L0_attn_b_in"]),
        "ln_g": np.asarray(i["L0_attn_ln_g"]).reshape(1, D), "ln_b": np.asarray(i["L0_attn_ln_b"]).reshape(1, D),
    })
    arrays.update({
        "w_q": np.asarray(i["L0_ffn_w_q"]), "bn_gamma": col(i["L0_ffn_bn_gamma"]), "bn_beta": col(i["L0_ffn_bn_beta"]),
        "pkeys": np.ascontiguousarray(np.asarray(i["L0_ffn_keys"]).transpose(3, 2, 0, 1).reshape(PK, 2 * PH * NKEY)),
        "embed": np.concatenate([np.asarray(i["L0_ffn_down_embed"]), np.asarray(i["L0_ffn_up_embed"])], axis=1),
    })
    arrays.update({
        "L1_WqT": t(i["L1_xattn_Wq"]), "L1_WkT": t(i["L1_xattn_Wk"]), "L1_WvT": t(i["L1_xattn_Wv"]), "L1_WoT": t(i["L1_xattn_Wo"]),
        "L1_bqT": col(i["L1_xattn_bq"]), "bk": col(i["L1_xattn_bk"]), "bv": col(i["L1_xattn_bv"]), "L1_bo": np.asarray(i["L1_xattn_bo"]).reshape(1, D),
        "w1T": t(i["L1_xattn_w1"]), "w2T": t(i["L1_xattn_w2"]), "w3T": t(i["L1_xattn_w3"]),
        "b12": np.stack([np.asarray(i["L1_xattn_b1"]), np.asarray(i["L1_xattn_b2"])], axis=1), "b3": np.asarray(i["L1_xattn_b3"]).reshape(1, 1),
    })
    qkv = np.asarray(i["L1_attn_w_qkv"]).reshape(D, H, 3, DH)
    arrays.update({n: np.ascontiguousarray(qkv[:, :, k].reshape(D, D)) for k, n in enumerate(("sa_q", "sa_k", "sa_v"))})
    arrays["sa_o"] = np.asarray(i["L1_attn_w_o"])
    w1 = np.concatenate([np.asarray(i["L1_ffn_shared_w1"])[None], np.asarray(i["L1_ffn_spec_w1"])])
    w2 = np.concatenate([np.asarray(i["L1_ffn_shared_w2"])[None], np.asarray(i["L1_ffn_spec_w2"])])
    b1 = np.concatenate([np.asarray(i["L1_ffn_shared_b1"])[None], np.asarray(i["L1_ffn_spec_b1"])])
    b2 = np.concatenate([np.asarray(i["L1_ffn_shared_b2"])[None], np.asarray(i["L1_ffn_spec_b2"])])
    n = 1 + NEXP
    w1 = w1.reshape(n, FC, P, DC, P).transpose(0, 1, 4, 3, 2).reshape(n * FC * P, D)
    w2 = w2.transpose(0, 2, 1).reshape(n * FC * P, D)
    arrays.update({
        "w12": np.ascontiguousarray(np.concatenate([w1, w2], axis=1)),
        "b1": np.ascontiguousarray(b1.reshape(n * FC, P).T), "b2": b2,
        "router_wT": t(i["L1_ffn_router_w"]), "router_b": np.asarray(i["L1_ffn_router_b"]).reshape(1, NEXP),
    })

    nc = _bacc.Bacc("TRN2", target_bir_lowering=False, num_devices=1)
    a = {n: nc.dram_tensor(f"in_{n}", v.shape, mybir.dt.from_np(v.dtype), kind="ExternalInput").ap() for n, v in arrays.items()}
    out = nc.dram_tensor("out_x", (B, S, D), F32, kind="ExternalOutput").ap()
    build(nc, a, out)
    r = _run(nc, [{f"in_{n}": v for n, v in arrays.items()}], core_ids=[0])
    return r.results[0]["out_x"]
```

```python
import math
from contextlib import ExitStack

import numpy as np

import concourse.bass as bass
from concourse import mybir

F32 = mybir.dt.float32
F32R = mybir.dt.float32r
I32 = mybir.dt.int32
U32 = mybir.dt.uint32
ALU = mybir.AluOpType
ACT = mybir.ActivationFunctionType
AX = mybir.AxisListType

P = 128
B, S, D = 8, 64, 512
T = B * S
TT = T // P
BT = P // S
DC = D // P
H, DH = 16, 32
HC = P // DH
PAIRS = H // 2
KEYS = 1601
KT = -(-KEYS // P)
NS = 16
PH, PK, NKEY, PTOP = 8, 128, 128, 8
NEXP = 8
FF = 2048
FC = FF // P
NEG = -1.0e30
LN_EPS = 1e-5
LOG_T_MIN, LOG_T_MAX = math.log(0.1), math.log(10.0)
DT_MIN, DT_MAX = 1e-4, 1.0
LOG_A_MIN, LOG_A_MAX = math.log(1e-8), math.log(1.0 - 1e-8)
BIG = 3.0e38

C_IDENT, C_ONES, C_CAUSAL = 0, P, 2 * P
C_STACK = 3 * P
C_HEAD = C_STACK + S
C_HALF = C_HEAD + HC
C_BAT = C_HALF + 2
C_STATE = C_BAT + B
C_IOTA = C_STATE + NS
C_TIME = C_IOTA + 8
C_TOP = C_TIME + S
C_BOT = C_TOP + P
C_DIAG = C_BOT + P
C_END = C_DIAG + 2 * DH


def constants():
    c = np.zeros((P, C_END), np.float32)
    p = np.arange(P)
    c[:, C_IDENT:C_IDENT + P] = np.eye(P)
    c[:, C_ONES:C_ONES + P] = 1.0
    same = (p[:, None] // S) == (p[None, :] // S)
    c[:, C_CAUSAL:C_CAUSAL + P] = np.where(same & (p[None, :] <= p[:, None]), 0.0, NEG)
    c[:, C_STACK:C_STACK + S] = np.concatenate([np.eye(S), np.eye(S)])
    c[:, C_HEAD:C_HEAD + HC] = (p[:, None] // DH) == np.arange(HC)
    c[:, C_HALF] = (p < S) / S
    c[:, C_HALF + 1] = (p >= S) / S
    c[:, C_BAT:C_BAT + B] = (p[:, None] // NS) == np.arange(B)
    c[:, C_STATE:C_STATE + NS] = (p[:, None] % NS) == np.arange(NS)
    c[:, C_IOTA:C_IOTA + 8] = np.arange(8)
    c[:, C_TIME:C_TIME + S] = np.arange(S)[::-1]
    c[:, C_TOP:C_TOP + P] = p < S
    c[:, C_BOT:C_BOT + P] = p >= S
    c[:, C_DIAG:C_DIAG + 2 * DH] = (p[:, None] // S) == (np.arange(2 * DH)[None, :] // DH)
    return c


class Chain:

    def __init__(self, eng, sem):
        self.eng, self.sem, self.n, self.at, self.i, self.per = eng, sem, 0, 0, None, 0

    def loop(self, i, per):
        self.i, self.per, self.at = i, per, 0

    def end(self, rounds):
        assert self.at == self.per, f"{self.sem}: {self.at} steps in a round, not {self.per}"
        self.n += rounds * self.per
        self.i, self.at = None, 0

    def inc(self, ins):
        ins.then_inc(self.sem, 1)
        self.at += 1
        if self.i is None:
            self.n, self.at = self.n + 1, 0

    def wait(self):
        if self.i is None:
            self.eng.wait_ge(self.sem, self.n)
        else:
            self.eng.wait_ge(self.sem, self.i * self.per + (self.n + self.at))

    def link(self, ins):
        self.inc(ins)
        self.wait()


class Scope:

    def __init__(self, nc, tag):
        self.nc, self.tag, self.ctx, self.sems = nc, tag, ExitStack(), []

    def __enter__(self):
        return self

    def __exit__(self, *e):
        self.nc.clear_and_free_semaphores(self.sems)
        self.nc.all_engine_barrier()
        return self.ctx.__exit__(*e)

    def sb(self, name, shape, dt=F32):
        return self.ctx.enter_context(self.nc.sbuf_tensor(f"{self.tag}_{name}", shape, dt))

    def ps(self, name, shape):
        return self.ctx.enter_context(self.nc.psum_tensor(f"{self.tag}_{name}", shape, F32))

    def sem(self, name):
        self.sems.append(self.nc.alloc_semaphore(f"{self.tag}_{name}"))
        return self.sems[-1]


class Lent:

    def __init__(self, flat):
        self.flat, self.at = flat, 0

    def __call__(self, name, shape):
        n = int(np.prod(shape[1:]))
        assert self.at + n <= self.flat.shape[1], name
        view = self.flat[:, self.at:self.at + n]
        self.at += n
        return view if len(shape) == 2 else view.rearrange("p (a b) -> p a b", b=shape[2])


class Weights:

    def __init__(self, sc, sources):
        self.sources, self.buf, self.sem, self.need = sources, {}, {}, {}
        for group, name, shape, _ in sources:
            self.buf[name] = sc.sb(name, shape)
            if group not in self.sem:
                self.sem[group], self.need[group] = sc.sem(group), 0
            self.need[group] += 16

    def load(self, sp):
        for group, name, _, src in self.sources:
            dst = self.buf[name]
            sp.dma_start(dst[:, :, :] if len(dst.shape) == 3 else dst[:, :], src).then_inc(self.sem[group], 16)

    def wait(self, eng, group):
        eng.wait_ge(self.sem[group], self.need[group])


def chunks(w):
    return w.rearrange("(k p) n -> p k n", p=P)


class Norm:

    def __init__(self, sc, tag, x, u, uT, ident, sb=None):
        self.x, self.u, self.uT, self.ident = x, u, uT, ident
        sb = sb or sc.sb
        self.stat = sb(tag + "stat", [P, TT, 6])
        self.mv = sb(tag + "mv", [P, TT, 2])
        self.ve = sb(tag + "ve", [P, TT])
        self.sd = sb(tag + "sd", [P, TT])
        self.rs = sb(tag + "rs", [P, TT])
        self.var_ready = sc.sem(tag + "var_ready")
        self.root_ready = sc.sem(tag + "root_ready")
        self.u_ready = sc.sem(tag + "u_ready")
        self.turned = sc.sem(tag + "turned")
        self.uT_ready = sc.sem(tag + "uT_ready")

    def dve_var(self, ch):
        v = ch.eng
        for t in range(TT):
            ch.inc(v.bn_stats(self.stat[:, t, :], self.x[:, t, :]))
        ch.wait()
        for t in range(TT):
            ch.inc(v.bn_aggr(self.mv[:, t, :], self.stat[:, t, :]))
        ch.wait()
        v.tensor_scalar(self.ve[:, :], self.mv[:, :, 1], LN_EPS, None, ALU.add).then_inc(self.var_ready, 1)

    def act_root(self, a):
        a.wait_ge(self.var_ready, 1)
        a.activation(self.sd[:, :], self.ve[:, :], ACT.Sqrt).then_inc(self.root_ready, 1)

    def dve_u(self, ch, gain=None, shift=None):
        v = ch.eng
        v.wait_ge(self.root_ready, 1)
        ch.link(v.reciprocal(self.rs[:, :], self.sd[:, :]))
        for t in range(TT):
            ins = v.tensor_scalar(self.u[:, t, :], self.x[:, t, :], self.mv[:, t, 0:1], self.rs[:, t:t + 1],
                                  ALU.subtract, ALU.mult)
            if gain is not None:
                ch.link(ins)
                ch.link(v.tensor_tensor(self.u[:, t, :], self.u[:, t, :], gain, ALU.mult))
                ins = v.tensor_tensor(self.u[:, t, :], self.u[:, t, :], shift, ALU.add)
            ins.then_inc(self.u_ready, 1)

    def pe_turn(self, pe, banks):
        for t in range(TT):
            pe.wait_ge(self.u_ready, t + 1)
            for d in range(DC):
                ins = pe.transpose(banks[t][:, d * P:(d + 1) * P], self.u[:, t, d * P:(d + 1) * P], self.ident)
            ins.then_inc(self.turned, 1)

    def evac(self, eng, banks, copy):
        for t in range(TT):
            eng.wait_ge(self.turned, t + 1)
            copy(self.uT[:, :, t * P:(t + 1) * P],
                 banks[t][:, :].rearrange("p (d n) -> p d n", d=DC)).then_inc(self.uT_ready, 1)


def product(pe, out, lhs, rhs, n, first=True, last=True):
    for k in range(n):
        ins = pe.matmul(out, lhs(k), rhs(k), start=first and k == 0, stop=last and k == n - 1)
    return ins


def split_product(pe, out, lhs_hi, lhs_lo, rhs_hi, rhs_lo, n, first=True, last=True):
    for k in range(n):
        pe.matmul(out, lhs_hi(k), rhs_hi(k), start=first and k == 0, stop=False)
        pe.matmul(out, lhs_hi(k), rhs_lo(k), start=False, stop=False)
        ins = pe.matmul(out, lhs_lo(k), rhs_hi(k), start=False, stop=last and k == n - 1)
    return ins


def load_and_norm(nc, x_dram, const_dram, const, x):
    with Scope(nc, "ld") as sc:
        done = sc.sem("done")
        with nc.Block() as block:
            @block.sync
            def _(sp):
                sp.dma_start(x[:, :, :], x_dram.rearrange("(i e) t d -> (e t) i d", e=BT)).then_inc(done, 16)
                sp.dma_start(const[:, :], const_dram).then_inc(done, 16)
                sp.wait_ge(done, 32)


def split_buffer(sc, name, shape):
    hi = sc.sb(name + "_hi", shape, F32R)
    at = -(-sc.nc.sbuf_base // 32) * 32
    lo = sc.sb(name + "_lo", shape, F32R)
    raw = sc.nc.alloc_sbuf_tensor_at(f"{sc.tag}_{name}_raw", shape, F32, offset=at)
    return hi, lo, raw


KW = -(-KEYS // KT) + (-(-KEYS // KT)) % 2
CHUNK_TILES = [3, 2, 2, 2, 2, 2]
NSLOT = 3
NCHUNK = len(CHUNK_TILES)
assert sum(CHUNK_TILES) == KT and NCHUNK % NSLOT == 0
TILE_KEYS = [min(KW, KEYS - t * KW) for t in range(KT)]
CHUNK_AT = [KW * sum(CHUNK_TILES[:n]) for n in range(NCHUNK)]
CHUNK_KEYS = [min(KEYS - CHUNK_AT[n], KW * CHUNK_TILES[n]) for n in range(NCHUNK)]
CHUNK_OF = [n for n in range(NCHUNK) for _ in range(CHUNK_TILES[n])]
CW = max(CHUNK_KEYS)
K_GROUPS = [(n, c, 4 // CHUNK_TILES[n]) for n in range(NCHUNK) for c in range(0, DC, 4 // CHUNK_TILES[n])]
SCORE_KEYS = [min(512, KEYS - n * 512) for n in range(4)]
QUADS = -(-KT // 4)


def attention_order(adapt, last):
    v = [("v", t) for t in range(KT)]
    k = [] if last else [("k",) + g for g in K_GROUPS]
    order = []
    for p, before in enumerate((2, 1, 1, 1, 1, 2, 1, 1) if adapt else (3, 3, 2, 2)):
        order += v[:before] + [("s", p)]
        del v[:before]
    order += v

    def next_k(n=1):
        order.extend(k[:n])
        del k[:n]

    if adapt:
        for step, n in (("mean", 1), ("feat", 1), ("h1", 1), ("h2", 1), ("t", 1), ("spread", 2)):
            order.append((step,))
            next_k(n)
    order.extend([("t", 0, 0), ("t", 0, 1)])
    for p in range(PAIRS):
        if not adapt and p >= PAIRS // 2:
            next_k(2)
        elif not adapt:
            order.append(("s", p + PAIRS // 2, 0))
        order.extend([("w", p, 0), ("t", p, 2), ("w", p, 1), ("t", p, 3)])
        if adapt:
            next_k(int(p < PAIRS - 2))
        elif p >= PAIRS // 2:
            next_k(1)
        else:
            order.append(("s", p + PAIRS // 2, 1))
        order.append(("w", p, 2))
        if p < PAIRS - 1:
            order.append(("t", p + 1, 0))
        order.append(("w", p, 3))
        if p < PAIRS - 1:
            order.append(("t", p + 1, 1))
    behind = 0 if adapt or last else 1
    next_k(len(k) - behind)
    order.append(("o",))
    next_k(behind)
    return order


def even(n):
    return n + n % 2


def scores_end(item):
    return item[0] == "s" and (len(item) == 2 or item[2] == 1)


class Round:

    def __init__(self, order, adapt):
        self.order = order
        self.uses = [i for i in order if (i[0] in "kvo") or (i[0] == "t" and len(i) == 3)]
        self.by, self.nth, self.count = [], [], {"act": 0, "dve": 0}
        for i in self.uses:
            if i[0] == "k":
                by = "act" if adapt else "dve"
            elif i[0] == "t" and adapt:
                by = ("dve", "act")[(i[1] + i[2]) % 2]
            elif i[0] == "t":
                by = "act" if (i[1], i[2]) >= (PAIRS // 2, 2) else "dve"
            else:
                by = "dve"
            self.count[by] += 1
            self.by.append(by)
            self.nth.append(self.count[by])
        self.at = {i: n for n, i in enumerate(self.uses)}


def cross_attention(nc, tag, const, x, oT, ctx_dram, wq_dram, wk_dram, wv_dram, mask_dram=None, adapt=None):
    scale = float(DH) ** -0.5
    with Scope(nc, tag) as sc:
        sem = sc.sem
        ctx = [split_buffer(sc, f"ctx{s}", [P, DC, CW + CW % 2]) for s in range(NSLOT)]
        wk = split_buffer(sc, "wk", [P, DC, D])
        wv = split_buffer(sc, "wv", [P, DC, D])
        if adapt:
            kT = sc.sb("kT", [P, DC, KEYS])
            qbd = sc.sb("qbd", [P, PAIRS, P])
        else:
            kst = sc.sb("kst", [P, PAIRS, KEYS + KEYS % 2], F32R)
            q_hi, q_lo = sc.sb("q_hi", [P, PAIRS, P], F32R), sc.sb("q_lo", [P, PAIRS, P], F32R)
        vk = sc.sb("vk", [P, KT, D])
        NSB = PAIRS if adapt else PAIRS // 2
        sco = sc.sb("sco", [P, NSB, KEYS])
        wT = sc.sb("wT", [P, 2, 4, P])
        lent = Lent(sco[:, :, :].rearrange("p b n -> p (b n)"))
        u, uT, wq = lent("u", [P, TT, D]), lent("uT", [P, DC, T]), lent("wq", [P, DC, D])
        norm_x = Norm(sc, "n", x, u, uT, const[:, C_IDENT:C_IDENT + P], lent)
        qT = oT
        mx, nmx, rsum, rinv = (sc.sb(n, [P, PAIRS]) for n in ("mx", "nmx", "rsum", "rinv"))
        onorm = sc.sb("onorm", [P, D])
        ps_s = sc.ps("ps_s", [P, 4 * 512])
        ring = [sc.ps(f"ring{i}", [P, 512]) for i in range(2)]
        ps_o = sc.ps("ps_o", [P, 2, 512])
        ps_m = ps_o[:, 1, :]
        if mask_dram is not None:
            mask = sc.sb("mask", [P, KEYS])
        if adapt:
            p1 = sc.sb("p1", [P, KEYS])
            bq = lent("bq", [P, DC])
            bk, bv = sc.sb("bk", [P, DC]), sc.sb("bv", [P, DC])
            w1T, w2T, w3T = sc.sb("w1T", [3, 64]), sc.sb("w2T", [64, 64]), sc.sb("w3T", [64, 1])
            b12, b3 = sc.sb("b12", [64, 2]), sc.sb("b3", [1, 1])
            kparts = sc.sb("kparts", [P, DC, NCHUNK])
            ksum = sc.sb("ksum", [P, DC])
            stats = sc.sb("stats", [P, PAIRS, 3])
            sums = sc.sb("sums", [P, PAIRS, 2])
            tmp, temp = sc.sb("tmp", [P, PAIRS]), sc.sb("temp", [P, PAIRS])
            featT = sc.sb("featT", [3, H])
            hid = sc.sb("hid", [64, 2, H])
            logt, invt = sc.sb("logt", [1, H]), sc.sb("invt", [1, H])

        w_in = [sem(f"w_in{s}") for s in range(2)]
        small_in, w_hi_ready, w_split = (sem(n) for n in ("small_in", "w_hi_ready", "w_split"))
        ctx_in = [sem(f"ctx_in{s}") for s in range(NSLOT)]
        ctx_hi_ready = sem("ctx_hi")
        ctx_split = sem("ctx_split")
        wq_in = sem("wq_in")
        q_done = sem("q_done")
        q_out = sem("q_out")
        first_k = sem("first_k")
        first_evac = sem("first_evac")
        k_hi = sem("k_hi")
        group = sem("group")
        act_evac = sem("act_evac")
        dve_evac = sem("dve_evac")
        q_ready = sem("q_ready")
        scored = sem("scored")
        taken = sem("taken")
        negated = sem("negated")
        probs = sem("probs")
        pv = sem("pv")
        normed = sem("normed")
        o_ready = sem("o_ready")
        mask_in = sem("mask_in")
        dve_step = sem("dve_step")
        pool_mark, pe_mark, dve_mark = sem("pool_mark"), sem("pe_mark"), sem("dve_mark")
        if adapt:
            (squared, plain, ksum_ready, mean_done, stats_ready, feat_done, feat_ready, h1_done, h1_ready, h2_done,
             h2_ready, t_done, t_clip, t_ready, spread, temp_ready) = (sem(n) for n in (
                "squared", "plain", "ksum_ready", "mean_done", "stats_ready", "feat_done", "feat_ready", "h1_done",
                "h1_ready", "h2_done", "h2_ready", "t_done", "t_clip", "t_ready", "spread", "temp_ready"))

        full, final = (Round(attention_order(adapt, last), adapt) for last in (False, True))
        PER = len(full.uses)
        assert PER % 2 == 0, "a round has to keep the banks' parity"
        evac_sem = {"act": act_evac, "dve": dve_evac}
        CHUNKS = 2 * NCHUNK
        last_v = [max(u for i, u in full.at.items() if i[0] == "v" and CHUNK_OF[i[1]] == n) for n in range(NCHUNK)]
        k_through = [max(j for j, g in enumerate(K_GROUPS) if g[0] == n) for n in range(NCHUNK)]
        last_k = [full.at[("k",) + K_GROUPS[j]] for j in k_through]
        through = last_v + last_k

        def emptied(eng, b, r, u):
            if u < 0:
                u += PER
                by = full.by[u]
                eng.wait_ge(evac_sem[by], b * full.count[by] + full.nth[u])
            else:
                by = r.by[u]
                eng.wait_ge(evac_sem[by], b * full.count[by] + (full.count[by] + r.nth[u]))

        def filled(eng, b, u):
            eng.wait_ge(group, b * PER + (PER + u + 1))

        def rounds(eng, body):
            with eng.Fori(0, B - 1) as b:
                body(b, full)
            body(B - 1, final)

        with nc.Block() as block:
            @block.sync
            def _(sp):
                def load(s, b, n):
                    sp.dma_start(ctx[s][2][:, :, 0:CHUNK_KEYS[n]],
                                 ctx_dram[bass.ds(b, 1), :, CHUNK_AT[n]:CHUNK_AT[n] + CHUNK_KEYS[n]].rearrange("o (k p) n -> p (o k) n", p=P)
                                 ).then_inc(ctx_in[s], 16)

                def load_weights(s, w, src):
                    sp.dma_start(w[2][:, :, :], src.rearrange("(k p) n -> p k n", p=P)).then_inc(w_in[s], 16)

                sp.dma_start(wq, chunks(wq_dram)).then_inc(wq_in, 16)
                load_weights(0, wk, wk_dram)
                load(0, 0, 0)
                if adapt:
                    sp.dma_start(bq, adapt["L1_bqT"]).then_inc(wq_in, 16)
                    for dst, src in ((bk, "bk"), (bv, "bv"), (w1T, "w1T"), (w2T, "w2T"), (w3T, "w3T"), (b12, "b12"), (b3, "b3")):
                        sp.dma_start(dst[:, :], adapt[src]).then_inc(small_in, 16)
                for n in range(1, NSLOT):
                    load(n, 0, n)
                load_weights(1, wv, wv_dram)
                for n in range(NSLOT, NCHUNK + NSLOT):
                    sp.wait_ge(first_k, k_through[n - NSLOT] + 1)
                    load(n % NSLOT, 0, n % NCHUNK)

                def body(b, r):
                    if mask_dram is not None:
                        sp.wait_ge(taken, b * PAIRS + 1)
                        sp.dma_start(mask[:, :].bitcast(I32), mask_dram[bass.ds(b, 1), :].to_broadcast([P, KEYS])).then_inc(mask_in, 16)
                    for i in range(NSLOT, CHUNKS + NSLOT if r is full else NCHUNK):
                        filled(sp, b, through[i - NSLOT])
                        load(i % NSLOT, b + int(i >= NCHUNK), i % NCHUNK)

                rounds(sp, body)

            @block.gpsimd
            def _(g):
                def split(s, n, arrived, at):
                    hi, lo, raw = ctx[s]
                    w = CHUNK_KEYS[n]
                    g.wait_ge(ctx_in[s], arrived)
                    g.sem_inc(pool_mark, 1)
                    g.tensor_copy(hi[:, :, 0:w], raw[:, :, 0:w]).then_inc(ctx_hi_ready, 1)
                    g.wait_ge(ctx_hi_ready, at)
                    g.tensor_tensor(lo[:, :, 0:w], raw[:, :, 0:w], hi[:, :, 0:w].bitcast(F32), ALU.subtract).then_inc(ctx_split, 1)

                for n in range(NCHUNK):
                    split(n % NSLOT, n, 16 * (n // NSLOT + 1), n + 1)

                def body(b, r):
                    for i in range(CHUNKS if r is full else NCHUNK):
                        split(i % NSLOT, i % NCHUNK, b * (16 * CHUNKS // NSLOT) + 16 * (NCHUNK // NSLOT + i // NSLOT + 1),
                              b * CHUNKS + (NCHUNK + i + 1))

                rounds(g, body)

            @block.tensor
            def _(pe):
                def project_k(bank, s, n, c0, m):
                    w = even(CHUNK_KEYS[n])
                    for j in range(m):
                        c = c0 + j
                        ins = split_product(pe, bank[:, j * w:(j + 1) * w],
                                            lambda k: wk[0][:, k, c * P:(c + 1) * P], lambda k: wk[1][:, k, c * P:(c + 1) * P],
                                            lambda k: ctx[s][0][:, k, 0:w], lambda k: ctx[s][1][:, k, 0:w], DC)
                    return ins

                banks = [ps_s[:, n * 512:(n + 1) * 512] for n in range(4)]
                norm_x.pe_turn(pe, banks)
                pe.wait_ge(norm_x.uT_ready, TT)
                pe.wait_ge(wq_in, 32 if adapt else 16)
                for c in range(DC):
                    product(pe, banks[c], lambda k: wq[:, k, c * P:(c + 1) * P], lambda k: uT[:, k, :], DC).then_inc(q_done, 1)
                pe.wait_ge(w_split, 1)
                for j, (n, c, m) in enumerate(K_GROUPS):
                    pe.wait_ge(ctx_split, n + 1)
                    if j >= 2:
                        pe.wait_ge(first_evac, j - 1)
                    project_k(ring[j % 2], n % NSLOT, n, c, m).then_inc(first_k, 1)
                pe.sem_inc(group, PER)
                pe.wait_ge(first_evac, len(K_GROUPS))
                pe.wait_ge(q_out, DC)
                pe.wait_ge(w_split, 2)
                if adapt:
                    pe.wait_ge(small_in, 16 * 7)

                def body(b, r):
                    def claim(item):
                        u = r.at[item]
                        emptied(pe, b, r, u - 2)
                        return ring[u % 2]

                    for item in r.order:
                        what, i = item[0], item[1:]
                        if what == "v":
                            t, n = i[0], CHUNK_OF[i[0]]
                            o, m, s = t * KW - CHUNK_AT[n], TILE_KEYS[t], n % NSLOT
                            if o == 0:
                                pe.wait_ge(ctx_split, b * CHUNKS + (NCHUNK + n + 1))
                            split_product(pe, claim(item)[0:m, :],
                                          lambda k: ctx[s][0][:, k, o:o + m], lambda k: ctx[s][1][:, k, o:o + m],
                                          lambda k: wv[0][:, k, :], lambda k: wv[1][:, k, :], DC).then_inc(group, 1)
                        elif what == "k":
                            n, c, m = i
                            if c == 0:
                                pe.wait_ge(ctx_split, b * CHUNKS + (2 * NCHUNK + n + 1))
                            if adapt and n == 0 and c == 0:
                                pe.wait_ge(ksum_ready, b + 1)
                            project_k(claim(item), (NCHUNK + n) % NSLOT, n, c, m).then_inc(group, 1)
                        elif what == "s":
                            p = i[0]
                            if p == 0:
                                pe.wait_ge(q_ready, b + 1)
                                emptied(pe, b, r, last_k[-1] - PER)
                            pe.wait_ge(taken, b * PAIRS + (p + 1))
                            for n in (range(4) if len(i) == 1 else range(2 * i[1], 2 * i[1] + 2)):
                                w = SCORE_KEYS[n]
                                if adapt:
                                    ins = pe.matmul(ps_s[:, n * 512:n * 512 + w], qbd[:, p, :],
                                                    kT[:, p // 2, n * 512:n * 512 + w], start=True, stop=True)
                                else:
                                    w += w % 2
                                    pe.matmul(ps_s[:, n * 512:n * 512 + w], q_hi[:, p, :], kst[:, p, n * 512:n * 512 + w],
                                              start=True, stop=False)
                                    ins = pe.matmul(ps_s[:, n * 512:n * 512 + w], q_lo[:, p, :],
                                                    kst[:, p, n * 512:n * 512 + w], start=False, stop=True)
                            if scores_end(item):
                                ins.then_inc(scored, 1)
                        elif what == "t" and i:
                            p, g = i
                            if g == 0:
                                pe.wait_ge(probs, b * PAIRS + (p + 1))
                            bank = claim(item)
                            for j in range(4 * g, min(KT, 4 * g + 4)):
                                m = TILE_KEYS[j]
                                ins = pe.transpose(bank[0:m, (j % 4) * P:(j % 4) * P + P],
                                                   sco[:, p % NSB, j * KW:j * KW + m], const[:, C_IDENT:C_IDENT + P])
                            ins.then_inc(group, 1)
                        elif what == "w":
                            p, g = i
                            emptied(pe, b, r, r.at[("t", p, g)])
                            if p == 0 and g == 0:
                                emptied(pe, b, r, r.at[("v", KT - 1)])
                            if g == 0:
                                pe.wait_ge(normed, b * PAIRS + (p + PAIRS - 1))
                            for j in range(4 * g, min(KT, 4 * g + 4)):
                                m = TILE_KEYS[j]
                                ins = pe.matmul(ps_o[:, p % 2, 0:P], wT[0:m, g % 2, j % 4, :], vk[0:m, j, P * (p // 2):P * (p // 2) + P],
                                                start=(j == 0), stop=(j == KT - 1), skip_group_check=True)
                            if g == QUADS - 1:
                                ins.then_inc(pv, 1)
                        elif what == "o":
                            bank = claim(item)
                            pe.wait_ge(o_ready, b + 1)
                            for c in range(DC):
                                ins = pe.matmul(bank[:, c * S:(c + 1) * S], onorm[:, c * P:(c + 1) * P],
                                                const[:, C_STACK:C_STACK + S], start=True, stop=True)
                            ins.then_inc(group, 1)
                        elif what == "mean":
                            pe.wait_ge(ksum_ready, b + 1)
                            for p in range(PAIRS):
                                ins = pe.matmul(ps_m[:, p:p + 1], qbd[:, p, :], ksum[:, p // 2:p // 2 + 1], start=True, stop=True)
                            ins.then_inc(mean_done, 1)
                        elif what == "feat":
                            pe.wait_ge(stats_ready, b + 1)
                            for p in range(PAIRS):
                                ins = pe.matmul(ps_m[0:3, 16 + 2 * p:18 + 2 * p], stats[:, p, :], const[:, C_HALF:C_HALF + 2], start=True, stop=True)
                            ins.then_inc(feat_done, 1)
                        elif what == "h1":
                            pe.wait_ge(feat_ready, b + 1)
                            pe.matmul(ps_m[0:64, 32:48], w1T[:, :], featT[:, :], start=True, stop=True).then_inc(h1_done, 1)
                        elif what == "h2":
                            pe.wait_ge(h1_ready, b + 1)
                            pe.sem_inc(pe_mark, 1)
                            pe.matmul(ps_m[0:64, 48:64], w2T[:, :], hid[:, 0, :], start=True, stop=True).then_inc(h2_done, 1)
                        elif what == "t":
                            pe.wait_ge(h2_ready, b + 1)
                            pe.sem_inc(pe_mark, 1)
                            pe.matmul(ps_m[0:1, 64:80], w3T[:, :], hid[:, 1, :], start=True, stop=True).then_inc(t_done, 1)
                        elif what == "spread":
                            pe.wait_ge(t_ready, b + 1)
                            iv = invt[0:1, :].rearrange("o (p e) -> o e p", e=2)
                            pe.matmul(ps_m[:, 80:88], const[0:1, C_TOP:C_TOP + P], iv[:, 0, :], start=True, stop=False)
                            pe.matmul(ps_m[:, 80:88], const[0:1, C_BOT:C_BOT + P], iv[:, 1, :], start=False, stop=True).then_inc(spread, 1)

                rounds(pe, body)

            def turned_views(g, bank):
                if 4 * g + 4 <= KT:
                    return wT[0:KW, g % 2, :, :].rearrange("p j n -> p (j n)"), bank[0:KW, :]
                assert KT % 4 == 1
                return wT[0:TILE_KEYS[-1], g % 2, 0, :], bank[0:TILE_KEYS[-1], 0:P]

            @block.scalar
            def _(a):
                a.sem_inc(act_evac, full.count["act"])
                norm_x.act_root(a)
                def split_weights(s, w):
                    a.wait_ge(w_in[s], 16)
                    a.activation(w[0][:, :, :], w[2][:, :, :], ACT.Copy).then_inc(w_hi_ready, 1)

                split_weights(0, wk)
                if adapt:
                    a.wait_ge(small_in, 16 * 7)

                def take_k(evacuated, bank, n, c0, m):
                    w = CHUNK_KEYS[n]
                    we = even(w)
                    if adapt:
                        for j in range(m):
                            c = c0 + j
                            ins = a.activation(kT[:, c, CHUNK_AT[n]:CHUNK_AT[n] + w], bank[:, j * we:j * we + w], ACT.Identity,
                                               bias=bk[:, c:c + 1], accum_out=kparts[:, c, n:n + 1])
                        ins.then_inc(evacuated, 1)
                        return
                    for half in range(2):
                        rows = slice(half * S, half * S + S)
                        ins = a.activation(kst[rows, 2 * c0 + half:2 * (c0 + m):2, CHUNK_AT[n]:CHUNK_AT[n] + we],
                                           bank[rows, 0:m * we].rearrange("p (j n) -> p j n", j=m), ACT.Copy)
                        ins.then_inc(k_hi, 1)

                split_weights(1, wv)
                if adapt:
                    a.wait_ge(wq_in, 32)
                for c in range(DC):
                    a.wait_ge(q_done, c + 1)
                    bank = ps_s[:, c * 512:(c + 1) * 512]
                    if adapt:
                        a.activation(qT[:, c, :], bank, ACT.Identity, bias=bq[:, c:c + 1]).then_inc(q_out, 1)
                    else:
                        a.activation(qT[:, c, :], bank, ACT.Copy).then_inc(q_out, 1)
                for j, (n, c, m) in enumerate(K_GROUPS):
                    a.wait_ge(first_k, j + 1)
                    take_k(first_evac, ring[j % 2], n, c, m)

                def body(b, r):
                    def weights(p):
                        row = sco[:, p % NSB, :]
                        a.activation(row, row, ACT.Exp, bias=nmx[:, p:p + 1], scale=temp[:, p:p + 1] if adapt else scale,
                                     accum_out=rsum[:, p:p + 1]).then_inc(probs, 1)

                    for item in r.order:
                        what, i = item[0], item[1:]
                        if scores_end(item):
                            p = i[0]
                            a.wait_ge(negated, b * PAIRS + (p + 1))
                            if adapt:
                                a.wait_ge(squared, b * PAIRS + (p + 1))
                                a.activation(p1[:, :], sco[:, p % NSB, :], ACT.Exp, bias=nmx[:, p:p + 1], scale=scale,
                                             accum_out=sums[:, p, 0:1]).then_inc(plain, 1)
                            else:
                                weights(p)
                        elif what == "h1":
                            a.wait_ge(h1_done, b + 1)
                            a.activation(hid[:, 0, :], ps_m[0:64, 32:48], ACT.Gelu, bias=b12[:, 0:1]).then_inc(h1_ready, 1)
                        elif what == "h2":
                            a.wait_ge(h2_done, b + 1)
                            a.activation(hid[:, 1, :], ps_m[0:64, 48:64], ACT.Gelu, bias=b12[:, 1:2]).then_inc(h2_ready, 1)
                        elif what == "t" and not i:
                            a.wait_ge(t_clip, b + 1)
                            a.activation(invt[:, :], logt[:, :], ACT.Exp, scale=-1.0).then_inc(t_ready, 1)
                        elif what == "spread":
                            a.wait_ge(temp_ready, b + 1)
                            weights(0)
                        elif what == "k":
                            filled(a, b, r.at[item])
                            take_k(act_evac, ring[r.at[item] % 2], *i)
                        elif what == "t" and r.by[r.at[item]] == "act":
                            filled(a, b, r.at[item])
                            dst, src = turned_views(i[1], ring[r.at[item] % 2])
                            a.activation(dst, src, ACT.Copy).then_inc(act_evac, 1)
                        elif what == "w" and i[1] == 0 and adapt and i[0] + 1 < PAIRS:
                            weights(i[0] + 1)

                rounds(a, body)

            @block.vector
            def _(v):
                ch = Chain(v, dve_step)
                v.sem_inc(dve_evac, full.count["dve"])
                v.sem_inc(taken, 1)
                if adapt:
                    v.sem_inc(squared, 1)
                v.sem_inc(normed, PAIRS)
                norm_x.dve_var(ch)
                norm_x.dve_u(ch)

                def split_weights(s, w):
                    v.wait_ge(w_hi_ready, s + 1)
                    v.tensor_tensor(w[1][:, :, :], w[2][:, :, :], w[0][:, :, :].bitcast(F32), ALU.subtract).then_inc(w_split, 1)

                def take_k_low(b, j, bank, n, c0, m):
                    w = even(CHUNK_KEYS[n])
                    for half in range(2):
                        rows, other = slice(half * S, half * S + S), slice((1 - half) * S, (2 - half) * S)
                        v.wait_ge(k_hi, b * (2 * len(K_GROUPS)) + (2 * j + half + 1))
                        at, pairs = slice(CHUNK_AT[n], CHUNK_AT[n] + w), slice(2 * c0 + half, 2 * (c0 + m), 2)
                        ins = v.tensor_tensor(kst[other, pairs, at], bank[rows, 0:m * w].rearrange("p (j n) -> p j n", j=m),
                                              kst[rows, pairs, at].bitcast(F32), ALU.subtract)
                    return ins

                split_weights(0, wk)
                norm_x.evac(v, [ps_s[:, n * 512:(n + 1) * 512] for n in range(4)], v.tensor_copy)
                split_weights(1, wv)
                if not adapt:
                    for j, (n, c, m) in enumerate(K_GROUPS):
                        take_k_low(0, j, ring[j % 2], n, c, m).then_inc(first_evac, 1)
                v.wait_ge(first_evac, len(K_GROUPS))
                v.wait_ge(q_out, DC)

                def body(b, r):
                    def square(p):
                        v.wait_ge(plain, b * PAIRS + (p + 1))
                        v.tensor_tensor_reduce(p1[:, :], p1[:, :], p1[:, :], 1.0, 0.0, ALU.mult, ALU.add,
                                               sums[:, p, 1:2]).then_inc(squared, 1)

                    def norm(p):
                        v.wait_ge(pv, b * PAIRS + (p + 1))
                        ch.link(v.reciprocal(rinv[:, p:p + 1], rsum[:, p:p + 1]))
                        v.tensor_scalar(onorm[:, 64 * p:64 * p + 64], ps_o[:, p % 2, 64 * (p % 2):64 * (p % 2) + 64],
                                        rinv[:, p:p + 1], None, ALU.mult).then_inc(normed, 1)

                    if adapt:
                        for p in range(PAIRS):
                            for e in range(2):
                                h = 2 * (p % 2) + e
                                ins = v.tensor_scalar(qbd[:, p, e * S:(e + 1) * S], qT[:, p // 2, bass.ds(b * S, S)],
                                                      const[:, C_HEAD + h:C_HEAD + h + 1], None, ALU.mult)
                        ins.then_inc(q_ready, 1)
                    else:
                        both = wT[:, :, :, :].rearrange("p a j n -> p (a j) n")
                        for half in range(2):
                            rows = slice(half * S, half * S + S)
                            for e in range(2):
                                h = 2 * half + e
                                for to in range(2):
                                    ch.inc(v.tensor_scalar(both[to * S:to * S + S, half::2, e * S:(e + 1) * S],
                                                           qT[rows, :, bass.ds(b * S, S)],
                                                           const[rows, C_HEAD + h:C_HEAD + h + 1], None, ALU.mult))
                        ch.wait()
                        ch.link(v.tensor_copy(q_hi[:, :, :], both))
                        v.tensor_tensor(q_lo[:, :, :], both, q_hi[:, :, :].bitcast(F32), ALU.subtract).then_inc(q_ready, 1)
                    if mask_dram is not None:
                        v.wait_ge(mask_in, b * 16 + 16)
                        ch.link(v.tensor_scalar(mask[:, :], mask[:, :].bitcast(I32), 0.0, NEG, ALU.is_equal, ALU.mult))
                    if adapt:
                        emptied(v, b, r, last_k[-1] - PER)
                        v.tensor_reduce(ksum[:, :], kparts[:, :, :], AX.X, ALU.add).then_inc(ksum_ready, 1)

                    for item in r.order:
                        what, i = item[0], item[1:]
                        if what == "v":
                            t, u = i[0], r.at[item]
                            filled(v, b, u)
                            v.tensor_copy(vk[0:TILE_KEYS[t], t, :], ring[u % 2][0:TILE_KEYS[t], :]).then_inc(dve_evac, 1)
                        elif scores_end(item):
                            p = i[0]
                            v.wait_ge(scored, b * PAIRS + (p + 1))
                            if mask_dram is not None:
                                v.sem_inc(dve_mark, 1)
                                v.tensor_tensor_reduce(sco[:, p % NSB, :], ps_s[:, 0:KEYS], mask[:, :], 1.0, -BIG,
                                                       ALU.add, ALU.max, mx[:, p:p + 1]).then_inc(taken, 1)
                            else:
                                v.tensor_scalar(sco[:, p % NSB, :], ps_s[:, 0:KEYS], 1.0, -BIG, ALU.mult, ALU.max,
                                                accum_out=mx[:, p:p + 1]).then_inc(taken, 1)
                            v.wait_ge(taken, b * PAIRS + (p + 2))
                            v.tensor_scalar(nmx[:, p:p + 1], mx[:, p:p + 1], -scale, None, ALU.mult).then_inc(negated, 1)
                            if adapt and p:
                                square(p - 1)
                        elif what == "mean":
                            square(PAIRS - 1)
                            v.wait_ge(squared, b * PAIRS + (PAIRS + 1))
                            ch.link(v.reciprocal(rinv[:, :], sums[:, :, 0]))
                            ch.link(v.tensor_tensor(tmp[:, :], rinv[:, :], rinv[:, :], ALU.mult))
                            ch.link(v.tensor_tensor(tmp[:, :], tmp[:, :], sums[:, :, 1], ALU.mult))
                            v.tensor_scalar(stats[:, :, 1], mx[:, :], scale, None, ALU.mult)
                            v.tensor_scalar(stats[:, :, 2], tmp[:, :], -1.0 / KEYS, 1.0 / (KEYS - 1), ALU.add, ALU.mult)
                            v.wait_ge(mean_done, b + 1)
                            v.tensor_scalar(stats[:, :, 0], ps_m[:, 0:PAIRS], scale / KEYS, None, ALU.mult).then_inc(stats_ready, 1)
                        elif what == "feat":
                            v.wait_ge(feat_done, b + 1)
                            v.tensor_copy(featT[:, :], ps_m[0:3, 16:32]).then_inc(feat_ready, 1)
                        elif what == "k" and not adapt:
                            take_k_low(b, len(K_GROUPS) + K_GROUPS.index(i), ring[r.at[item] % 2], *i).then_inc(dve_evac, 1)
                        elif what == "t" and not i:
                            v.wait_ge(t_done, b + 1)
                            ch.link(v.tensor_scalar(logt[:, :], ps_m[0:1, 64:80], b3[:, 0:1], LOG_T_MAX, ALU.add, ALU.min))
                            v.tensor_scalar(logt[:, :], logt[:, :], LOG_T_MIN, None, ALU.max).then_inc(t_clip, 1)
                        elif what == "spread":
                            v.wait_ge(spread, b + 1)
                            ch.link(v.tensor_scalar(temp[:, :], ps_m[:, 80:88], 0.5, None, ALU.mult))
                            ch.link(v.tensor_tensor(nmx[:, :], mx[:, :], temp[:, :], ALU.mult))
                            v.tensor_scalar(nmx[:, :], nmx[:, :], -1.0, None, ALU.mult).then_inc(temp_ready, 1)
                        elif what == "t" and r.by[r.at[item]] == "dve":
                            filled(v, b, r.at[item])
                            v.tensor_copy(*turned_views(i[1], ring[r.at[item] % 2])).then_inc(dve_evac, 1)
                        elif what == "w" and i[1] == 1 and i[0]:
                            norm(i[0] - 1)
                        elif item == ("w", PAIRS - 1, QUADS - 1):
                            norm(PAIRS - 1)
                            v.wait_ge(normed, b * PAIRS + 2 * PAIRS)
                            own = const[:, C_DIAG:C_DIAG + 2 * DH].unsqueeze(1).to_broadcast([P, PAIRS, 2 * DH])
                            split = onorm[:, :].rearrange("p (j n) -> p j n", n=2 * DH)
                            v.tensor_tensor(split, split, own, ALU.mult).then_inc(o_ready, 1)
                        elif what == "o":
                            filled(v, b, r.at[item])
                            v.sem_inc(dve_mark, 1)
                            v.tensor_copy(qT[:, :, bass.ds(b * S, S)],
                                          ring[r.at[item] % 2][:, 0:DC * S].rearrange("p (c n) -> p c n", c=DC)).then_inc(dve_evac, 1)

                PER_STEPS = PAIRS + (6 if adapt else 10)
                with v.Fori(0, B - 1) as b:
                    ch.loop(b, PER_STEPS)
                    body(b, full)
                ch.end(B - 1)
                body(B - 1, final)
                if adapt:
                    v.wait_ge(small_in, 16 * 7)
                    v.wait_ge(dve_evac, B * full.count["dve"] + final.count["dve"])
                    for c in range(DC):
                        v.tensor_scalar(qT[:, c, :], qT[:, c, :], bv[:, c:c + 1], None, ALU.add)


def output_stage(nc, tag, x, aT, ahead, wo_dram, bo_dram=None):
    with Scope(nc, tag) as sc:
        wo = sc.sb("wo", [P, DC, D])
        bo = sc.sb("bo", [P, D])
        banks = [sc.ps(f"b{i}", [P, 512]) for i in range(TT)]
        w_in, done, added, step = (sc.sem(n) for n in ("w_in", "done", "added", "step"))
        with nc.Block() as block:
            @block.sync
            def _(sp):
                sp.dma_start(wo[:, :, :], wo_dram.rearrange("(k p) n -> p k n", p=P)).then_inc(w_in, 16)
                if bo_dram is not None:
                    sp.dma_start(bo[:, :], bo_dram.to_broadcast([P, D])).then_inc(w_in, 16)
                ahead.load(sp)

            @block.tensor
            def _(pe):
                pe.wait_ge(w_in, 16 if bo_dram is None else 32)
                for t in range(TT):
                    product(pe, banks[t][:, :], lambda k: aT[:, k, t * P:(t + 1) * P], lambda k: wo[:, k, :], DC).then_inc(done, 1)

            @block.vector
            def _(v):
                ch = Chain(v, step)
                if bo_dram is not None:
                    v.wait_ge(w_in, 32)
                    for t in range(TT):
                        ch.inc(v.tensor_tensor(x[:, t, :], x[:, t, :], bo[:, :], ALU.add))
                    ch.wait()
                for t in range(TT):
                    v.wait_ge(done, t + 1)
                    v.tensor_tensor(x[:, t, :], x[:, t, :], banks[t][:, :], ALU.add)


def store(nc, out_dram, x):
    with Scope(nc, "st") as sc:
        done = sc.sem("done")
        with nc.Block() as block:
            @block.sync
            def _(sp):
                sp.dma_start(out_dram.rearrange("(i e) t d -> (e t) i d", e=BT), x[:, :, :]).then_inc(done, 16)
                sp.wait_ge(done, 16)


def mixer_weights(sc, a):
    return Weights(sc, [
        ("big_in", "gain", [P, D], a["ln_g"].to_broadcast([P, D])),
        ("big_in", "shift", [P, D], a["ln_b"].to_broadcast([P, D])),
        ("big_in", "w_in", [P, DC, 2 * D], chunks(a["W_inT"])),
        ("big_in", "w_out", [P, DC, D], chunks(a["W_outT"])),
    ])


def mixer_stage(nc, const, x, a, weights, ahead):
    with Scope(nc, "mx") as sc:
        sb, sem = sc.sb, sc.sem
        u, xn = sb("u", [P, TT, D]), sb("xn", [P, TT, D])
        xnT = sb("xnT", [P, DC, T])
        xp, z = sb("xp", [P, DC, T]), sb("z", [P, DC, T])
        w_in, w_out, gain, shift = (weights.buf[n] for n in ("w_in", "w_out", "gain", "shift"))
        b_out = sb("b_out", [P, D])
        wc = sb("wc", [P, D])
        W_PAD = (B - 1) * NS
        wb = sb("wb", [P, DC, 2 * W_PAD + NS])
        b_in, d_skip, dt = sb("b_in", [P, 2 * DC]), sb("d_skip", [P, DC]), sb("dt", [P, DC])
        la = sb("la", [P, DC, NS])
        ea = sb("ea", [P, DC, NS])
        ex = sb("ex", [P, DC, NS * S])
        amean = sb("amean", [P, S])
        sel = sb("sel", [P, NS, S])
        dtm = sb("dtm", [P, 1])
        bp = sb("bp", [P, 2 * S - 1])
        conv = sb("conv", [P, S, S])
        xm = sb("xm", [P, S])
        xmx = sb("xmx", [P, B, S])
        y = sb("y", [P, DC, T])
        bank = [sc.ps(f"b{i}", [P, 512]) for i in range(8)]
        outer = Norm(sc, "no", x, u, None, None)
        inner = Norm(sc, "ni", u, xn, xnT, const[:, C_IDENT:C_IDENT + P])
        (small_in, dt_exp, al_ready, ea_ready, tl_ready, ex_ready, dt_ready, a_sum, xz_done, xp_ready,
         z_ready, wb_ready, b_done, xm_ready, y_sum, y_ready, out_done, step) = (sem(n) for n in (
            "small_in", "dt_exp", "al_ready", "ea_ready", "tl_ready", "ex_ready", "dt_ready", "a_sum",
            "xz_done", "xp_ready", "z_ready", "wb_ready", "b_done", "xm_ready", "y_sum", "y_ready", "out_done", "step"))
        wb_in = sem("wb_in")
        SMALL = 5 + B
        with nc.Block() as block:
            @block.sync
            def _(sp):
                sp.dma_start(la[:, :, :], a["A_log"].rearrange("(k p) s -> p k s", p=P)).then_inc(small_in, 16)
                for dst, src in ((dt, "log_dt"), (d_skip, "D_skip"), (b_in, "b_in")):
                    sp.dma_start(dst[:, :], a[src]).then_inc(small_in, 16)
                for b in range(B):
                    sp.dma_start(wc[b * NS:(b + 1) * NS, :], a["W_CT"]).then_inc(small_in, 16)
                sp.dma_start(b_out[:, :], a["b_out"].to_broadcast([P, D])).then_inc(small_in, 16)
                sp.wait_ge(wb_ready, 1)
                sp.dma_start(wb[:, :, W_PAD:W_PAD + NS], a["W_BT"].rearrange("(k p) s -> p k s", p=P)).then_inc(wb_in, 16)
                ahead.load(sp)

            @block.gpsimd
            def _(g):
                g.memset(bp[:, 0:S - 1], 0.0)
                g.memset(wb[:, :, :], 0.0).then_inc(wb_ready, 1)

            @block.scalar
            def _(s):
                outer.act_root(s)
                inner.act_root(s)
                s.wait_ge(small_in, 16 * SMALL)
                s.activation(dt[:, :], dt[:, :], ACT.Exp).then_inc(dt_exp, 1)
                s.wait_ge(al_ready, 1)
                s.activation(ea[:, :, :], la[:, :, :], ACT.Exp).then_inc(ea_ready, 1)
                for k in range(DC):
                    s.wait_ge(tl_ready, k + 1)
                    s.activation(ex[:, k, :], ex[:, k, :], ACT.Exp).then_inc(ex_ready, 1)
                for g in range(DC):
                    s.wait_ge(xz_done, g + 1)
                    s.activation(xp[:, g, :], bank[g][:, :], ACT.Identity, bias=b_in[:, g:g + 1]).then_inc(xp_ready, 1)
                for g in range(DC, 2 * DC):
                    s.wait_ge(xz_done, g + 1)
                    s.activation(z[:, g - DC, :], bank[g - DC][:, :], ACT.Silu, bias=b_in[:, g:g + 1]).then_inc(z_ready, 1)

            @block.tensor
            def _(pe):
                inner.pe_turn(pe, bank)
                pe.wait_ge(inner.uT_ready, TT)
                weights.wait(pe, "big_in")

                def project(g):
                    if g >= DC:
                        pe.wait_ge(xp_ready, g - DC + 1)
                    product(pe, bank[g % 4][:, :], lambda k: w_in[:, k, g * P:(g + 1) * P], lambda k: xnT[:, k, :], DC).then_inc(xz_done, 1)

                for g in range(DC):
                    project(g)
                pe.wait_ge(ex_ready, DC)
                for half in range(2):
                    product(pe, bank[4 + half][:, :], lambda k: const[:, C_ONES:C_ONES + P],
                            lambda k: ex[:, k, half * 512:(half + 1) * 512], DC)
                pe.wait_ge(dt_ready, 1)
                pe.matmul(bank[6][:, 0:DC], const[:, C_ONES:C_ONES + P], dt[:, :], start=True, stop=True).then_inc(a_sum, 1)
                pe.wait_ge(wb_in, 16)
                pe.wait_ge(xp_ready, DC)
                for b in range(B):
                    for k in range(DC):
                        at = W_PAD - b * NS
                        ins = pe.matmul(bank[7][:, 0:S], wb[:, k, at:at + P], xp[:, k, b * S:(b + 1) * S],
                                        start=(b == 0 and k == 0), stop=(b == B - 1 and k == DC - 1))
                ins.then_inc(b_done, 1)
                for g in range(DC, 2 * DC):
                    project(g)
                pe.wait_ge(xm_ready, 1)
                pe.wait_ge(z_ready, DC)
                for k in range(DC):
                    pe.matmul(bank[k][:, :], wc[:, k * P:(k + 1) * P], xmx[:, :, :].rearrange("p b t -> p (b t)"),
                              start=True, stop=True).then_inc(y_sum, 1)
                pe.wait_ge(y_ready, DC)
                for t in range(TT):
                    product(pe, bank[4 + t][:, :], lambda k: y[:, k, t * P:(t + 1) * P], lambda k: w_out[:, k, :], DC).then_inc(out_done, 1)

            @block.vector
            def _(v):
                ch = Chain(v, step)
                outer.dve_var(ch)
                outer.dve_u(ch)
                v.wait_ge(outer.u_ready, TT)
                inner.dve_var(ch)
                weights.wait(v, "big_in")
                inner.dve_u(ch, gain[:, :], shift[:, :])
                inner.evac(v, bank, v.tensor_copy)
                v.wait_ge(small_in, 16 * SMALL)
                v.tensor_scalar(la[:, :, :], la[:, :, :], 80.0, None, ALU.min).then_inc(al_ready, 1)
                v.wait_ge(dt_exp, 1)
                v.tensor_scalar(dt[:, :], dt[:, :], DT_MIN, DT_MAX, ALU.max, ALU.min).then_inc(dt_ready, 1)
                v.wait_ge(ea_ready, 1)
                v.wait_ge(dt_ready, 1)
                ch.link(v.tensor_tensor(la[:, :, :], ea[:, :, :], dt[:, :].unsqueeze(2).to_broadcast([P, DC, NS]), ALU.mult))
                ch.link(v.tensor_scalar(la[:, :, :], la[:, :, :], -1.0, LOG_A_MIN, ALU.mult, ALU.max))
                ch.link(v.tensor_scalar(la[:, :, :], la[:, :, :], LOG_A_MAX, None, ALU.min))
                for k in range(DC):
                    v.tensor_tensor(ex[:, k, :].rearrange("p (s t) -> p s t", s=NS),
                                    la[:, k, :].unsqueeze(2).to_broadcast([P, NS, S]),
                                    const[:, C_TIME:C_TIME + S].unsqueeze(1).to_broadcast([P, NS, S]), ALU.mult).then_inc(tl_ready, 1)
                v.wait_ge(a_sum, 1)
                for half in range(2):
                    n = NS // 2
                    ch.inc(v.tensor_tensor(sel[:, half * n:(half + 1) * n, :], bank[4 + half][:, :].rearrange("p (s t) -> p s t", s=n),
                                           const[:, C_STATE + half * n:C_STATE + (half + 1) * n].unsqueeze(2).to_broadcast([P, n, S]), ALU.mult))
                ch.link(v.tensor_reduce(dtm[:, :], bank[6][:, 0:DC], AX.X, ALU.add))
                ch.link(v.tensor_reduce(amean[:, :], sel[:, :, :].rearrange("p s t -> p t s"), AX.X, ALU.add))
                ch.link(v.tensor_scalar(dtm[:, :], dtm[:, :], 1.0 / D, None, ALU.mult))
                v.wait_ge(b_done, 1)
                v.wait_ge(wb_ready, 1)
                ch.link(v.tensor_scalar(bp[:, S - 1:2 * S - 1], bank[7][:, 0:S], dtm[:, 0:1], 1.0 / D, ALU.mult, ALU.mult))
                windows = bass.AP(tensor=bp[:, :].tensor, offset=0, ap=[[2 * S - 1, P], [1, S], [1, S]])
                ch.link(v.tensor_tensor(conv[:, :, :], windows, amean[:, :].unsqueeze(1).to_broadcast([P, S, S]), ALU.mult))
                ch.link(v.tensor_reduce(xm[:, :], conv[:, :, :], AX.X, ALU.add))
                v.tensor_tensor(xmx[:, :, :], xm[:, :].unsqueeze(1).to_broadcast([P, B, S]),
                                const[:, C_BAT:C_BAT + B].unsqueeze(2).to_broadcast([P, B, S]), ALU.mult).then_inc(xm_ready, 1)
                v.wait_ge(z_ready, DC)
                for k in range(DC):
                    v.wait_ge(y_sum, k + 1)
                    ch.link(v.scalar_tensor_tensor(y[:, k, :], xp[:, k, :], d_skip[:, k:k + 1], bank[k][:, :], ALU.mult, ALU.add))
                    v.tensor_tensor(y[:, k, :], y[:, k, :], z[:, k, :], ALU.mult).then_inc(y_ready, 1)
                for t in range(TT):
                    ch.inc(v.tensor_tensor(x[:, t, :], x[:, t, :], u[:, t, :], ALU.add))
                ch.wait()
                for t in range(TT):
                    ch.inc(v.tensor_tensor(x[:, t, :], x[:, t, :], b_out[:, :], ALU.add))
                ch.wait()
                for t in range(TT):
                    v.wait_ge(out_done, t + 1)
                    v.tensor_tensor(x[:, t, :], x[:, t, :], bank[4 + t][:, :], ALU.add)


def retrieval_weights(sc, a):
    return Weights(sc, [
        ("w_in", "wq", [P, DC, 2 * PH * PK], chunks(a["w_q"])),
        ("small_in", "keys", [P, 2 * PH * NKEY], a["pkeys"]),
        ("small_in", "gamma", [P, 2 * PH], a["bn_gamma"]),
        ("small_in", "beta", [P, 2 * PH], a["bn_beta"]),
    ])


def retrieval_stage(nc, const, x, a, weights):
    G = 2 * PH
    N = 4
    GROUPS = PH * PTOP // N
    RING = 4
    SEARCH_AFTER, CHOOSE_AFTER, LOOK_UP_AFTER = (3, 5), 8, 11
    embed = a["embed"]
    assert GROUPS % RING == 0
    with Scope(nc, "rt") as sc:
        sb, sem = sc.sb, sc.sem
        u = sb("u", [P, TT, D])
        idx = sb("idx", [P, TT, PH * PTOP], I32)
        weight = sb("weight", [P, TT, PH * PTOP])
        rows = sb("rows", [P, RING, N, 2 * D])
        diag = sb("diag", [P, 2, N, P])
        idx_c = sb("idx_c", [P, 2, PH * PTOP], I32)
        dot, act, coef = (sb(n, [P, 2, N]) for n in ("dot", "act", "coef"))
        uT = sb("uT", [P, DC, T])
        wq, keys, gamma, beta = (weights.buf[n] for n in ("wq", "keys", "gamma", "beta"))
        q = sb("q", [P, G, T])
        stat, mv = sb("stat", [P, G, 6]), sb("mv", [P, G, 2])
        ve, sd, gs, sh = (sb(n, [P, G]) for n in ("ve", "sd", "gs", "sh"))
        s8 = sb("s8", [P, G, PTOP])
        i8 = sb("i8", [P, G, PTOP], U32)
        i8f = sb("i8f", [P, G, PTOP])
        sums = sb("sums", [P, PH, PTOP, PTOP])
        t8 = sb("t8", [P, PH, PTOP])
        pk = sb("pk", [P, PH, PTOP], U32)
        pki = sb("pki", [P, 2, PH, PTOP], U32)
        pkf = sb("pkf", [P, 2, PH, PTOP])
        eq = sb("eq", [P, PH, PTOP, PTOP])
        ixy = sb("ixy", [P, 2, PH, PTOP])
        e8 = sb("e8", [P, PH, PTOP])
        tot = sb("tot", [P, PH])
        bank = [sc.ps(f"b{i}", [P, 512]) for i in range(8)]
        norm = Norm(sc, "n", x, u, uT, const[:, C_IDENT:C_IDENT + P])
        landed = [sem(f"landed{r}") for r in range(RING)]
        chosen, dots, coefs, added, gelus, diags, used, idx_ready, pool_mark = (
            sem(n) for n in ("chosen", "dots", "coefs", "added", "gelus", "diags", "used", "idx_ready", "pool_mark"))
        (q_done, q_out, q_root, q_var, q_normed, sim_done, sim_used, shifted, e_ready, step) = (
            sem(n) for n in ("q_done", "q_out", "q_root", "q_var", "q_normed", "sim_done",
                             "sim_used", "shifted", "e_ready", "step"))
        with nc.Block() as block:
            @block.gpsimd
            def _(g):
                with g.Fori(0, TT // 2) as i:
                    for e in range(2):
                        g.wait_ge(chosen, 2 * i + (e + 1))
                        g.sem_inc(pool_mark, 1)
                        g.tensor_copy(idx_c[:, e, :], idx[:, bass.ds(2 * i + e, 1), :].rearrange("p o n -> p (o n)")).then_inc(idx_ready, 1)
                        g.wait_ge(idx_ready, 2 * i + (e + 1))
                        for n in range(GROUPS):
                            g.wait_ge(used, i * (2 * GROUPS) + (e * GROUPS + n + 1))
                            g.sem_inc(pool_mark, 1)
                            for k in range(N):
                                g.indirect_dma_start(rows[:, n % RING, k, :], None, embed,
                                                     bass.IndirectOffsetOnAxis(ap=idx_c[:, e, n * N + k:n * N + k + 1], axis=0)
                                                     ).then_inc(landed[n % RING], 16)

            @block.tensor
            def _(pe):
                norm.pe_turn(pe, bank)
                pe.wait_ge(norm.uT_ready, TT)
                weights.wait(pe, "w_in")
                for g in range(G):
                    if g >= 8:
                        pe.wait_ge(q_out, g - 7)
                    product(pe, bank[g % 8][:, :], lambda k: wq[:, k, g * PK:(g + 1) * PK], lambda k: uT[:, k, :], DC).then_inc(q_done, 1)
                weights.wait(pe, "small_in")
                pe.wait_ge(q_normed, G)

                def compare(t):
                    for g in range(G):
                        ins = pe.matmul(bank[g // 4][:, g % 4 * NKEY:(g % 4 + 1) * NKEY],
                                        q[:, g, t * P:(t + 1) * P], keys[:, g * NKEY:(g + 1) * NKEY], start=True, stop=True)
                    ins.then_inc(sim_done, 1)

                pe.sem_inc(used, RING)
                compare(0)
                for t in range(TT):
                    if t + 1 < TT:
                        pe.wait_ge(sim_used, 2 * (t + 1))
                        compare(t + 1)
                    if t >= 2:
                        pe.wait_ge(added, t - 1)
                    for n in range(GROUPS):
                        m = t * GROUPS + n
                        pe.wait_ge(diags, m + 1)
                        for k in range(N):
                            ins = pe.matmul(bank[4 + t % 2][:, :], diag[:, m % 2, k, :], rows[:, n % RING, k, D:2 * D],
                                            start=(n == 0 and k == 0), stop=(n == GROUPS - 1 and k == N - 1))
                        ins.then_inc(used, 1)

            @block.scalar
            def _(s):
                norm.act_root(s)
                for g in range(G):
                    s.wait_ge(q_done, g + 1)
                    s.activation(q[:, g, :], bank[g % 8][:, :], ACT.Copy).then_inc(q_out, 1)
                s.wait_ge(q_var, 1)
                s.activation(sd[:, :], ve[:, :], ACT.Sqrt).then_inc(q_root, 1)

                def exponent(t):
                    s.wait_ge(shifted, t + 1)
                    s.activation(e8[:, :, :], e8[:, :, :], ACT.Exp).then_inc(e_ready, 1)

                exponent(0)
                for t in range(TT):
                    for n in range(GROUPS):
                        m = t * GROUPS + n
                        s.wait_ge(dots, m + 1)
                        s.activation(act[:, m % 2, :], dot[:, m % 2, :], ACT.Gelu_apprx_tanh).then_inc(gelus, 1)
                        if n == LOOK_UP_AFTER and t + 1 < TT:
                            exponent(t + 1)
                        s.wait_ge(coefs, m + 1)
                        if m >= 2:
                            s.wait_ge(used, RING + m - 1)
                        for k in range(N):
                            ins = s.activation(diag[:, m % 2, k, :], const[:, C_IDENT:C_IDENT + P], ACT.Copy, scale=coef[:, m % 2, k:k + 1])
                        ins.then_inc(diags, 1)

            @block.vector
            def _(v):
                ch = Chain(v, step)
                norm.dve_var(ch)
                norm.dve_u(ch)
                norm.evac(v, bank, v.tensor_copy)
                for g in range(G):
                    v.wait_ge(q_out, g + 1)
                    ch.inc(v.bn_stats(stat[:, g, :], q[:, g, :]))
                ch.wait()
                for g in range(G):
                    ch.inc(v.bn_aggr(mv[:, g, :], stat[:, g, :]))
                ch.wait()
                v.tensor_scalar(ve[:, :], mv[:, :, 1], LN_EPS, None, ALU.add).then_inc(q_var, 1)
                v.wait_ge(q_root, 1)
                weights.wait(v, "small_in")
                ch.link(v.reciprocal(gs[:, :], sd[:, :]))
                ch.link(v.tensor_tensor(gs[:, :], gs[:, :], gamma[:, :], ALU.mult))
                ch.link(v.tensor_tensor(sh[:, :], mv[:, :, 0], gs[:, :], ALU.mult))
                ch.link(v.tensor_tensor(sh[:, :], beta[:, :], sh[:, :], ALU.subtract))
                for g in range(G):
                    v.tensor_scalar(q[:, g, :], q[:, g, :], gs[:, g:g + 1], sh[:, g:g + 1], ALU.mult, ALU.add).then_inc(q_normed, 1)
                iota = const[:, C_IOTA:C_IOTA + 8]
                shape = [P, PH, PTOP, PTOP]

                def search(t, side):
                    v.wait_ge(sim_done, t + 1)
                    sims = [bank[g // 4][:, g % 4 * NKEY:(g % 4 + 1) * NKEY] for g in range(G)]
                    for g in range(side * PH, side * PH + PH):
                        ch.inc(v.max(out=s8[:, g, :], in_=sims[g]))
                    ch.wait()
                    for g in range(side * PH, side * PH + PH):
                        ins = v.max_index(out=i8[:, g, :], in_max=s8[:, g, :], in_values=sims[g])
                    ins.then_inc(sim_used, 1)

                def choose(t):
                    ch.link(v.tensor_tensor(sums[:, :, :, :], s8[:, 0:PH, :].unsqueeze(3).to_broadcast(shape),
                                            s8[:, PH:G, :].unsqueeze(2).to_broadcast(shape), ALU.add))
                    flat = sums[:, :, :, :].rearrange("p h i j -> p h (i j)")
                    for h in range(PH):
                        ch.inc(v.max(out=t8[:, h, :], in_=flat[:, h, :]))
                    ch.wait()
                    for h in range(PH):
                        ch.inc(v.max_index(out=pk[:, h, :], in_max=t8[:, h, :], in_values=flat[:, h, :]))
                    v.tensor_tensor(e8[:, :, :], t8[:, :, :], t8[:, :, 0:1].to_broadcast([P, PH, PTOP]), ALU.subtract).then_inc(shifted, 1)
                    v.wait_ge(sim_used, 2 * (t + 1))
                    ch.inc(v.tensor_copy(i8f[:, :, :], i8[:, :, :]))
                    ch.wait()
                    ch.inc(v.tensor_single_scalar(pki[:, 0, :, :], pk[:, :, :], 3, ALU.logical_shift_right))
                    ch.link(v.tensor_single_scalar(pki[:, 1, :, :], pk[:, :, :], 7, ALU.bitwise_and))
                    ch.link(v.tensor_copy(pkf[:, :, :, :], pki[:, :, :, :]))

                def look_up(t):
                    for side in range(2):
                        ch.link(v.tensor_tensor(eq[:, :, :, :], pkf[:, side, :, :].unsqueeze(3).to_broadcast(shape),
                                                iota.unsqueeze(1).unsqueeze(1).to_broadcast(shape), ALU.is_equal))
                        ch.link(v.tensor_tensor(eq[:, :, :, :], eq[:, :, :, :],
                                                i8f[:, side * PH:(side + 1) * PH, :].unsqueeze(2).to_broadcast(shape), ALU.mult))
                        ch.link(v.tensor_reduce(ixy[:, side, :, :], eq[:, :, :, :], AX.X, ALU.add))
                    ch.inc(v.scalar_tensor_tensor(idx[:, t, :], ixy[:, 0, :, :].rearrange("p h k -> p (h k)"), float(NKEY),
                                                  ixy[:, 1, :, :].rearrange("p h k -> p (h k)"), ALU.mult, ALU.add))
                    v.wait_ge(e_ready, t + 1)
                    ch.link(v.tensor_reduce(tot[:, :], e8[:, :, :], AX.X, ALU.add))
                    ch.link(v.reciprocal(tot[:, :], tot[:, :]))
                    v.tensor_tensor(weight[:, t, :].rearrange("p (h k) -> p h k", h=PH), e8[:, :, :],
                                            tot[:, :].unsqueeze(2).to_broadcast([P, PH, PTOP]), ALU.mult).then_inc(chosen, 1)

                def add_tile(t):
                    v.wait_ge(used, RING + (t + 1) * GROUPS)
                    v.tensor_tensor(x[:, t, :], x[:, t, :], bank[4 + t % 2][:, :], ALU.add).then_inc(added, 1)

                def take_coefs(m):
                    v.wait_ge(gelus, m + 1)
                    if m >= 2:
                        v.wait_ge(diags, m - 1)
                    t, n = divmod(m, GROUPS)
                    v.tensor_tensor(coef[:, m % 2, :], act[:, m % 2, :], weight[:, t, n * N:(n + 1) * N], ALU.mult).then_inc(coefs, 1)

                v.wait_ge(norm.u_ready, TT)
                search(0, 0)
                search(0, 1)
                choose(0)
                look_up(0)
                v.wait_ge(chosen, 1)
                for t in range(TT):
                    for n in range(GROUPS):
                        m = t * GROUPS + n
                        v.wait_ge(landed[n % RING], 16 * N * (m // RING + 1))
                        for k in range(N):
                            down = rows[:, n % RING, k, 0:D]
                            ins = v.tensor_tensor_reduce(down, u[:, t, :], down, 1.0, 0.0, ALU.mult, ALU.add, dot[:, m % 2, k:k + 1])
                        ins.then_inc(dots, 1)
                        if m:
                            take_coefs(m - 1)
                        if t + 1 < TT:
                            if n in SEARCH_AFTER:
                                search(t + 1, SEARCH_AFTER.index(n))
                            if n == CHOOSE_AFTER:
                                choose(t + 1)
                            if n == LOOK_UP_AFTER:
                                look_up(t + 1)
                                v.wait_ge(chosen, t + 2)
                        if n == 1 and t:
                            add_tile(t - 1)
                take_coefs(TT * GROUPS - 1)
                add_tile(TT - 1)


def self_attention_weights(sc, a):
    return Weights(sc, [("w_in", n, [P, DC, D], chunks(a[n])) for n in ("sa_q", "sa_k", "sa_v")]
                   + [("wo_in", "sa_o", [P, DC, D], chunks(a["sa_o"]))])


def self_attention(nc, const, x, weights):
    scale = float(D) ** -0.5
    with Scope(nc, "sa") as sc:
        sb, sem = sc.sb, sc.sem
        u, uT = sb("u", [P, TT, D]), sb("uT", [P, DC, T])
        wq, wk, wv, wo = (weights.buf[n] for n in ("sa_q", "sa_k", "sa_v", "sa_o"))
        qT, kT = sb("qT", [P, DC, T]), sb("kT", [P, DC, T])
        vt = sb("vt", [P, TT, D])
        s_sb = sb("s", [P, 2, H, P])
        mx, nmx, tot = (sb(n, [P, 2, H]) for n in ("mx", "nmx", "tot"))
        wT = sb("wT", [P, H, P])
        o = sb("o", [P, 2, D])
        oT = sb("oT", [P, DC, P])
        pa = sc.ps("pa", [P, 4, 512])
        pb = sc.ps("pb", [P, 4, 512])
        banks = [pa[:, i, :] for i in range(4)] + [pb[:, i, :] for i in range(4)]
        norm = Norm(sc, "n", x, u, uT, const[:, C_IDENT:C_IDENT + P])
        (q_done, q_out, v_out, scored, taken, peaked, probs, turned, wT_ready, pv, o_ready, o_turned,
         oT_ready, done, added, step) = (sem(n) for n in (
            "q_done", "q_out", "v_out", "scored", "taken", "peaked", "probs", "turned",
            "wT_ready", "pv", "o_ready", "o_turned", "oT_ready", "done", "added", "step"))
        with nc.Block() as block:
            @block.tensor
            def _(pe):
                norm.pe_turn(pe, banks)
                pe.wait_ge(norm.uT_ready, TT)
                weights.wait(pe, "w_in")
                for c in range(DC):
                    product(pe, banks[c], lambda k: wq[:, k, c * P:(c + 1) * P], lambda k: uT[:, k, :], DC).then_inc(q_done, 1)
                for c in range(DC):
                    product(pe, banks[4 + c], lambda k: wk[:, k, c * P:(c + 1) * P], lambda k: uT[:, k, :], DC).then_inc(q_done, 1)
                for t in range(TT):
                    pe.wait_ge(q_out, t + 1)
                    product(pe, banks[t], lambda k: uT[:, k, t * P:(t + 1) * P], lambda k: wv[:, k, :], DC).then_inc(q_done, 1)
                weights.wait(pe, "wo_in")
                pe.wait_ge(q_out, 2 * DC)
                pe.wait_ge(v_out, TT)

                def scores(t):
                    for h in range(H):
                        c, i = h // HC, h % HC
                        ins = pe.matmul(pa[:, i, c * P:(c + 1) * P], qT[i * DH:(i + 1) * DH, c, t * P:(t + 1) * P],
                                        kT[i * DH:(i + 1) * DH, c, t * P:(t + 1) * P], start=True, stop=True)
                    ins.then_inc(scored, 1)

                scores(0)
                for t in range(TT):
                    pe.wait_ge(taken, HC * (t + 1))
                    if t + 1 < TT:
                        scores(t + 1)
                    pe.wait_ge(probs, t + 1)
                    if t >= 1:
                        pe.wait_ge(added, t)
                    for h in range(H):
                        ins = pe.transpose(pb[:, h // 4, (h % 4) * P:(h % 4 + 1) * P], s_sb[:, t % 2, h, :], const[:, C_IDENT:C_IDENT + P])
                        if h % 4 == 3:
                            ins.then_inc(turned, 1)
                    for h in range(H):
                        if h % 4 == 0:
                            pe.wait_ge(wT_ready, 4 * t + h // 4 + 1)
                        ins = pe.matmul(pb[:, h // 4, (h % 4) * P:(h % 4 + 1) * P], wT[:, h, :],
                                        vt[:, t, (h // HC) * P:(h // HC + 1) * P], start=True, stop=True)
                    ins.then_inc(pv, 1)
                    pe.wait_ge(o_ready, DC * (t + 1))
                    for c in range(DC):
                        ins = pe.transpose(pb[:, 0, c * P:(c + 1) * P], o[:, t % 2, c * P:(c + 1) * P], const[:, C_IDENT:C_IDENT + P])
                    ins.then_inc(o_turned, 1)
                    pe.wait_ge(oT_ready, t + 1)
                    product(pe, pb[:, 1, :], lambda k: oT[:, k, :], lambda k: wo[:, k, :], DC).then_inc(done, 1)

            @block.scalar
            def _(s):
                norm.act_root(s)
                for c in range(DC):
                    s.wait_ge(q_done, c + 1)
                    s.activation(qT[:, c, :], banks[c], ACT.Copy).then_inc(q_out, 1)
                for c in range(DC):
                    s.wait_ge(q_done, DC + c + 1)
                    s.activation(kT[:, c, :], banks[4 + c], ACT.Copy).then_inc(q_out, 1)
                for t in range(TT):
                    s.wait_ge(peaked, t + 1)
                    for h in range(H):
                        row = s_sb[:, t % 2, h, :]
                        ins = s.activation(row, row, ACT.Exp, bias=nmx[:, t % 2, h:h + 1], accum_out=tot[:, t % 2, h:h + 1])
                    ins.then_inc(probs, 1)
                    for g in range(4):
                        s.wait_ge(turned, 4 * t + g + 1)
                        if g == 0 and t >= 1:
                            s.wait_ge(pv, t)
                        s.activation(wT[:, 4 * g:4 * g + 4, :].rearrange("p h n -> p (h n)"), pb[:, g, :], ACT.Copy).then_inc(wT_ready, 1)

            @block.vector
            def _(v):
                ch = Chain(v, step)
                norm.dve_var(ch)
                norm.dve_u(ch)
                norm.evac(v, banks, v.tensor_copy)
                for t in range(TT):
                    v.wait_ge(q_done, 2 * DC + t + 1)
                    v.tensor_copy(vt[:, t, :], banks[t]).then_inc(v_out, 1)

                def soften(t):
                    v.wait_ge(scored, t + 1)
                    if t >= 2:
                        v.wait_ge(turned, 4 * (t - 1))
                    s = s_sb[:, t % 2, :, :]
                    for i in range(HC):
                        v.scalar_tensor_tensor(s.rearrange("p (c i) n -> p i c n", i=HC)[:, i, :, :],
                                               pa[:, i, :].rearrange("p (c n) -> p c n", n=P), scale,
                                               const[:, C_CAUSAL:C_CAUSAL + P].unsqueeze(1).to_broadcast([P, DC, P]),
                                               ALU.mult, ALU.add).then_inc(taken, 1)
                    v.wait_ge(taken, HC * (t + 1))
                    ch.link(v.tensor_reduce(mx[:, t % 2, :], s, AX.X, ALU.max))
                    v.tensor_scalar(nmx[:, t % 2, :], mx[:, t % 2, :], -1.0, None, ALU.mult).then_inc(peaked, 1)

                soften(0)
                for t in range(TT):
                    v.wait_ge(probs, t + 1)
                    ch.link(v.reciprocal(tot[:, t % 2, :], tot[:, t % 2, :]))
                    if t + 1 < TT:
                        soften(t + 1)
                    v.wait_ge(pv, t + 1)
                    for c in range(DC):
                        own = bass.AP(tensor=pb[:, :, :].tensor, offset=512 * c, ap=[[4 * 512, P], [P + DH, HC], [1, DH]])
                        v.tensor_tensor(o[:, t % 2, c * P:(c + 1) * P].rearrange("p (i n) -> p i n", i=HC), own,
                                        tot[:, t % 2, c * HC:(c + 1) * HC].unsqueeze(2).to_broadcast([P, HC, DH]),
                                        ALU.mult).then_inc(o_ready, 1)
                    v.wait_ge(o_turned, t + 1)
                    v.tensor_copy(oT[:, :, :].rearrange("p c n -> p (c n)"), pb[:, 0, :]).then_inc(oT_ready, 1)
                    v.wait_ge(done, t + 1)
                    v.tensor_tensor(x[:, t, :], x[:, t, :], pb[:, 1, :], ALU.add).then_inc(added, 1)


def expert_stage(nc, const, x, a):
    E = 1 + NEXP
    RING, HRING, AHEAD = 4, 4, 2
    with Scope(nc, "ex") as sc:
        sb, sem = sc.sb, sc.sem
        u, uT = sb("u", [P, TT, D]), sb("uT", [P, DC, T])
        u_hi, u_lo = sb("u_hi", [P, DC, T], F32R), sb("u_lo", [P, DC, T], F32R)
        w = [split_buffer(sc, f"w{r}", [P, 2 * D]) for r in range(RING)]
        b1, b2 = sb("b1", [P, E * FC]), sb("b2", [E, D])
        rw, rb = sb("rw", [P, DC, NEXP]), sb("rb", [P, NEXP])
        lg, m8, i8f = sb("lg", [P, TT, NEXP]), sb("m8", [P, TT, 8]), sb("i8f", [P, TT, 8])
        i8 = sb("i8", [P, TT, 8], U32)
        e2, tot = sb("e2", [P, TT, 2]), sb("tot", [P, TT])
        pick = sb("pick", [P, TT, 2, NEXP])
        share = sb("share", [P, TT, E])
        shareT = sb("shareT", [E, T])
        shares = sb("shares", [P, E, T])
        g_sb, gs = sb("g", [P, 2, T]), sb("gs", [P, 2, T])
        h_hi, h_lo = ([sb(f"h_{n}{r}", [P, T], F32R) for r in range(2)] for n in ("hi", "lo"))
        py = [sc.ps(f"py{t}", [P, 512]) for t in range(TT)]
        ph = [sc.ps(f"ph{r}", [P, 512]) for r in range(HRING)]
        norm = Norm(sc, "n", x, u, uT, const[:, C_IDENT:C_IDENT + P])
        landed = [sem(f"landed{r}") for r in range(RING)]
        (small_in, u_hi_ready, u_lo_ready, routed, shifted, e_ready, share_ready, share_turned, shareT_ready, spread,
         spread_out, w_hi_ready, w_lo_ready, inner, gelus, scaled, h_hi_ready, h_lo_ready, used, step) = (sem(n) for n in (
            "small_in", "u_hi_ready", "u_lo_ready", "routed", "shifted", "e_ready", "share_ready", "share_turned",
            "shareT_ready", "spread", "spread_out", "w_hi_ready", "w_lo_ready", "inner", "gelus", "scaled",
            "h_hi_ready", "h_lo_ready", "used", "step"))


        def networks(eng, body):
            body(0)
            with eng.Fori(1, E - 1) as e:
                body(e)
            body(E - 1)

        def until(eng, s, e, f, back):
            if isinstance(e, int) and e * FC + f - back < 0:
                return
            if isinstance(e, int):
                eng.wait_ge(s, e * FC + f - back + 1)
            else:
                eng.wait_ge(s, e * FC + (f - back + 1))

        with nc.Block() as block:
            @block.sync
            def _(sp):
                sp.dma_start(rw[:, :, :], a["router_wT"].rearrange("(k p) n -> p k n", p=P)).then_inc(small_in, 16)
                sp.dma_start(rb[:, :], a["router_b"].to_broadcast([P, NEXP])).then_inc(small_in, 16)
                sp.dma_start(b1[:, :], a["b1"]).then_inc(small_in, 16)
                sp.dma_start(b2[:, :], a["b2"]).then_inc(small_in, 16)

                def load(e):
                    for f in range(FC):
                        until(sp, used, e, f, RING)
                        if isinstance(e, int):
                            src = a["w12"][(e * FC + f) * P:(e * FC + f + 1) * P, :]
                        else:
                            src = a["w12"][bass.ds(e * (FC * P) + f * P, P), :]
                        sp.dma_start(w[f % RING][2][:, :], src).then_inc(landed[f % RING], 16)
                networks(sp, load)

            @block.gpsimd
            def _(g):
                def low(e):
                    for f in range(FC):
                        hi, lo, raw = w[f % RING]
                        until(g, w_hi_ready, e, f, 0)
                        g.tensor_tensor(lo[:, :], raw[:, :], hi[:, :].bitcast(F32), ALU.subtract).then_inc(w_lo_ready, 1)
                networks(g, low)

            @block.tensor
            def _(pe):
                norm.pe_turn(pe, py)
                pe.wait_ge(norm.uT_ready, TT)
                pe.wait_ge(small_in, 64)
                for t in range(TT):
                    ins = product(pe, ph[0][:, t * NEXP:(t + 1) * NEXP], lambda k: uT[:, k, t * P:(t + 1) * P], lambda k: rw[:, k, :], DC)
                ins.then_inc(routed, 1)
                pe.wait_ge(share_ready, 1)
                for t in range(TT):
                    ins = pe.transpose(ph[1][0:E, t * P:(t + 1) * P], share[:, t, :], const[:, C_IDENT:C_IDENT + P])
                ins.then_inc(share_turned, 1)
                pe.wait_ge(shareT_ready, 1)
                for e in range(E):
                    if e >= 2:
                        pe.wait_ge(spread_out, e - 1)
                    pe.matmul(ph[2 + e % 2][:, :], const[0:E, C_IDENT + e:C_IDENT + e + 1].to_broadcast([E, P]), shareT[:, :],
                              start=True, stop=True).then_inc(spread, 1)
                for t in range(TT):
                    pe.matmul(py[t][:, :], shareT[:, t * P:(t + 1) * P], b2[:, :], start=True, stop=False)
                pe.wait_ge(u_lo_ready, 1)
                pe.wait_ge(spread_out, E)

                def first(e, f):
                    until(pe, w_lo_ready, e, f, 0)
                    until(pe, gelus, e, f, HRING)
                    hi, lo, _ = w[f % RING]
                    split_product(pe, ph[f % HRING][:, :],
                                  lambda k: hi[:, k * P:(k + 1) * P], lambda k: lo[:, k * P:(k + 1) * P],
                                  lambda k: u_hi[:, k, :], lambda k: u_lo[:, k, :], DC).then_inc(inner, 1)

                def second(e, f, last=False):
                    until(pe, h_lo_ready, e, f, 0)
                    hi, lo, _ = w[f % RING]
                    hh, hl = h_hi[f % 2], h_lo[f % 2]
                    for t in range(TT):
                        ins = split_product(pe, py[t][:, :], lambda k: hh[:, t * P:(t + 1) * P], lambda k: hl[:, t * P:(t + 1) * P],
                                            lambda k: hi[:, D:2 * D], lambda k: lo[:, D:2 * D], 1, first=False, last=last)
                    ins.then_inc(used, 1)

                def network(e):
                    for f in range(FC):
                        first(e, f)
                        if not (isinstance(e, int) and e * FC + f == 0):
                            second(e, f - 1)
                networks(pe, network)
                second(E - 1, FC - 1, last=True)

            @block.scalar
            def _(s):
                norm.act_root(s)
                s.wait_ge(norm.uT_ready, TT)
                s.activation(u_hi[:, :, :], uT[:, :, :], ACT.Copy).then_inc(u_hi_ready, 1)
                s.wait_ge(shifted, 1)
                s.activation(e2[:, :, :], e2[:, :, :], ACT.Exp).then_inc(e_ready, 1)
                for e in range(E):
                    s.wait_ge(spread, e + 1)
                    s.activation(shares[:, e, :], ph[2 + e % 2][:, :], ACT.Copy).then_inc(spread_out, 1)

                def high(e, f):
                    if isinstance(e, int):
                        if e * FC + f >= E * FC:
                            return
                        s.wait_ge(landed[f % RING], 16 * ((e * FC + f) // RING + 1))
                    else:
                        s.wait_ge(landed[f % RING], e * (16 * FC // RING) + 16 * (f // RING + 1))
                    s.activation(w[f % RING][0][:, :], w[f % RING][2][:, :], ACT.Copy).then_inc(w_hi_ready, 1)

                for f in range(AHEAD):
                    high(0, f)

                def network(e):
                    for f in range(FC):
                        until(s, inner, e, f, 0)
                        until(s, scaled, e, f, 2)
                        bias = b1[:, e * FC + f:e * FC + f + 1] if isinstance(e, int) else b1[:, bass.ds(e * FC + f, 1)]
                        s.activation(g_sb[:, f % 2, :], ph[f % HRING][:, :], ACT.Gelu_apprx_tanh, bias=bias).then_inc(gelus, 1)
                        high(e, f + AHEAD)
                        until(s, scaled, e, f, 0)
                        until(s, used, e, f, 2)
                        s.activation(h_hi[f % 2][:, :], gs[:, f % 2, :], ACT.Copy).then_inc(h_hi_ready, 1)
                networks(s, network)

            @block.vector
            def _(v):
                ch = Chain(v, step)
                norm.dve_var(ch)
                norm.dve_u(ch)
                norm.evac(v, py, v.tensor_copy)
                v.wait_ge(u_hi_ready, 1)
                v.tensor_tensor(u_lo[:, :, :], uT[:, :, :], u_hi[:, :, :].bitcast(F32), ALU.subtract).then_inc(u_lo_ready, 1)
                v.wait_ge(routed, 1)
                v.wait_ge(small_in, 64)
                ch.link(v.tensor_tensor(lg[:, :, :], ph[0][:, 0:TT * NEXP].rearrange("p (t e) -> p t e", t=TT),
                                        rb[:, :].unsqueeze(1).to_broadcast([P, TT, NEXP]), ALU.add))
                for t in range(TT):
                    ch.inc(v.max(out=m8[:, t, :], in_=lg[:, t, :]))
                ch.wait()
                for t in range(TT):
                    ch.inc(v.max_index(out=i8[:, t, :], in_max=m8[:, t, :], in_values=lg[:, t, :]))
                v.tensor_tensor(e2[:, :, :], m8[:, :, 0:2], m8[:, :, 0:1].to_broadcast([P, TT, 2]), ALU.subtract).then_inc(shifted, 1)
                ch.wait()
                ch.inc(v.tensor_copy(i8f[:, :, :], i8[:, :, :]))
                v.wait_ge(e_ready, 1)
                ch.link(v.tensor_reduce(tot[:, :], e2[:, :, :], AX.X, ALU.add))
                ch.link(v.reciprocal(tot[:, :], tot[:, :]))
                ch.link(v.tensor_tensor(e2[:, :, :], e2[:, :, :], tot[:, :].unsqueeze(2).to_broadcast([P, TT, 2]), ALU.mult))
                ch.inc(v.memset(share[:, :, 0], 1.0))
                for t in range(TT):
                    for k in range(2):
                        ch.inc(v.tensor_scalar(pick[:, t, k, :], const[:, C_IOTA:C_IOTA + NEXP], i8f[:, t, k:k + 1], e2[:, t, k:k + 1],
                                               ALU.is_equal, ALU.mult))
                ch.wait()
                v.tensor_tensor(share[:, :, 1:E], pick[:, :, 0, :], pick[:, :, 1, :], ALU.add).then_inc(share_ready, 1)
                v.wait_ge(share_turned, 1)
                v.tensor_copy(shareT[:, :], ph[1][0:E, :]).then_inc(shareT_ready, 1)
                v.wait_ge(spread_out, E)

                def network(e):
                    for f in range(FC):
                        until(v, gelus, e, f, 0)
                        until(v, h_lo_ready, e, f, 2)
                        mine = shares[:, e, :] if isinstance(e, int) else shares[:, bass.ds(e, 1), :].rearrange("p o n -> p (o n)")
                        v.tensor_tensor(gs[:, f % 2, :], g_sb[:, f % 2, :], mine, ALU.mult).then_inc(scaled, 1)
                        until(v, h_hi_ready, e, f, 0)
                        v.tensor_tensor(h_lo[f % 2][:, :], gs[:, f % 2, :], h_hi[f % 2][:, :].bitcast(F32), ALU.subtract).then_inc(h_lo_ready, 1)
                networks(v, network)
                v.wait_ge(used, E * FC)
                for t in range(TT):
                    v.tensor_tensor(x[:, t, :], x[:, t, :], py[t][:, :], ALU.add)


def build(nc, a, out):
    with ExitStack() as ctx:
        x = ctx.enter_context(nc.sbuf_tensor("x", [P, TT, D], F32))
        const = ctx.enter_context(nc.sbuf_tensor("const", [P, C_END], F32))
        load_and_norm(nc, a["x"], a["constants"], const, x)
        with nc.sbuf_tensor("oT0", [P, DC, T], F32) as oT:
            cross_attention(nc, "c0", const, x, oT, a["ctxT"], a["L0_xattn_Wq"], a["L0_xattn_Wk"], a["L0_xattn_Wv"], mask_dram=a["mask"])
            with Scope(nc, "rw") as rw:
                for_retrieval = retrieval_weights(rw, a)
                with Scope(nc, "mw") as mw:
                    for_mixer = mixer_weights(mw, a)
                    output_stage(nc, "o0", x, oT, for_mixer, a["L0_xattn_Wo"])
                    mixer_stage(nc, const, x, a, for_mixer, for_retrieval)
                retrieval_stage(nc, const, x, a, for_retrieval)
        with nc.sbuf_tensor("oT1", [P, DC, T], F32) as oT:
            cross_attention(nc, "c1", const, x, oT, a["ctxT"], a["L1_WqT"], a["L1_WkT"], a["L1_WvT"], adapt=a)
            with Scope(nc, "aw") as aw:
                for_self = self_attention_weights(aw, a)
                output_stage(nc, "o1", x, oT, for_self, a["L1_WoT"], a["L1_bo"])
                self_attention(nc, const, x, for_self)
        expert_stage(nc, const, x, a)
        store(nc, out, x)


def kernel(**i):
    import concourse.bacc as _bacc
    from concourse.bass_utils import run_bass_kernel_spmd as _run

    def col(v):
        return np.ascontiguousarray(np.asarray(v).reshape(-1, P).T)

    def t(w):
        return np.ascontiguousarray(np.asarray(w).T)

    arrays = {
        "x": np.asarray(i["x"]),
        "constants": constants(),
        "ctxT": np.ascontiguousarray(np.asarray(i["ctx_1024"]).transpose(0, 2, 1)),
        "mask": np.asarray(i["mask_BxS2_ik0"]),
        "L0_xattn_Wq": np.asarray(i["L0_xattn_Wq"]), "L0_xattn_Wk": np.asarray(i["L0_xattn_Wk"]),
        "L0_xattn_Wv": np.asarray(i["L0_xattn_Wv"]), "L0_xattn_Wo": np.asarray(i["L0_xattn_Wo"]),
    }
    arrays.update({
        "A_log": np.asarray(i["L0_attn_A_log"]), "W_BT": t(i["L0_attn_W_B"]), "W_CT": t(i["L0_attn_W_C"]),
        "W_inT": t(i["L0_attn_W_in"]), "W_outT": t(i["L0_attn_W_out"]), "b_out": np.asarray(i["L0_attn_b_out"]).reshape(1, D),
        "D_skip": col(i["L0_attn_D_skip"]), "log_dt": col(i["L0_attn_log_dt"]), "b_in": col(i["L0_attn_b_in"]),
        "ln_g": np.asarray(i["L0_attn_ln_g"]).reshape(1, D), "ln_b": np.asarray(i["L0_attn_ln_b"]).reshape(1, D),
    })
    arrays.update({
        "w_q": np.asarray(i["L0_ffn_w_q"]), "bn_gamma": col(i["L0_ffn_bn_gamma"]), "bn_beta": col(i["L0_ffn_bn_beta"]),
        "pkeys": np.ascontiguousarray(np.asarray(i["L0_ffn_keys"]).transpose(3, 2, 0, 1).reshape(PK, 2 * PH * NKEY)),
        "embed": np.concatenate([np.asarray(i["L0_ffn_down_embed"]), np.asarray(i["L0_ffn_up_embed"])], axis=1),
    })
    arrays.update({
        "L1_WqT": t(i["L1_xattn_Wq"]), "L1_WkT": t(i["L1_xattn_Wk"]), "L1_WvT": t(i["L1_xattn_Wv"]), "L1_WoT": t(i["L1_xattn_Wo"]),
        "L1_bqT": col(i["L1_xattn_bq"]), "bk": col(i["L1_xattn_bk"]), "bv": col(i["L1_xattn_bv"]), "L1_bo": np.asarray(i["L1_xattn_bo"]).reshape(1, D),
        "w1T": t(i["L1_xattn_w1"]), "w2T": t(i["L1_xattn_w2"]), "w3T": t(i["L1_xattn_w3"]),
        "b12": np.stack([np.asarray(i["L1_xattn_b1"]), np.asarray(i["L1_xattn_b2"])], axis=1), "b3": np.asarray(i["L1_xattn_b3"]).reshape(1, 1),
    })
    qkv = np.asarray(i["L1_attn_w_qkv"]).reshape(D, H, 3, DH)
    arrays.update({n: np.ascontiguousarray(qkv[:, :, k].reshape(D, D)) for k, n in enumerate(("sa_q", "sa_k", "sa_v"))})
    arrays["sa_o"] = np.asarray(i["L1_attn_w_o"])
    w1 = np.concatenate([np.asarray(i["L1_ffn_shared_w1"])[None], np.asarray(i["L1_ffn_spec_w1"])])
    w2 = np.concatenate([np.asarray(i["L1_ffn_shared_w2"])[None], np.asarray(i["L1_ffn_spec_w2"])])
    b1 = np.concatenate([np.asarray(i["L1_ffn_shared_b1"])[None], np.asarray(i["L1_ffn_spec_b1"])])
    b2 = np.concatenate([np.asarray(i["L1_ffn_shared_b2"])[None], np.asarray(i["L1_ffn_spec_b2"])])
    n = 1 + NEXP
    w1 = w1.reshape(n, FC, P, DC, P).transpose(0, 1, 4, 3, 2).reshape(n * FC * P, D)
    w2 = w2.transpose(0, 2, 1).reshape(n * FC * P, D)
    arrays.update({
        "w12": np.ascontiguousarray(np.concatenate([w1, w2], axis=1)),
        "b1": np.ascontiguousarray(b1.reshape(n * FC, P).T), "b2": b2,
        "router_wT": t(i["L1_ffn_router_w"]), "router_b": np.asarray(i["L1_ffn_router_b"]).reshape(1, NEXP),
    })

    nc = _bacc.Bacc("TRN2", target_bir_lowering=False, num_devices=1)
    a = {n: nc.dram_tensor(f"in_{n}", v.shape, mybir.dt.from_np(v.dtype), kind="ExternalInput").ap() for n, v in arrays.items()}
    out = nc.dram_tensor("out_x", (B, S, D), F32, kind="ExternalOutput").ap()
    build(nc, a, out)
    r = _run(nc, [{f"in_{n}": v for n, v in arrays.items()}], core_ids=[0])
    return r.results[0]["out_x"]
```
